# Optimizing a Trainium2 kernel written in Bass

```python
import numpy as np
import jax
import jax.numpy as jnp

def _softmax(x, axis=-1):
    return jax.nn.softmax(x, axis=axis)

def _gelu(x):
    return jax.nn.gelu(x, approximate=True)

def _silu(x):
    return jax.nn.silu(x)

def _sigmoid(x):
    return jax.nn.sigmoid(x)

def _layernorm(x, axis=-1, eps=1e-05):
    m = jnp.mean(x, axis=axis, keepdims=True)
    v = jnp.var(x, axis=axis, keepdims=True)
    return (x - m) / jnp.sqrt(v + eps)

def _scatter_add(tgt, idx, src, axis=0):
    return tgt.at[idx].add(src)

def _segment_sum(src, seg, n):
    return jax.ops.segment_sum(src, seg, n)
kernel_name = 'mk_sandwich_d1_jaxref_r8_66b27e'

def setup_inputs(seed: int=0):
    np.random.seed(seed)
    _w = jnp.asarray

    def _L0_attn_setup():
        import jax, jax.numpy as jnp
        import numpy as np
        H = 16
        HD = 64
        W = 128
        G = 32
        EPS = 1e-06
        NEG = -1e+30
        key = jax.random.key(seed)
        ks = jax.random.split(key, 7)
        B, S, D = (1, 1024, 128)
        inner = H * HD
        s = 0.02
        return {'x': jax.random.normal(ks[0], (B, S, D), jnp.float32), 'norm_w': jnp.ones((D,), jnp.float32), 'w_q': jax.random.normal(ks[1], (D, inner), jnp.float32) * s, 'w_k': jax.random.normal(ks[2], (D, inner), jnp.float32) * s, 'w_v': jax.random.normal(ks[3], (D, inner), jnp.float32) * s, 'w_out': jax.random.normal(ks[4], (inner, D), jnp.float32) * s, 'scorer_w': jax.random.normal(ks[5], (D, 1), jnp.float32) * s, 'scorer_b': jnp.zeros((1,), jnp.float32)}
    _L0_attn_in = _L0_attn_setup()

    def _L0_ffn_setup():
        import jax, jax.numpy as jnp
        import numpy as np
        NUM_EXPERTS = 8
        CAPACITY = 80
        key = jax.random.key(seed)
        ks = jax.random.split(key, 5)
        D, E, F = (128, NUM_EXPERTS, 512)
        inputs = jax.random.normal(ks[0], (2, 256, D), dtype=jnp.float32)
        gate_w = jax.random.normal(ks[1], (D, E), dtype=jnp.float32) * 0.02
        gate_b = jnp.zeros((E,), dtype=jnp.float32)
        w1 = jax.random.normal(ks[2], (E, D, F), dtype=jnp.float32) * 0.02
        b1 = jnp.zeros((E, F), dtype=jnp.float32)
        w2 = jax.random.normal(ks[3], (E, F, D), dtype=jnp.float32) * 0.02
        b2 = jnp.zeros((E, D), dtype=jnp.float32)
        return {'inputs': inputs, 'gate_w': gate_w, 'gate_b': gate_b, 'w1': w1, 'b1': b1, 'w2': w2, 'b2': b2}
    _L0_ffn_in = _L0_ffn_setup()
    _d = {'L0_attn_x': _L0_attn_in['x'], 'L0_attn_norm_w': _L0_attn_in['norm_w'], 'L0_attn_w_q': _L0_attn_in['w_q'], 'L0_attn_w_k': _L0_attn_in['w_k'], 'L0_attn_w_v': _L0_attn_in['w_v'], 'L0_attn_w_out': _L0_attn_in['w_out'], 'L0_attn_scorer_w': _L0_attn_in['scorer_w'], 'L0_attn_scorer_b': _L0_attn_in['scorer_b'], 'L0_ffn_gate_w': _L0_ffn_in['gate_w'], 'L0_ffn_gate_b': _L0_ffn_in['gate_b'], 'L0_ffn_w1': _L0_ffn_in['w1'], 'L0_ffn_b1': _L0_ffn_in['b1'], 'L0_ffn_w2': _L0_ffn_in['w2'], 'L0_ffn_b2': _L0_ffn_in['b2']}
    _x0 = _d['L0_attn_x']
    _d['L0_attn_x'] = jax.random.normal(jax.random.fold_in(jax.random.key(seed), 1), (1, 2048, 128), dtype=_x0.dtype)
    del _x0
    return _d

def reference(L0_attn_x, L0_attn_norm_w, L0_attn_w_q, L0_attn_w_k, L0_attn_w_v, L0_attn_w_out, L0_attn_scorer_w, L0_attn_scorer_b, L0_ffn_gate_w, L0_ffn_gate_b, L0_ffn_w1, L0_ffn_b1, L0_ffn_w2, L0_ffn_b2):

    def _L0_attn_ref(x, norm_w, w_q, w_k, w_v, w_out, scorer_w, scorer_b):
        import jax, jax.numpy as jnp
        import numpy as np
        H = 16
        HD = 64
        W = 128
        G = 32
        EPS = 1e-06
        NEG = -1e+30
        B, S, D = x.shape
        h = x * jax.lax.rsqrt(jnp.mean(x * x, axis=-1, keepdims=True) + EPS) * norm_w

        def proj(w):
            return jnp.einsum('bsd,de->bse', h, w).reshape(B, S, H, HD).transpose(0, 2, 1, 3)
        q, k, v = (proj(w_q), proj(w_k), proj(w_v))
        scale = HD ** (-0.5)
        nW = S // W
        qw = q.reshape(B, H, nW, W, HD)
        kw = k.reshape(B, H, nW, W, HD)
        vw = v.reshape(B, H, nW, W, HD)
        ll = jnp.einsum('bhnqd,bhnkd->bhnqk', qw, kw) * scale
        cm = jnp.tril(jnp.ones((W, W), bool))
        ll = jnp.where(cm, ll, NEG).reshape(B, H, S, W)
        scores = (jnp.einsum('bsd,do->bso', h, scorer_w) + scorer_b)[..., 0]
        _, idx = jax.lax.top_k(scores, G)
        kg = jnp.take_along_axis(k, idx[:, None, :, None], axis=2)
        vg = jnp.take_along_axis(v, idx[:, None, :, None], axis=2)
        lg = jnp.einsum('bhsd,bhgd->bhsg', q, kg) * scale
        pos = jnp.arange(S)
        gmask = idx[:, None, None, :] <= pos[None, None, :, None]
        lg = jnp.where(gmask, lg, NEG)
        attn = jax.nn.softmax(jnp.concatenate([ll, lg], axis=-1), axis=-1)
        a_loc = attn[..., :W].reshape(B, H, nW, W, W)
        o = jnp.einsum('bhnqk,bhnkd->bhnqd', a_loc, vw).reshape(B, H, S, HD)
        o = o + jnp.einsum('bhsg,bhgd->bhsd', attn[..., W:], vg)
        o = o.transpose(0, 2, 1, 3).reshape(B, S, H * HD)
        return x + jnp.einsum('bse,ed->bsd', o, w_out)

    def _L0_ffn_ref(inputs, gate_w, gate_b, w1, b1, w2, b2):
        import jax, jax.numpy as jnp
        import numpy as np
        NUM_EXPERTS = 8
        CAPACITY = 80
        D = inputs.shape[-1]
        tokens = inputs.reshape(-1, D)
        logits = tokens @ gate_w + gate_b
        probs = jax.nn.softmax(logits, axis=-1)
        expert_idx = jnp.argmax(probs, axis=-1)
        mask1 = jax.nn.one_hot(expert_idx, NUM_EXPERTS, dtype=jnp.float32)
        pos = jnp.sum(jnp.cumsum(mask1, axis=0) * mask1, axis=-1) - 1.0
        pos = pos.astype(jnp.int32)
        keep = (pos < CAPACITY).astype(jnp.float32)
        gate_prob = jnp.sum(probs * mask1, axis=-1)
        pos_oh = jax.nn.one_hot(pos, CAPACITY, dtype=jnp.float32)
        sec_mask = mask1[:, :, None] * pos_oh[:, None, :] * keep[:, None, None]
        combine_weights = sec_mask * gate_prob[:, None, None]
        dispatch = jnp.einsum('nec,nd->ecd', sec_mask, tokens)
        h = jax.nn.gelu(jnp.einsum('ecd,edf->ecf', dispatch, w1) + b1[:, None, :])
        expert_out = jnp.einsum('ecf,efd->ecd', h, w2) + b2[:, None, :]
        out = jnp.einsum('nec,ecd->nd', combine_weights, expert_out)
        return out.reshape(inputs.shape)
    x = L0_attn_x
    x = x + _layernorm(_L0_attn_ref(_layernorm(x, axis=-1), L0_attn_norm_w, L0_attn_w_q, L0_attn_w_k, L0_attn_w_v, L0_attn_w_out, L0_attn_scorer_w, L0_attn_scorer_b), axis=-1)
    x = x + _layernorm(_L0_ffn_ref(_layernorm(x, axis=-1), L0_ffn_gate_w, L0_ffn_gate_b, L0_ffn_w1, L0_ffn_b1, L0_ffn_w2, L0_ffn_b2), axis=-1)
    return x

_drawn_inputs = setup_inputs


def setup_inputs(seed=0):
    import zlib

    import numpy as np

    out = dict(_drawn_inputs(seed))
    spreads = {'L0_attn_norm_w': (1.0, 0.2),
     'L0_ffn_gate_b': (0.0, 0.1),
     'L0_ffn_b1': (0.0, 0.1),
     'L0_ffn_b2': (0.0, 0.1)}
    factors = {'L0_attn_w_q': 3.087, 'L0_attn_w_k': 3.775}
    for name, (base, spread) in spreads.items():
        noise = np.random.default_rng([zlib.crc32(name.encode()), seed]).standard_normal(out[name].shape)
        drawn = base * np.exp(spread * noise) if base else spread * noise
        out[name] = jnp.asarray(drawn.astype(out[name].dtype))
    for name, factor in factors.items():
        out[name] = (out[name] * factor).astype(out[name].dtype)
    return out
```

```python
from contextlib import ExitStack

import concourse.bass as bass
from concourse import mybir


def build(nc, x, norm_w, w_q, w_k, w_v, w_out, scorer_w, scorer_b, gate_w, gate_b, w1, b1, w2, b2, out):
    f32, f16, u32 = mybir.dt.float32, mybir.dt.float16, mybir.dt.uint32
    ALU, ACT, AX = mybir.AluOpType, mybir.ActivationFunctionType, mybir.AxisListType
    RED = bass.bass_isa.ReduceOp

    P = 128
    S, D = x.shape[1], x.shape[2]
    INNER = w_q.shape[1]
    HD = 64
    H = INNER // HD
    NW = S // P
    G = 32
    K1 = P + G
    CH = INNER // P
    GRP = 4
    NG = H // GRP
    E, F = w1.shape[0], w1.shape[2]
    CAP = 80
    SLOTS = E * CAP
    FC = F // P
    NEG = -2e38
    RMS_EPS, LN_EPS = 1e-6, 1e-5
    WS = 16.0
    EXPONENT = 0x7F800000

    ctx = ExitStack()
    with ctx:
        def sb(name, shape, dt=f32):
            return ctx.enter_context(nc.sbuf_tensor(name, shape, dt))

        def sem(name):
            return ctx.enter_context(nc.semaphore(name))

        X = sb("X", [P, NW, D])
        XN = sb("XN", [P, NW, D])
        GF = sb("GF", [P, NW, D])
        GH, GL = sb("GH", [P, NW, D], f16), sb("GL", [P, NW, D], f16)
        GTH, GTL = sb("GTH", [P, S], f16), sb("GTL", [P, S], f16)
        WB = sb("WB", [P, 5 * INNER])
        WF = [WB[:, i * INNER:(i + 1) * INNER] for i in range(4)]
        WPH, WPL = sb("WPH", [P, 4 * INNER], f16), sb("WPL", [P, 4 * INNER], f16)
        WH, WL = ([t[:, i * INNER:(i + 1) * INNER] for i in range(4)] for t in (WPH, WPL))
        nwcol, nwrow, swrow = sb("nwcol", [P, 1]), sb("nwrow", [P, D]), sb("swrow", [P, D])
        sbcol, nwabs = sb("sbcol", [P, 1]), sb("nwabs", [P, 1])
        gw_sb, gb_sb = sb("gw_sb", [P, E]), sb("gb_sb", [P, E])
        w1_sb, w2_sb = sb("w1_sb", [P, E, F]), sb("w2_sb", [P, E, FC, D])
        W1H, W1L = (t[:].rearrange("p (e f) -> p e f", f=F) for t in (WPH, WPL))
        b1r, b1c, b2b = sb("b1r", [E * FC, P]), sb("b1c", [P, E * FC]), sb("b2b", [P, E, D])

        ident = sb("ident", [P, P])
        upper = sb("upper", [P, P], f16)
        ones = sb("ones", [P, P], f16)
        mask = sb("mask", [P, K1])
        iota_g = sb("iota_g", [P, G])
        iota_s = sb("iota_s", [P, SLOTS], f16)
        ntok = sb("ntok", [P, NW])
        rev_e, base_e = sb("rev_e", [P, E]), sb("base_e", [P, E])
        mhalf = sb("mhalf", [P, NW])
        half_of = sb("half_of", [P, 2])
        zero_row = sb("zero_row", [1, D])
        epscol, idle_p, idle_v = sb("epscol", [P, 1]), sb("idle_p", [P, 1]), sb("idle_v", [P, 1])

        st6 = sb("st6", [P, NW, 6])
        mv = sb("mv", [P, NW, 2])
        vtmp, rstd, rms = sb("vtmp", [P, NW]), sb("rstd", [P, NW]), sb("rms", [P, NW])
        wmax = sb("wmax", [P, 5])
        wred, wpow, winv, wsc = (sb(n, [P, 5]) for n in ("wred", "wpow", "winv", "wsc"))
        cexp, cneg, cy, ch = (sb(n, [P, 1]) for n in ("cexp", "cneg", "cy", "ch"))

        scol = sb("scol", [P, NW])
        srow, t16 = sb("srow", [NW, P]), sb("t16", [NW, G])
        tall, tmax = sb("tall", [P, NW * G]), sb("tmax", [P, 8])
        gteq = sb("gteq", [P, NW, 2])
        gteq16, gtex16 = sb("gteq16", [P, NW, 2], f16), sb("gtex16", [P, NW, 2], f16)
        PAD = 64
        pfa, pfb = sb("pfa", [P, PAD + NW * E]), sb("pfb", [P, PAD + NW * E])
        tot16, ngt, need = sb("tot16", [P, 1], f16), sb("ngt", [P, 1]), sb("need", [P, 1])
        keq, kslot, gslot = (sb(n, [P, NW]) for n in ("keq", "kslot", "gslot"))
        OH = sb("OH", [P, NW, G], f16)
        OHN = sb("OHN", [P, NW, G])
        gi_s, gi_c = sb("gi_s", [P, G], f16), sb("gi_c", [P, G])
        GM = sb("GM", [P, NW, G])
        HGH, HGL = sb("HGH", [P, 4, G], f16), sb("HGL", [P, 4, G], f16)

        QH, QL = sb("QH", [P, CH, P], f16), sb("QL", [P, CH, P], f16)
        KNH, KNL = sb("KNH", [P, CH, P], f16), sb("KNL", [P, CH, P], f16)
        KGH, KGL = sb("KGH", [P, CH, G], f16), sb("KGL", [P, CH, G], f16)
        KPH, KPL = sb("KPH", [P, CH, 2, K1], f16), sb("KPL", [P, CH, 2, K1], f16)
        VH, VL = sb("VH", [P, INNER], f16), sb("VL", [P, INNER], f16)
        VGH, VGL = sb("VGH", [P, NG, GRP * HD], f16), sb("VGL", [P, NG, GRP * HD], f16)
        SM = sb("SM", [P, GRP, K1])
        mx, nb, ssum, rinv = (sb(n, [P, GRP]) for n in ("mx", "nb", "ssum", "rinv"))
        PR = sb("PR", [P, GRP, K1])
        PG = sb("PG", [P, GRP, G])
        PTH, PTL = sb("PTH", [P, GRP, P], f16), sb("PTL", [P, GRP, P], f16)
        PGH, PGL = sb("PGH", [P, P], f16), sb("PGL", [P, P], f16)
        OS = sb("OS", [P, INNER])
        OTH, OTL = sb("OTH", [P, CH, P], f16), sb("OTL", [P, CH, P], f16)
        R = sb("R", [P, D])
        ra, xa = sb("ra", [P, D]), sb("xa", [P, D])
        X1 = sb("X1", [P, NW, D])
        s1, m1, v1, r1 = sb("s1", [P, 6]), sb("m1", [P, 2]), sb("v1", [P, 1]), sb("r1", [P, 1])
        s2, m2, v2, r2 = sb("s2", [P, 6]), sb("m2", [P, 2]), sb("v2", [P, 1]), sb("r2", [P, 1])

        T, TH, TL = GF, GH, GL
        TT = X[:].rearrange("p w d -> p (w d)")
        L, L2, Lm = sb("L", [P, NW, E]), sb("L2", [P, NW, E]), sb("Lm", [P, NW, E])
        lmax, rv, esum, gp = (sb(n, [P, NW]) for n in ("lmax", "rv", "esum", "gp"))
        M16, MX16 = sb("M16", [P, NW, E], f16), sb("MX16", [P, NW, E], f16)
        pos, ebase, kept, slot1, slotv, gix = (sb(n, [P, NW]) for n in ("pos", "ebase", "kept", "slot1", "slotv", "gix"))
        gidx = sb("gidx", [P, NW], u32)
        SEC = WB[:].bitcast(f16).rearrange("p (w s) -> p w s", s=SLOTS)
        DTH, DTL = sb("DTH", [P, SLOTS], f16), sb("DTL", [P, SLOTS], f16)
        HA = sb("HA", [P, 2, FC * CAP])
        HS = sb("HS", [P, E, FC, CAP])
        EO = OS[0:CAP, :].rearrange("p (e d) -> p e d", d=D)
        Y = X
        OUT = XN

        ps = [ctx.enter_context(nc.psum_tensor(f"ps{i}", [P, 512], f32)) for i in range(8)]
        SB_, PJ = [ps[0], ps[1]], [ps[2], ps[3]]
        PT, PTG, OB, MISC = ps[4], ps[5], ps[6], ps[7]

        top_dram = nc.dram_tensor("top_scratch", [NW, G], f32, kind="Internal").ap()
        eo_dram = nc.dram_tensor("expert_scratch", [SLOTS + 1, D], f32, kind="Internal").ap()

        ld_x = [sem(f"ld_x{i}") for i in range(4)]
        (ld_small, ld_w, ld_moe, top_out, top_in, zrow_out, eo_out, gathered, s_out) = map(
            sem, ("ld_small", "ld_w", "ld_moe", "top_out", "top_in", "zrow_out", "eo_out", "gathered", "s_out"))
        (c_pool, c_wmax, c_wred, c_wsc, c_wh, c_wl, c_stat, c_rstd, c_g, c_gh, c_gl, c_gt, c_gth, c_gtl) = map(
            sem, ("c_pool", "c_wmax", "c_wred", "c_wsc", "c_wh", "c_wl", "c_stat", "c_rstd", "c_g", "c_gh", "c_gl",
                  "c_gt", "c_gth", "c_gtl"))
        dve_chain, pool_chain, act_chain = sem("dve_chain"), sem("pool_chain"), sem("act_chain")
        (c_scol, c_srow, c_t16, c_sel, c_cum, c_ngt, c_tot, c_oh, c_hg, c_hgs, c_gi, c_gir, c_kg, c_kgs, c_kgp,
         c_vg, c_vgh, c_vgl, c_b1) = map(
            sem, ("c_scol", "c_srow", "c_t16", "c_sel", "c_cum", "c_ngt", "c_tot", "c_oh", "c_hg", "c_hgs", "c_gi",
                  "c_gir", "c_kg", "c_kgs", "c_kgp", "c_vg", "c_vgh", "c_vgl", "c_b1"))
        (scores_done, scores_read, negmax_ready, exp_done, rinv_ready, unit_done, unit_hi, unit_lo, k_padded,
         pt_done, pt_hi, pt_lo, ptg_done, ptg_hi, ptg_lo, pv_done, o_ready, y_done, y_read, var_ready, eps_added,
         ln_rstd, ln_step, mask_set, pg_ready) = map(
            sem, ("scores_done", "scores_read", "negmax_ready", "exp_done", "rinv_ready", "unit_done", "unit_hi",
                  "unit_lo", "k_padded", "pt_done", "pt_hi", "pt_lo", "ptg_done", "ptg_hi", "ptg_lo", "pv_done",
                  "o_ready", "y_done", "y_read", "var_ready", "eps_added", "ln_rstd", "ln_step", "mask_set", "pg_ready"))
        (t_ready, tl_ready, th_ready, tt_done, tt_sb, lg_done, m_ready, lm_ready, le_ready, mcum, sec_ready,
         disp_done, dt_hi, dt_lo, h_done, h_act, h_sum, e_done, eo_sb, idx_ready, w1_hi, w1_lo, fin_var, fin_rstd,
         fin_mul, fin_add) = map(
            sem, ("t_ready", "tl_ready", "th_ready", "tt_done", "tt_sb", "lg_done", "m_ready", "lm_ready",
                  "le_ready", "mcum", "sec_ready", "disp_done", "dt_hi", "dt_lo", "h_done", "h_act", "h_sum", "e_done",
                  "eo_sb", "idx_ready", "w1_hi", "w1_lo", "fin_var", "fin_rstd", "fin_mul", "fin_add"))

        x_v = x[0].rearrange("(w p) d -> p w d", p=P)
        out_v = out[0].rearrange("(w p) d -> p w d", p=P)
        XL = 4

        UNIT = {"q0": 0, "k0": 1, "oT0": 2, "oT1": 3, "v1": 4, "k1": 5, "q1": 6, "v0": 7}

        def unit_no(name, w):
            if isinstance(w, int) and w == 0 and name in ("q0", "k0"):
                return 5 + UNIT[name]
            if isinstance(w, int) and w == NW - 1:
                return 3 + 8 * w + {"oT0": 0, "oT1": 1, "v1": 2}[name]
            if isinstance(w, int) and w == NW:
                return 3 + 8 * (w - 1) + {"oT0": 3, "oT1": 4}[name]
            return w * 8 + (3 + UNIT[name])

        def unit_bank(name, w):
            if isinstance(w, int):
                return PJ[unit_no(name, w) % 2]
            return PJ[(3 + UNIT[name]) % 2]

        FIRST = ["q0", "k0", "q1", "k1", "v0"]

        def steps(w):
            last = isinstance(w, int) and w == NW - 1
            first = isinstance(w, int) and w == 0
            ahead = lambda names: [] if last else names
            before = [ahead(["q0", "k0"]), ["v1"], ahead(["k1", "q1"]), ahead(["v0"])]
            after = [[] if first else ["oT0", "oT1"], [], [], []]
            return before, after

        def nxt(w, j):
            if j < NG - 1:
                return w, j + 1
            return None if isinstance(w, int) and w == NW - 1 else (w + 1, 0)

        with nc.Block() as block:

            @block.sync
            def _(sp):
                for i in range(NW // XL):
                    sp.dma_start(X[:, i * XL:(i + 1) * XL, :], x_v[:, i * XL:(i + 1) * XL, :]).then_inc(ld_x[i], 16)
                for i, w in enumerate((w_q, w_k, w_v)):
                    sp.dma_start(WF[i], w).then_inc(ld_w, 16)
                sp.dma_start(WF[3].rearrange("p (c d) -> p c d", d=D),
                             w_out.rearrange("(c p) d -> p c d", p=P)).then_inc(ld_w, 16)
                sp.dma_start(w1_sb[:], w1.rearrange("e d f -> d e f")).then_inc(ld_moe, 16)
                sp.dma_start(w2_sb[:], w2.rearrange("e (c p) d -> p e c d", p=P)).then_inc(ld_moe, 16)
                sp.wait_ge(c_t16, 1)
                sp.dma_start(top_dram, t16[:]).then_inc(top_out, 16)
                sp.wait_ge(top_out, 16)
                sp.dma_start(tall[:], top_dram.rearrange("(a w) g -> a (w g)", a=1).partition_broadcast(P)
                             .rearrange("p a n -> p (a n)")).then_inc(top_in, 16)
                for i in range(2):
                    sp.wait_ge(eo_sb, (i + 1) * E // 2)
                    e0, e1 = i * E // 2, (i + 1) * E // 2
                    sp.dma_start(eo_dram[e0 * CAP:e1 * CAP, :].rearrange("(e s) d -> s e d", s=CAP),
                                 EO[:, e0:e1, :]).then_inc(eo_out, 16)
                for i in range(NW // XL):
                    sp.wait_ge(fin_add, i + 1)
                    sp.dma_start(out_v[:, i * XL:(i + 1) * XL, :], OUT[:, i * XL:(i + 1) * XL, :]).then_inc(s_out, 16)
                sp.wait_ge(s_out, 16 * (NW // XL))

            @block.gpsimd
            def _(pool):
                g = nc.gpsimd
                g.memset(mhalf[:], -0.5)
                g.memset(ident[:], 0.0)
                g.memset(upper[:], 1.0)
                g.memset(ones[:], 1.0)
                g.memset(mask[:, 0:P], 0.0)
                g.memset(zero_row[:], 0.0)
                g.memset(epscol[:], LN_EPS)
                g.memset(VGH[:], 0.0)
                g.memset(VGL[:], 0.0)
                g.memset(half_of[:], 1.0)
                g.memset(pfa[:], 0.0)
                g.memset(pfb[:], 0.0)
                g.iota(iota_g[:], pattern=[[1, G]], base=1, channel_multiplier=0, allow_small_or_imprecise_dtypes=True)
                g.iota(iota_s[:], pattern=[[1, SLOTS]], base=0, channel_multiplier=0,
                       allow_small_or_imprecise_dtypes=True)
                g.iota(ntok[:], pattern=[[P, NW]], base=0, channel_multiplier=1, allow_small_or_imprecise_dtypes=True)
                g.iota(rev_e[:], pattern=[[-1, E]], base=E, channel_multiplier=0, allow_small_or_imprecise_dtypes=True)
                g.iota(base_e[:], pattern=[[CAP, E]], base=0, channel_multiplier=0,
                       allow_small_or_imprecise_dtypes=True).then_inc(pool_chain, 1)
                pool.wait_ge(pool_chain, 1)
                g.affine_select(out=ident[:], in_=ident[:], compare_op=ALU.not_equal, fill=1.0, base=0,
                                pattern=[[-1, P]], channel_multiplier=1)
                g.affine_select(out=upper[:], in_=upper[:], compare_op=ALU.is_ge, fill=0.0, base=0,
                                pattern=[[1, P]], channel_multiplier=-1)
                g.affine_select(out=mask[:, 0:P], in_=mask[:, 0:P], compare_op=ALU.is_ge, fill=NEG, base=0,
                                pattern=[[-1, P]], channel_multiplier=1)
                g.affine_select(out=half_of[:, 0:1], in_=half_of[:, 0:1], compare_op=ALU.is_ge, fill=0.0, base=HD - 1,
                                pattern=[[0, 1]], channel_multiplier=-1)
                g.affine_select(out=half_of[:, 1:2], in_=half_of[:, 1:2], compare_op=ALU.is_ge, fill=0.0, base=-HD,
                                pattern=[[0, 1]], channel_multiplier=1).then_inc(c_pool, 1)
                g.dma_start(eo_dram[SLOTS:SLOTS + 1, :], zero_row[:]).then_inc(zrow_out, 16)

                for i in range(2):
                    pool.wait_ge(c_stat, i + 1)
                    dst = (rstd, rms)[i]
                    g.tensor_tensor(dst[:], vtmp[:], mhalf[:], ALU.pow).then_inc(c_rstd, 1)
                pool.wait_ge(c_wmax, 1)
                g.partition_all_reduce(wred[:], wmax[:], P, RED.max).then_inc(c_wred, 1)

                pool.wait_ge(c_kgs, 1)
                for src, dst in ((KGH, KPH), (KGL, KPL)):
                    for a in range(2):
                        last = g.tensor_scalar(dst[:, :, a, P:K1], src[:], half_of[:, a:a + 1], 1.0, ALU.mult, ALU.mult)
                last.then_inc(c_kgp, 1)

                def pad_keys(half, hi_count, lo_count, scores_count, pads_before):
                    pool.wait_ge(unit_hi, hi_count)
                    pool.wait_ge(unit_lo, lo_count)
                    if scores_count is not None:
                        pool.wait_ge(scores_done, scores_count)
                    if pads_before is not None:
                        pool.wait_ge(k_padded, pads_before)
                    g.tensor_tensor(idle_p[:], mhalf[:, 0:1], mhalf[:, 0:1], ALU.add)
                    c0, c1 = half * CH // 2, (half + 1) * CH // 2
                    for src, dst in ((KNH, KPH), (KNL, KPL)):
                        for a in range(2):
                            last = g.tensor_scalar(dst[:, c0:c1, a, 0:P], src[:, c0:c1, :], half_of[:, a:a + 1], 1.0,
                                                   ALU.mult, ALU.mult)
                    last.then_inc(k_padded, 1)

                def ln_pow(n, var, vt, r):
                    pool.wait_ge(var_ready, n)
                    g.tensor_tensor(vt[:], var[:, 1:2], epscol[:], ALU.add).then_inc(eps_added, 1)
                    pool.wait_ge(eps_added, n)
                    g.tensor_tensor(r[:], vt[:], mhalf[:, 0:1], ALU.pow).then_inc(ln_rstd, 1)

                def body(w, first=False, last=False):
                    if not last:
                        n = unit_no("k0", w) + 1
                        pad_keys(0, n, n, w * 8 + 4, w * 2 + 2)
                    if not first:
                        ln_pow(w * 2 - 1, m1, v1, r1)
                    if not last:
                        n = unit_no("k1", w) + 1
                        pad_keys(1, n, n, w * 8 + 8, w * 2 + 3)
                    if not first:
                        ln_pow(w * 2, m2, v2, r2)

                pad_keys(0, 2, 2, None, None)
                pad_keys(1, 4, 4, None, 1)
                body(0, first=True)
                with pool.Fori(1, NW - 1) as w:
                    body(w)
                body(NW - 1, last=True)
                ln_pow(2 * NW - 1, m1, v1, r1)
                ln_pow(2 * NW, m2, v2, r2)

                for i in range(4):
                    q = slice(i * NW // 4, (i + 1) * NW // 4)
                    pool.wait_ge(t_ready, NW)
                    pool.wait_ge(th_ready, i + 1)
                    g.tensor_tensor(TL[:, q, :], T[:, q, :], TH[:, q, :], ALU.subtract).then_inc(tl_ready, 1)

                pool.wait_ge(idx_ready, 1)
                pool.wait_ge(eo_out, 32)
                pool.wait_ge(zrow_out, 16)
                for w in range(NW):
                    g.indirect_dma_start(out=Y[:, w, :], out_offset=None, in_=eo_dram,
                                         in_offset=bass.IndirectOffsetOnAxis(ap=gidx[:, w:w + 1], axis=0)
                                         ).then_inc(gathered, 16)
                for i in range(NW // XL):
                    c = slice(i * XL, (i + 1) * XL)
                    pool.wait_ge(fin_var, i + 1)
                    g.tensor_tensor(rstd[:, c], vtmp[:, c], mhalf[:, c], ALU.pow).then_inc(fin_rstd, 1)

            @block.scalar
            def _(act):
                a_ = nc.scalar
                act.dma_start(nwcol[:], norm_w.rearrange("(p a) -> p a", a=1)).then_inc(ld_small, 16)
                act.dma_start(nwrow[:], norm_w.rearrange("(a d) -> a d", a=1).partition_broadcast(P)
                              .rearrange("p a d -> p (a d)")).then_inc(ld_small, 16)
                act.dma_start(swrow[:], scorer_w.rearrange("d a -> a d").partition_broadcast(P)
                              .rearrange("p a d -> p (a d)")).then_inc(ld_small, 16)
                act.dma_start(sbcol[:], scorer_b.rearrange("(a d) -> a d", a=1).partition_broadcast(P)
                              .rearrange("p a d -> p (a d)")).then_inc(ld_small, 16)
                act.dma_start(gw_sb[:], gate_w).then_inc(ld_small, 16)
                act.dma_start(gb_sb[:], gate_b.rearrange("(a d) -> a d", a=1).partition_broadcast(P)
                              .rearrange("p a d -> p (a d)")).then_inc(ld_small, 16)
                act.dma_start(b1r[:], b1.rearrange("e (c p) -> (e c) p", p=P)).then_inc(ld_small, 16)
                act.dma_start(b2b[:], b2.rearrange("(a e) d -> a (e d)", a=1).partition_broadcast(P)
                              .rearrange("p a (e d) -> p (a e) d", e=E)).then_inc(ld_small, 16)

                act.wait_ge(c_g, 1)
                a_.activation(GH[:], GF[:], ACT.Copy).then_inc(c_gh, 1)
                for i in range(4):
                    act.wait_ge(c_gt, i + 1)
                    a_.activation(GTH[:, i * 512:(i + 1) * 512], PJ[i % 2][:], ACT.Copy).then_inc(c_gth, 1)
                act.wait_ge(c_wsc, 1)
                for i in range(4):
                    a_.activation(WH[i], WF[i], ACT.Copy, scale=wsc[:, i:i + 1]).then_inc(c_wh, 1)

                def head_of(unit, dst, bank):
                    act.wait_ge(unit_done, unit + 1)
                    a_.activation(dst, bank[:], ACT.Copy).then_inc(unit_hi, 1)

                def dest(name):
                    half = int(name[-1])
                    if name[0] == "v":
                        return VH[:, half * 512:(half + 1) * 512]
                    t = {"q": QH, "k": KNH, "o": OTH}[name[0]]
                    return t[:, half * 4:(half + 1) * 4, :].rearrange("p c n -> p (c n)")

                for i, name in enumerate(FIRST):
                    head_of(i, dest(name), PJ[i % 2])

                act.wait_ge(c_vg, 1)
                for half in range(2):
                    for i in range(GRP):
                        src = PT if half == 0 else OB
                        last = a_.activation(
                            VGH[i * G:(i + 1) * G, half * 2:half * 2 + 2, i * HD:(i + 1) * HD],
                            src[i * G:(i + 1) * G, :].rearrange("p (j i d) -> p j i d", j=2, i=GRP)[:, :, i, :], ACT.Copy)
                last.then_inc(c_vgh, 1)

                def exps(w, j):
                    act.wait_ge(negmax_ready, w * 4 + (j + 1))
                    if not (isinstance(w, int) and w == 0 and j == 0):
                        act.wait_ge(rinv_ready, w * 4 + j)
                        act.wait_ge(pg_ready, w * 4 + j)
                        act.wait_ge(pt_done, w * 4 + j)
                    for i in range(GRP):
                        last = a_.activation(PR[:, i, :], SM[:, i, :], ACT.Exp, bias=nb[:, i:i + 1], scale=cexp[:],
                                             accum_out=ssum[:, i:i + 1])
                    last.then_inc(exp_done, 1)

                def body(w, first=False, last=False):
                    before, after = steps(w)
                    for j in range(NG):
                        for name in before[j]:
                            if name == "v1" and not first:
                                act.wait_ge(pv_done, w * 4)
                            if name == "v0":
                                act.wait_ge(pv_done, w * 4 + 2)
                            if name in ("q0", "k0"):
                                act.wait_ge(scores_done, w * 8 + 4)
                                act.wait_ge(k_padded, w * 2 + 1)
                            if name in ("q1", "k1"):
                                act.wait_ge(scores_done, w * 8 + 8)
                                act.wait_ge(k_padded, w * 2 + 2)
                            head_of(unit_no(name, w), dest(name), unit_bank(name, w))
                        if not (first and j == 0):
                            act.wait_ge(pv_done, w * 4 + j)
                        act.wait_ge(pt_done, w * 4 + (j + 1))
                        a_.activation(PTH[:].rearrange("p h n -> p (h n)"), PT[:], ACT.Copy).then_inc(pt_hi, 1)
                        act.wait_ge(ptg_done, w * 4 + (j + 1))
                        a_.activation(PGH[:], PTG[:, 0:P], ACT.Copy).then_inc(ptg_hi, 1)
                        for name in after[j]:
                            head_of(unit_no(name, w), dest(name), unit_bank(name, w))
                        n = nxt(w, j)
                        if n:
                            exps(*n)

                exps(0, 0)
                body(0, first=True)
                with act.Fori(1, NW - 1) as w:
                    body(w)
                body(NW - 1, last=True)
                for name in ("oT0", "oT1"):
                    head_of(unit_no(name, NW), dest(name), unit_bank(name, NW))

                act.wait_ge(t_ready, NW)
                for i in range(4):
                    q = slice(i * NW // 4, (i + 1) * NW // 4)
                    a_.activation(TH[:, q, :], T[:, q, :], ACT.Copy).then_inc(th_ready, 1)
                for i in range(4):
                    act.wait_ge(tt_done, i + 1)
                    a_.activation(TT[:, i * 512:(i + 1) * 512], ps[i][:], ACT.Copy).then_inc(tt_sb, 1)
                for i in range(4):
                    a_.activation(W1H[:, 2 * i:2 * i + 2, :], w1_sb[:, 2 * i:2 * i + 2, :], ACT.Copy,
                                  scale=wsc[:, 4:5]).then_inc(w1_hi, 1)
                act.wait_ge(lm_ready, 1)
                a_.activation(L2[:], Lm[:], ACT.Exp).then_inc(le_ready, 1)
                act.wait_ge(disp_done, 1)
                a_.activation(DTH[:, 0:512], ps[0][:], ACT.Copy).then_inc(dt_hi, 1)
                a_.activation(DTH[:, 512:SLOTS], ps[1][:, 0:SLOTS - 512], ACT.Copy).then_inc(dt_hi, 1)
                for e in range(E):
                    act.wait_ge(h_sum, e + 1)
                    a_.activation(HS[:, e].rearrange("p c s -> p (c s)"), HA[:, e % 2, :], ACT.Gelu_apprx_tanh
                                  ).then_inc(h_act, 1)

            @block.vector
            def _(dve):
                v = nc.vector
                chain = [0]

                def link(ins):
                    chain[0] += 1
                    ins.then_inc(dve_chain, 1)
                    dve.wait_ge(dve_chain, chain[0])

                for w in range(NW):
                    if w % XL == 0:
                        dve.wait_ge(ld_x[w // XL], 16)
                    last = v.bn_stats(st6[:, w, :], X[:, w, :])
                link(last)
                for w in range(NW):
                    last = v.bn_aggr(mv[:, w, :], st6[:, w, :])
                link(last)
                v.tensor_scalar(vtmp[:], mv[:, :, 1], LN_EPS, None, ALU.add).then_inc(c_stat, 1)
                dve.wait_ge(c_rstd, 1)
                link(v.tensor_tensor(rms[:], rstd[:], rstd[:], ALU.mult))
                link(v.tensor_tensor(rms[:], rms[:], mv[:, :, 1], ALU.mult))
                v.tensor_scalar(vtmp[:], rms[:], RMS_EPS, None, ALU.add).then_inc(c_stat, 1)
                for w in range(NW):
                    last = v.tensor_scalar(XN[:, w, :], X[:, w, :], mv[:, w, 0:1], rstd[:, w:w + 1],
                                           ALU.subtract, ALU.mult)
                link(last)
                dve.wait_ge(c_rstd, 2)
                for w in range(NW):
                    last = v.tensor_scalar(GF[:, w, :], XN[:, w, :], rms[:, w:w + 1], None, ALU.mult)
                last.then_inc(c_g, 1)
                dve.wait_ge(c_g, 1)

                dve.wait_ge(ld_small, 16 * 8)
                link(v.tensor_tensor(nwrow[:], nwrow[:], swrow[:], ALU.mult))
                for w in range(NW):
                    last = v.tensor_tensor_reduce(out=X1[:, w, :], in0=GF[:, w, :], in1=nwrow[:], scale=1.0, scalar=0.0,
                                                  op0=ALU.mult, op1=ALU.add, accum_out=scol[:, w:w + 1])
                link(last)
                v.tensor_scalar(scol[:], scol[:], sbcol[:], None, ALU.add).then_inc(c_scol, 1)

                dve.wait_ge(ld_w, 64)
                dve.wait_ge(ld_moe, 32)
                for i in range(4):
                    v.tensor_reduce(wmax[:, i:i + 1], WF[i], AX.X, ALU.max, apply_absolute_value=True)
                link(v.tensor_reduce(wmax[:, 4:5], w1_sb[:], AX.XY, ALU.max, apply_absolute_value=True))
                link(v.tensor_reduce(nwabs[:], nwcol[:], AX.X, ALU.max, apply_absolute_value=True))
                v.tensor_scalar(wmax[:, 0:3], wmax[:, 0:3], nwabs[:], None, ALU.mult).then_inc(c_wmax, 1)

                dve.wait_ge(c_gh, 1)
                v.tensor_tensor(GL[:], GF[:], GH[:], ALU.subtract).then_inc(c_gl, 1)
                for i in range(4):
                    dve.wait_ge(c_gth, i + 1)
                    v.tensor_tensor(GTL[:, i * 512:(i + 1) * 512], PJ[i % 2][:], GTH[:, i * 512:(i + 1) * 512],
                                    ALU.subtract).then_inc(c_gtl, 1)

                dve.wait_ge(c_wred, 1)
                link(v.tensor_scalar(wred[:], wred[:], 1e-30, None, ALU.max))
                link(v.tensor_scalar(wpow[:].bitcast(u32), wred[:].bitcast(u32), EXPONENT, None, ALU.bitwise_and))
                link(v.reciprocal(winv[:], wpow[:]))
                link(v.tensor_scalar(wsc[:], winv[:], WS, None, ALU.mult))
                link(v.tensor_scalar(wsc[:, 0:3], wsc[:, 0:3], nwcol[:], None, ALU.mult))
                link(v.tensor_tensor(cexp[:], wpow[:, 0:1], wpow[:, 1:2], ALU.mult))
                v.tensor_scalar(cneg[:], cexp[:], -(HD ** -0.5) / WS ** 2, None, ALU.mult)
                link(v.tensor_scalar(cexp[:], cexp[:], (HD ** -0.5) / WS ** 2, None, ALU.mult))
                link(v.tensor_tensor(cy[:], wpow[:, 2:3], wpow[:, 3:4], ALU.mult))
                v.tensor_scalar(cy[:], cy[:], 1 / WS ** 2, None, ALU.mult)
                v.tensor_scalar(ch[:], wpow[:, 4:5], 1 / WS, None, ALU.mult).then_inc(c_wsc, 1)
                for i in range(4):
                    dve.wait_ge(c_wh, i + 1)
                    v.scalar_tensor_tensor(WL[i], WF[i], wsc[:, i:i + 1], WH[i], ALU.mult, ALU.subtract
                                           ).then_inc(c_wl, 1)

                dve.wait_ge(c_srow, 1)
                link(v.tensor_copy(srow[:], MISC[0:NW, 0:P]))
                for r in range(G // 8):
                    link(v.max(t16[:, 8 * r:8 * r + 8], srow[:]))
                    if r < G // 8 - 1:
                        link(v.match_replace(srow[:], t16[:, 8 * r:8 * r + 8], srow[:], -3e38))
                dve.sem_inc(c_t16, 1)
                def rest_of(unit, dst, hi, bank):
                    dve.wait_ge(unit_hi, unit + 1)
                    v.tensor_tensor(dst, bank[:], hi, ALU.subtract).then_inc(unit_lo, 1)

                def parts(name):
                    half = int(name[-1])
                    if name[0] == "v":
                        return VL[:, half * 512:(half + 1) * 512], VH[:, half * 512:(half + 1) * 512]
                    return [t[:, half * 4:(half + 1) * 4, :].rearrange("p c n -> p (c n)") for t in
                            {"q": (QL, QH), "k": (KNL, KNH), "o": (OTL, OTH)}[name[0]]]

                for i, name in enumerate(FIRST):
                    rest_of(i, *parts(name), PJ[i % 2])
                dve.wait_ge(top_in, 16)
                for r in range(G // 8):
                    link(v.max(tmax[:], tall[:]))
                    if r < G // 8 - 1:
                        link(v.match_replace(tall[:], tmax[:], tall[:], -3e38))
                v.tensor_scalar(gteq[:, :, 0], scol[:], tmax[:, 7:8], None, ALU.is_gt)
                link(v.tensor_scalar(gteq[:, :, 1], scol[:], tmax[:, 7:8], None, ALU.is_equal))
                dve.wait_ge(c_pool, 1)

                def window_prefix(src, n):
                    a, b = pfa, pfb
                    link(v.tensor_copy(a[:, PAD:PAD + NW * n], src))
                    k = n
                    while k < NW * n:
                        link(v.tensor_tensor(b[:, PAD:PAD + NW * n], a[:, PAD:PAD + NW * n],
                                             a[:, PAD - k:PAD + NW * n - k], ALU.add))
                        a, b = b, a
                        k *= 2
                    return a

                pf = window_prefix(gteq[:].rearrange("p w e -> p (w e)"), 2)
                v.tensor_copy(gteq16[:], gteq[:])
                v.tensor_copy(tot16[:], pf[:, PAD + 2 * NW - 2:PAD + 2 * NW - 1])
                v.tensor_copy(gtex16[:].rearrange("p w e -> p (w e)"), pf[:, PAD - 2:PAD + 2 * NW - 2]).then_inc(c_sel, 1)
                dve.wait_ge(c_cum, 1)
                cum = MISC[:, 128:128 + 2 * NW].rearrange("p (w e) -> p w e", e=2)
                link(v.tensor_copy(ngt[:], MISC[:, 192:193]))
                link(v.tensor_scalar(need[:], ngt[:], -1.0, float(G), ALU.mult, ALU.add))
                link(v.tensor_scalar(keq[:], cum[:, :, 1], need[:], None, ALU.is_le))
                link(v.tensor_tensor(keq[:], keq[:], gteq[:, :, 1], ALU.mult))
                link(v.tensor_scalar(kslot[:], cum[:, :, 1], ngt[:], None, ALU.add))
                link(v.tensor_tensor(kslot[:], kslot[:], keq[:], ALU.mult))
                link(v.tensor_tensor(gslot[:], cum[:, :, 0], gteq[:, :, 0], ALU.mult))
                link(v.tensor_tensor(gslot[:], gslot[:], kslot[:], ALU.add))
                link(v.tensor_tensor(OH[:], gslot[:].unsqueeze(2).broadcast_to([P, NW, G]),
                                     iota_g[:].unsqueeze(1).broadcast_to([P, NW, G]), ALU.is_equal))
                dve.sem_inc(c_oh, 1)
                link(v.tensor_tensor(OHN[:], OH[:], ntok[:].unsqueeze(2).broadcast_to([P, NW, G]), ALU.mult))
                link(v.tensor_reduce(gi_c[:], OHN[:].rearrange("p w g -> p g w"), AX.X, ALU.add))
                v.tensor_copy(gi_s[:], gi_c[:]).then_inc(c_gi, 1)
                dve.wait_ge(c_gir, 1)
                link(v.tensor_copy(gi_c[:], MISC[:, 256:256 + G]))
                link(v.tensor_tensor(GM[:], gi_c[:].unsqueeze(1).broadcast_to([P, NW, G]),
                                     ntok[:].unsqueeze(2).broadcast_to([P, NW, G]), ALU.is_gt))
                link(v.tensor_scalar(GM[:], GM[:], NEG, None, ALU.mult))
                dve.wait_ge(c_hg, 1)
                v.tensor_copy(HGH[:], PT[:, 0:G].unsqueeze(1).broadcast_to([P, 4, G]))
                v.tensor_copy(HGL[:], PT[:, G:2 * G].unsqueeze(1).broadcast_to([P, 4, G])).then_inc(c_hgs, 1)
                dve.wait_ge(c_kg, 1)
                kg = PTG[:, 0:CH * G].rearrange("p (c g) -> p c g", g=G)
                link(v.tensor_copy(KGH[:], kg))
                v.tensor_tensor(KGL[:], kg, KGH[:], ALU.subtract).then_inc(c_kgs, 1)

                dve.wait_ge(c_vgh, 1)
                for half in range(2):
                    for i in range(GRP):
                        src = PT if half == 0 else OB
                        dst = (slice(i * G, (i + 1) * G), slice(half * 2, half * 2 + 2), slice(i * HD, (i + 1) * HD))
                        last = v.tensor_tensor(
                            VGL[dst], src[i * G:(i + 1) * G, :].rearrange("p (j i d) -> p j i d", j=2, i=GRP)[:, :, i, :],
                            VGH[dst], ALU.subtract)
                last.then_inc(c_vgl, 1)
                dve.wait_ge(c_b1, 1)
                v.tensor_copy(b1c[:], MISC[:, 448:448 + E * FC]).then_inc(y_read, 1)

                def maxima(w, j):
                    if j == 0:
                        if not (isinstance(w, int) and w == 0):
                            dve.wait_ge(scores_read, w * 4)
                        v.tensor_copy(mask[:, P:K1], GM[:, w, :]).then_inc(mask_set, 1)
                        dve.wait_ge(mask_set, w + 1)
                        v.memset(idle_v[:], 0.0)
                    for i in range(GRP):
                        last = v.tensor_tensor_reduce(out=SM[:, i, :], in0=SB_[i // 2][:, (i % 2) * K1:(i % 2 + 1) * K1],
                                                      in1=mask[:], scale=1.0, scalar=-3e38, op0=ALU.add, op1=ALU.max,
                                                      accum_out=mx[:, i:i + 1])
                    last.then_inc(scores_read, 1)
                    dve.wait_ge(scores_read, w * 4 + (j + 1))
                    v.tensor_scalar(nb[:], mx[:], cneg[:], None, ALU.mult).then_inc(negmax_ready, 1)

                def take_o(w, j, first=False):
                    dve.wait_ge(pv_done, w * 4 + (j + 1))
                    if j == 0 and not first:
                        dve.wait_ge(unit_done, (w * 8 + (3 + UNIT["oT1"] + 1)) if not isinstance(w, int)
                                    else unit_no("oT1", w) + 1)
                    v.tensor_tensor(OS[:, j * GRP * HD:(j + 1) * GRP * HD].rearrange("p (h d) -> p h d", d=HD),
                                    OB[:, 0:GRP * HD].rearrange("p (h d) -> p h d", d=HD),
                                    rinv[:].unsqueeze(2).broadcast_to([P, GRP, HD]), ALU.mult).then_inc(o_ready, 1)

                def take_r(w):
                    dve.wait_ge(y_done, w)
                    v.scalar_tensor_tensor(R[:], MISC[:, 0:D], cy[:], XN[:, w - 1, :], ALU.mult, ALU.add
                                           ).then_inc(y_read, 1)
                    dve.wait_ge(y_read, w + 1)
                    v.bn_stats(s1[:], R[:]).then_inc(ln_step, 1)
                    dve.wait_ge(ln_step, w * 6 - 5)
                    v.memset(idle_v[:], 0.0)
                    v.bn_aggr(m1[:], s1[:]).then_inc(var_ready, 1)

                def take_x1(w):
                    dve.wait_ge(ln_rstd, w * 2 - 1)
                    dve.wait_ge(var_ready, w * 2 - 1)
                    v.tensor_scalar(ra[:], R[:], m1[:, 0:1], r1[:], ALU.subtract, ALU.mult).then_inc(ln_step, 1)
                    dve.wait_ge(ln_step, w * 6 - 4)
                    v.tensor_tensor(xa[:], ra[:], X[:, w - 1, :], ALU.add).then_inc(ln_step, 1)
                    dve.wait_ge(ln_step, w * 6 - 3)
                    v.bn_stats(s2[:], xa[:]).then_inc(ln_step, 1)
                    dve.wait_ge(ln_step, w * 6 - 2)
                    v.tensor_copy(X1[:, w - 1, :], xa[:])
                    v.bn_aggr(m2[:], s2[:]).then_inc(var_ready, 1)

                def take_t(w):
                    dve.wait_ge(ln_rstd, w * 2)
                    dve.wait_ge(var_ready, w * 2)
                    v.tensor_scalar(ra[:], xa[:], m2[:, 0:1], r2[:], ALU.subtract, ALU.mult).then_inc(ln_step, 1)
                    dve.wait_ge(ln_step, w * 6 - 1)
                    v.tensor_copy(T[:, w - 1, :], ra[:]).then_inc(t_ready, 1)
                    v.nop().then_inc(ln_step, 1)

                def body(w, first=False, last=False):
                    before, after = steps(w)
                    for j in range(NG):
                        if j > 0:
                            take_o(w, j - 1, first)
                        elif not first:
                            take_o(w - 1, NG - 1)
                        dve.wait_ge(exp_done, w * 4 + (j + 1))
                        if not (first and j == 0):
                            dve.wait_ge(o_ready, w * 4 + j)
                        v.reciprocal(rinv[:], ssum[:]).then_inc(rinv_ready, 1)
                        if not (first and j == 0):
                            dve.wait_ge(ptg_done, w * 4 + j)
                        n = nxt(w, j)
                        if n:
                            dve.wait_ge(scores_done, n[0] * 8 + (2 * n[1] + 2))
                        v.tensor_copy(PG[:], PR[:, :, P:K1]).then_inc(pg_ready, 1)
                        if n:
                            maxima(*n)
                        dve.wait_ge(rinv_ready, w * 4 + (j + 1))
                        for name in before[j]:
                            rest_of(unit_no(name, w), *parts(name), unit_bank(name, w))
                        dve.wait_ge(pt_hi, w * 4 + (j + 1))
                        v.tensor_tensor(PTL[:].rearrange("p h n -> p (h n)"), PT[:],
                                        PTH[:].rearrange("p h n -> p (h n)"), ALU.subtract).then_inc(pt_lo, 1)
                        dve.wait_ge(ptg_hi, w * 4 + (j + 1))
                        v.tensor_tensor(PGL[:], PTG[:, 0:P], PGH[:], ALU.subtract).then_inc(ptg_lo, 1)
                        for name in after[j]:
                            rest_of(unit_no(name, w), *parts(name), unit_bank(name, w))
                        if not first:
                            if j == 1:
                                take_r(w)
                            if j == 2:
                                take_x1(w)
                            if j == 3:
                                take_t(w)

                dve.wait_ge(scores_done, 2)
                maxima(0, 0)
                body(0, first=True)
                with dve.Fori(1, NW - 1) as w:
                    body(w)
                body(NW - 1, last=True)
                take_o(NW - 1, NG - 1)
                for name in ("oT0", "oT1"):
                    rest_of(unit_no(name, NW), *parts(name), unit_bank(name, NW))
                take_r(NW)
                take_x1(NW)
                take_t(NW)

                dve.wait_ge(lg_done, 1)
                link(v.tensor_tensor(L[:], MISC[:, 0:NW * E].rearrange("p (w e) -> p w e", e=E),
                                     gb_sb[:].unsqueeze(1).broadcast_to([P, NW, E]), ALU.add))
                link(v.tensor_reduce(lmax[:], L[:], AX.X, ALU.max))
                lmax_b = lmax[:].unsqueeze(2).broadcast_to([P, NW, E])
                v.tensor_tensor(Lm[:], L[:], lmax_b, ALU.subtract).then_inc(lm_ready, 1)
                link(v.tensor_tensor(L[:], L[:], lmax_b, ALU.is_equal))
                link(v.tensor_tensor(L[:], L[:], rev_e[:].unsqueeze(1).broadcast_to([P, NW, E]), ALU.mult))
                link(v.tensor_reduce(rv[:], L[:], AX.X, ALU.max))
                link(v.tensor_tensor(L[:], L[:], rv[:].unsqueeze(2).broadcast_to([P, NW, E]), ALU.is_equal))
                link(v.memset(pfa[:, 0:PAD], 0.0))
                pf = window_prefix(L[:].rearrange("p w e -> p (w e)"), E)
                v.tensor_copy(M16[:], L[:])
                v.tensor_copy(MX16[:].rearrange("p w e -> p (w e)"), pf[:, PAD - E:PAD + NW * E - E]).then_inc(m_ready, 1)
                dve.wait_ge(le_ready, 1)
                link(v.tensor_reduce(esum[:], L2[:], AX.X, ALU.add))
                v.reciprocal(gp[:], esum[:])
                link(v.tensor_tensor(L2[:], L[:], base_e[:].unsqueeze(1).broadcast_to([P, NW, E]), ALU.mult))
                link(v.tensor_reduce(ebase[:], L2[:], AX.X, ALU.add))
                dve.wait_ge(mcum, 1)
                link(v.tensor_tensor(L[:], MISC[:, 128:128 + NW * E].rearrange("p (w e) -> p w e", e=E), L[:], ALU.mult))
                link(v.tensor_reduce(pos[:], L[:], AX.X, ALU.add))
                v.tensor_scalar(kept[:], pos[:], float(CAP), None, ALU.is_le)
                link(v.tensor_tensor(slot1[:], pos[:], ebase[:], ALU.add))
                link(v.tensor_tensor(slot1[:], slot1[:], kept[:], ALU.mult))
                link(v.tensor_scalar(slotv[:], slot1[:], -1.0, None, ALU.add))
                for w in range(NW):
                    v.tensor_scalar(SEC[:, w, :], iota_s[:], slotv[:, w:w + 1], None, ALU.is_equal).then_inc(sec_ready, 1)
                link(v.tensor_scalar(gix[:], kept[:], -float(SLOTS + 1), float(SLOTS + 1), ALU.mult, ALU.add))
                link(v.tensor_tensor(gix[:], gix[:], slotv[:], ALU.add))
                v.tensor_copy(gidx[:], gix[:]).then_inc(idx_ready, 1)
                for i in range(4):
                    dve.wait_ge(w1_hi, i + 1)
                    e = slice(2 * i, 2 * i + 2)
                    v.scalar_tensor_tensor(W1L[:, e].rearrange("p e f -> p (e f)"), w1_sb[:, e].rearrange("p e f -> p (e f)"),
                                           wsc[:, 4:5], W1H[:, e].rearrange("p e f -> p (e f)"), ALU.mult, ALU.subtract
                                           ).then_inc(w1_lo, 1)
                dve.wait_ge(dt_hi, 1)
                v.tensor_tensor(DTL[:, 0:512], ps[0][:], DTH[:, 0:512], ALU.subtract).then_inc(dt_lo, 1)
                dve.wait_ge(dt_hi, 2)
                v.tensor_tensor(DTL[:, 512:SLOTS], ps[1][:, 0:SLOTS - 512], DTH[:, 512:SLOTS], ALU.subtract).then_inc(dt_lo, 1)

                def bias_out(e):
                    dve.wait_ge(e_done, e + 1)
                    v.tensor_tensor(EO[:, e, :], ps[6 + e % 2][0:CAP, 0:D], b2b[0:CAP, e, :], ALU.add).then_inc(eo_sb, 1)

                for e in range(E):
                    dve.wait_ge(h_done, e + 1)
                    if e >= 2:
                        dve.wait_ge(h_act, e - 1)
                    v.scalar_tensor_tensor(HA[:, e % 2, :].rearrange("p (c s) -> p c s", s=CAP),
                                           ps[2 + e % 4][:, 0:FC * CAP].rearrange("p (c s) -> p c s", s=CAP), ch[:],
                                           b1c[:, e * FC:(e + 1) * FC].unsqueeze(2).broadcast_to([P, FC, CAP]),
                                           ALU.mult, ALU.add).then_inc(h_sum, 1)
                    if e >= 1:
                        bias_out(e - 1)
                bias_out(E - 1)

                for i in range(NW // XL):
                    c = slice(i * XL, (i + 1) * XL)
                    dve.wait_ge(gathered, 16 * NW)
                    for w in range(i * XL, (i + 1) * XL):
                        last = v.bn_stats(st6[:, w, :], Y[:, w, :])
                    link(last)
                    for w in range(i * XL, (i + 1) * XL):
                        last = v.bn_aggr(mv[:, w, :], st6[:, w, :])
                    link(last)
                    link(v.tensor_tensor(vtmp[:, c], mv[:, c, 1], gp[:, c], ALU.mult))
                    link(v.tensor_tensor(vtmp[:, c], vtmp[:, c], gp[:, c], ALU.mult))
                    link(v.tensor_scalar(vtmp[:, c], vtmp[:, c], LN_EPS, None, ALU.add))
                    dve.sem_inc(fin_var, 1)
                for i in range(NW // XL):
                    c = slice(i * XL, (i + 1) * XL)
                    dve.wait_ge(fin_rstd, i + 1)
                    link(v.tensor_tensor(rms[:, c], rstd[:, c], gp[:, c], ALU.mult))
                    for w in range(i * XL, (i + 1) * XL):
                        last = v.tensor_scalar(Y[:, w, :], Y[:, w, :], mv[:, w, 0:1], rms[:, w:w + 1],
                                               ALU.subtract, ALU.mult)
                    link(last)
                    v.tensor_tensor(OUT[:, c, :], Y[:, c, :], X1[:, c, :], ALU.add).then_inc(fin_add, 1)

            @block.tensor
            def _(pe):
                mm, tr = nc.tensor.matmul, nc.tensor.transpose

                def three(dst, lh, ll, rh, rl, start, stop):
                    mm(dst, lh, rh, start=start, stop=False)
                    mm(dst, lh, rl, start=False, stop=False)
                    return mm(dst, ll, rh, start=False, stop=stop)

                pe.wait_ge(c_pool, 1)
                pe.wait_ge(c_g, 1)
                for i in range(4):
                    if i >= 2:
                        pe.wait_ge(c_gtl, i - 1)
                    for k in range(4):
                        last = tr(PJ[i % 2][:, k * P:(k + 1) * P], GF[:, 4 * i + k, :], ident[:])
                    last.then_inc(c_gt, 1)
                pe.wait_ge(c_scol, 1)
                tr(MISC[0:NW, 0:P], scol[:], ident[:]).then_inc(c_srow, 1)

                def weight_unit(name, w, bank, unit, count_inc=True):
                    if unit is not None:
                        pe.wait_ge(unit_lo, unit - 1)
                    half = int(name[-1])
                    gh, gl = GTH[:, bass.ts(w, P)], GTL[:, bass.ts(w, P)]
                    if name[0] == "v":
                        f = slice(half * 512, (half + 1) * 512)
                        last = three(bank[:], gh, gl, WH[2][:, f], WL[2][:, f], True, True)
                    else:
                        i = "qk".index(name[0])
                        for c in range(4):
                            f = slice((half * 4 + c) * P, (half * 4 + c + 1) * P)
                            last = three(bank[:, c * P:(c + 1) * P], WH[i][:, f], WL[i][:, f], gh, gl, True, True)
                    last.then_inc(unit_done, 1)

                pe.wait_ge(c_wl, 3)
                pe.wait_ge(c_gtl, 4)
                for i, name in enumerate(FIRST):
                    weight_unit(name, 0, PJ[i % 2], i if i >= 2 else None)

                pe.wait_ge(c_sel, 1)
                mm(MISC[:, 128:128 + 2 * NW], upper[:], gteq16[:].rearrange("p w e -> p (w e)"), start=True, stop=False)
                mm(MISC[:, 128:128 + 2 * NW], ones[:], gtex16[:].rearrange("p w e -> p (w e)"), start=False, stop=True)
                mm(MISC[:, 192:193], ones[:], tot16[:], start=True, stop=True).then_inc(c_cum, 1)
                pe.wait_ge(c_gi, 1)
                mm(MISC[:, 256:256 + G], ones[:], gi_s[:], start=True, stop=True).then_inc(c_gir, 1)
                pe.wait_ge(c_gl, 1)
                for part, src in ((0, GH), (G, GL)):
                    for w in range(NW):
                        last = mm(PT[:, part:part + G], src[:, w, :], OH[:, w, :], start=(w == 0), stop=(w == NW - 1))
                last.then_inc(c_hg, 1)
                pe.wait_ge(c_hgs, 1)
                for c in range(CH):
                    f = slice(c * P, (c + 1) * P)
                    last = three(PTG[:, c * G:(c + 1) * G], WH[1][:, f], WL[1][:, f], HGH[:, 0, :], HGL[:, 0, :], True, True)
                last.then_inc(c_kg, 1)
                hgh, hgl = (t[:].rearrange("p a g -> p (a g)") for t in (HGH, HGL))
                for half, bank in enumerate((PT, OB)):
                    f = slice(half * 512, (half + 1) * 512)
                    last = three(bank[:], hgh, hgl, WH[2][:, f], WL[2][:, f], True, True)
                last.then_inc(c_vg, 1)
                pe.wait_ge(ld_small, 16 * 8)
                tr(MISC[:, 448:448 + E * FC], b1r[:], ident[0:E * FC, 0:E * FC]).then_inc(c_b1, 1)
                pe.wait_ge(c_kgp, 1)
                pe.wait_ge(c_vgl, 1)
                pe.wait_ge(c_wl, 4)

                def scores(w, j):
                    first = isinstance(w, int) and w == 0
                    if j == 0:
                        pe.wait_ge(k_padded, w * 2 + 1)
                        pe.wait_ge(unit_lo, 5 if first else (w * 8 + (3 - 8 + UNIT["k0"] + 1) if not isinstance(w, int)
                                                             else unit_no("k0", w - 1) + 1))
                    if j == 2:
                        pe.wait_ge(k_padded, w * 2 + 2)
                        pe.wait_ge(unit_lo, 5 if first else (w * 8 + (3 - 8 + UNIT["q1"] + 1)))
                    if not (first and j == 0):
                        pe.wait_ge(scores_read, w * 4 + j)
                    for a in range(2):
                        c = 2 * j + a
                        three(SB_[a][:, 0:2 * K1], QH[:, c, :], QL[:, c, :], KPH[:, c].rearrange("p a k -> p (a k)"),
                              KPL[:, c].rearrange("p a k -> p (a k)"), True, True).then_inc(scores_done, 1)

                def turn_probs(w, j):
                    pe.wait_ge(exp_done, w * 4 + (j + 1))
                    if not (isinstance(w, int) and w == 0 and j == 0):
                        pe.wait_ge(pt_lo, w * 4 + j)
                    for i in range(GRP):
                        last = tr(PT[:, i * P:(i + 1) * P], PR[:, i, 0:P], ident[:])
                    last.then_inc(pt_done, 1)
                    pe.wait_ge(pg_ready, w * 4 + (j + 1))
                    if not (isinstance(w, int) and w == 0 and j == 0):
                        pe.wait_ge(ptg_lo, w * 4 + j)
                    tr(PTG[:, 0:P], PG[:].rearrange("p h g -> p (h g)"), ident[:]).then_inc(ptg_done, 1)

                def values(w, j):
                    if not (isinstance(w, int) and w == 0 and j == 0):
                        pe.wait_ge(o_ready, w * 4 + j)
                    if j == 2:
                        pe.wait_ge(unit_lo, unit_no("v1", w) + 1)
                    if j == 0 and not (isinstance(w, int) and w == 0):
                        pe.wait_ge(unit_lo, w * 8 + (3 - 8 + UNIT["v0"] + 1))
                    pe.wait_ge(ptg_lo, w * 4 + (j + 1))
                    pe.wait_ge(pt_lo, w * 4 + (j + 1))
                    three(OB[:, 0:GRP * HD], PGH[:], PGL[:], VGH[:, j, :], VGL[:, j, :], True, False)
                    for i in range(GRP):
                        f = slice((GRP * j + i) * HD, (GRP * j + i + 1) * HD)
                        last = three(OB[:, i * HD:(i + 1) * HD], PTH[:, i, :], PTL[:, i, :], VH[:, f], VL[:, f],
                                     False, i == GRP - 1)
                    last.then_inc(pv_done, 1)

                def turn_o(w, name):
                    n = unit_no(name, w)
                    pe.wait_ge(unit_lo, n - 1)
                    half = int(name[-1])
                    for c in range(4):
                        f = slice((half * 4 + c) * P, (half * 4 + c + 1) * P)
                        last = tr(unit_bank(name, w)[:, c * P:(c + 1) * P], OS[:, f], ident[:])
                    last.then_inc(unit_done, 1)

                def project(w):
                    pe.wait_ge(unit_lo, unit_no("oT1", w) + 1)
                    pe.wait_ge(y_read, w)
                    for c in range(CH):
                        f = slice(c * D, (c + 1) * D)
                        last = three(MISC[:, 0:D], OTH[:, c, :], OTL[:, c, :], WH[3][:, f], WL[3][:, f], c == 0, c == CH - 1)
                    last.then_inc(y_done, 1)

                def body(w, first=False, last=False):
                    before, after = steps(w)
                    for j in range(NG):
                        n = nxt(w, j)
                        if n:
                            scores(*n)
                        for name in before[j]:
                            weight_unit(name, w if name == "v1" else w + 1, unit_bank(name, w), unit_no(name, w))
                        turn_probs(w, j)
                        if after[j]:
                            pe.wait_ge(o_ready, w * 4)
                        for name in after[j]:
                            turn_o(w, name)
                        if j == 1 and not first:
                            project(w)
                        values(w, j)

                scores(0, 0)
                body(0, first=True)
                with pe.Fori(1, NW - 1) as w:
                    body(w)
                body(NW - 1, last=True)
                pe.wait_ge(o_ready, NW * 4)
                turn_o(NW, "oT0")
                turn_o(NW, "oT1")
                project(NW)

                pe.wait_ge(t_ready, NW)
                for i in range(4):
                    for k in range(4):
                        last = tr(ps[i][:, k * P:(k + 1) * P], T[:, 4 * i + k, :], ident[:])
                    last.then_inc(tt_done, 1)
                pe.wait_ge(y_read, NW + 1)
                for w in range(NW):
                    if w % 4 == 0:
                        pe.wait_ge(tt_sb, w // 4 + 1)
                    last = mm(MISC[:, w * E:(w + 1) * E], TT[:, w * P:(w + 1) * P], gw_sb[:], start=True, stop=True)
                last.then_inc(lg_done, 1)
                pe.wait_ge(m_ready, 1)
                me = MISC[:, 128:128 + NW * E]
                mm(me, upper[:], M16[:].rearrange("p w e -> p (w e)"), start=True, stop=False)
                mm(me, ones[:], MX16[:].rearrange("p w e -> p (w e)"), start=False, stop=True).then_inc(mcum, 1)
                pe.wait_ge(tt_sb, 4)
                for w in range(NW):
                    pe.wait_ge(sec_ready, w + 1)
                    pe.wait_ge(tl_ready, w // 4 + 1)
                    for src in (TH, TL):
                        a, b = (w == 0 and src is TH), (w == NW - 1 and src is TL)
                        mm(ps[0][:], src[:, w, :], SEC[:, w, 0:512], start=a, stop=b)
                        last = mm(ps[1][:, 0:SLOTS - 512], src[:, w, :], SEC[:, w, 512:SLOTS], start=a, stop=b)
                last.then_inc(disp_done, 1)

                pe.wait_ge(dt_lo, 2)

                def down(e):
                    pe.wait_ge(h_act, e + 1)
                    if e >= 2:
                        pe.wait_ge(eo_sb, e - 1)
                    for c in range(FC):
                        last = mm(ps[6 + e % 2][0:CAP, 0:D], HS[:, e, c, :], w2_sb[:, e, c, :], start=(c == 0), stop=(c == FC - 1))
                    last.then_inc(e_done, 1)

                for e in range(E):
                    pe.wait_ge(w1_lo, e // 2 + 1)
                    if e >= 4:
                        pe.wait_ge(h_sum, e - 3)
                    s = slice(e * CAP, (e + 1) * CAP)
                    for c in range(FC):
                        f = slice(c * P, (c + 1) * P)
                        last = three(ps[2 + e % 4][:, c * CAP:(c + 1) * CAP], W1H[:, e, f], W1L[:, e, f],
                                     DTH[:, s], DTL[:, s], True, True)
                    last.then_inc(h_done, 1)
                    if e >= 2:
                        down(e - 2)
                down(E - 2)
                down(E - 1)


_INS = ['L0_attn_x', 'L0_attn_norm_w', 'L0_attn_w_q', 'L0_attn_w_k', 'L0_attn_w_v', 'L0_attn_w_out',
        'L0_attn_scorer_w', 'L0_attn_scorer_b', 'L0_ffn_gate_w', 'L0_ffn_gate_b', 'L0_ffn_w1', 'L0_ffn_b1',
        'L0_ffn_w2', 'L0_ffn_b2']


def kernel(**inputs):
    import numpy as _np
    import concourse.bacc as _bacc
    from concourse import mybir as _mybir
    from concourse.bass_utils import run_bass_kernel_spmd as _run

    nc = _bacc.Bacc("TRN2", target_bir_lowering=False, num_devices=1)
    arrays, args = {}, []
    for name in _INS:
        a = _np.ascontiguousarray(inputs[name])
        arrays[f"in_{name}"] = a
        args.append(nc.dram_tensor(f"in_{name}", a.shape, _mybir.dt.from_np(a.dtype), kind="ExternalInput").ap())
    shape = inputs['L0_attn_x'].shape
    args.append(nc.dram_tensor("out_0", shape, _mybir.dt.float32, kind="ExternalOutput").ap())
    build(nc, *args)
    r = _run(nc, [arrays], core_ids=[0])
    return r.results[0]["out_0"]
```

```python
from contextlib import ExitStack

import concourse.bass as bass
from concourse import mybir


def build(nc, x, norm_w, w_q, w_k, w_v, w_out, scorer_w, scorer_b, gate_w, gate_b, w1, b1, w2, b2, out):
    f32, f16, u32 = mybir.dt.float32, mybir.dt.float16, mybir.dt.uint32
    ALU, ACT, AX = mybir.AluOpType, mybir.ActivationFunctionType, mybir.AxisListType
    RED = bass.bass_isa.ReduceOp

    P = 128
    S, D = x.shape[1], x.shape[2]
    INNER = w_q.shape[1]
    HD = 64
    H = INNER // HD
    NW = S // P
    G = 32
    K1 = P + G
    CH = INNER // P
    GRP = 4
    NG = H // GRP
    E, F = w1.shape[0], w1.shape[2]
    CAP = 80
    SLOTS = E * CAP
    FC = F // P
    NEG = -2e38
    RMS_EPS, LN_EPS = 1e-6, 1e-5
    WS = 16.0
    EXPONENT = 0x7F800000

    ctx = ExitStack()
    with ctx:
        def sb(name, shape, dt=f32):
            return ctx.enter_context(nc.sbuf_tensor(name, shape, dt))

        def sem(name):
            return ctx.enter_context(nc.semaphore(name))

        X = sb("X", [P, NW, D])
        XN = sb("XN", [P, NW, D])
        GF = sb("GF", [P, NW, D])
        GH, GL = sb("GH", [P, NW, D], f16), sb("GL", [P, NW, D], f16)
        GTH, GTL = sb("GTH", [P, S], f16), sb("GTL", [P, S], f16)
        WB = sb("WB", [P, 5 * INNER])
        WF = [WB[:, i * INNER:(i + 1) * INNER] for i in range(4)]
        WPH, WPL = sb("WPH", [P, 4 * INNER], f16), sb("WPL", [P, 4 * INNER], f16)
        WH, WL = ([t[:, i * INNER:(i + 1) * INNER] for i in range(4)] for t in (WPH, WPL))
        nwcol, nwrow, swrow = sb("nwcol", [P, 1]), sb("nwrow", [P, D]), sb("swrow", [P, D])
        sbcol, nwabs = sb("sbcol", [P, 1]), sb("nwabs", [P, 1])
        gw_sb, gb_sb = sb("gw_sb", [P, E]), sb("gb_sb", [P, E])
        w1_sb, w2_sb = sb("w1_sb", [P, E, F]), sb("w2_sb", [P, E, FC, D])
        W1H, W1L = (t[:].rearrange("p (e f) -> p e f", f=F) for t in (WPH, WPL))
        b1r, b1c, b2b = sb("b1r", [E * FC, P]), sb("b1c", [P, E * FC]), sb("b2b", [P, E, D])

        ident = sb("ident", [P, P])
        upper = sb("upper", [P, P], f16)
        ones = sb("ones", [P, P], f16)
        mask = sb("mask", [P, K1])
        iota_g = sb("iota_g", [P, G])
        iota_s = sb("iota_s", [P, SLOTS], f16)
        ntok = sb("ntok", [P, NW])
        rev_e, base_e = sb("rev_e", [P, E]), sb("base_e", [P, E])
        mhalf = sb("mhalf", [P, NW])
        half_of = sb("half_of", [P, 2])
        zero_row = sb("zero_row", [1, D])
        epscol = sb("epscol", [P, 1])
        idle_p, idle_q, idle_v, idle_w = (sb(n, [P, 1]) for n in ("idle_p", "idle_q", "idle_v", "idle_w"))

        st6 = sb("st6", [P, NW, 6])
        mv = sb("mv", [P, NW, 2])
        vtmp, rstd, rms = sb("vtmp", [P, NW]), sb("rstd", [P, NW]), sb("rms", [P, NW])
        wmax = sb("wmax", [P, 5])
        wred, wpow, winv, wsc = (sb(n, [P, 5]) for n in ("wred", "wpow", "winv", "wsc"))
        cexp, cneg, cy, ch = (sb(n, [P, 1]) for n in ("cexp", "cneg", "cy", "ch"))

        scol = sb("scol", [P, NW])
        srow, t16 = sb("srow", [NW, P]), sb("t16", [NW, G])
        tmax = sb("tmax", [P, 8])
        gteq = sb("gteq", [P, NW, 2])
        gteq16, gtex16 = sb("gteq16", [P, NW, 2], f16), sb("gtex16", [P, NW, 2], f16)
        PAD = 64
        pfa, pfb = sb("pfa", [P, PAD + NW * E]), sb("pfb", [P, PAD + NW * E])
        tot16, ngt, need = sb("tot16", [P, 1], f16), sb("ngt", [P, 1]), sb("need", [P, 1])
        keq, kslot, gslot = (sb(n, [P, NW]) for n in ("keq", "kslot", "gslot"))
        OH = sb("OH", [P, NW, G], f16)
        gi_s, gi_c = sb("gi_s", [P, G], f16), sb("gi_c", [P, G])
        GM = sb("GM", [P, NW, G])
        HGH, HGL = sb("HGH", [P, 4, G], f16), sb("HGL", [P, 4, G], f16)

        QH, QL = sb("QH", [P, CH, P], f16), sb("QL", [P, CH, P], f16)
        KNH, KNL = sb("KNH", [P, CH, P], f16), sb("KNL", [P, CH, P], f16)
        KGH, KGL = sb("KGH", [P, CH, G], f16), sb("KGL", [P, CH, G], f16)
        KPH, KPL = sb("KPH", [P, CH, 2, K1], f16), sb("KPL", [P, CH, 2, K1], f16)
        VF = sb("VF", [P, INNER])
        VH, VL = sb("VH", [P, INNER], f16), sb("VL", [P, INNER], f16)
        VGH, VGL = sb("VGH", [P, NG, GRP * HD], f16), sb("VGL", [P, NG, GRP * HD], f16)
        SM, PR = sb("SM", [P, 2, GRP, K1]), sb("PR", [P, 2, GRP, K1])
        SM_flat = SM[:].rearrange("p a h k -> p (a h k)")
        tall = SM_flat[:, 0:NW * G]
        OHN = SM_flat[:, NW * G:2 * NW * G].rearrange("p (w g) -> p w g", g=G)
        mn, ssum, rinv = (sb(n, [P, 2, GRP]) for n in ("mn", "ssum", "rinv"))
        PG = sb("PG", [P, GRP, G])
        PTH, PTL = sb("PTH", [P, 2, GRP, P], f16), sb("PTL", [P, 2, GRP, P], f16)
        PGH, PGL = sb("PGH", [P, 2, P], f16), sb("PGL", [P, 2, P], f16)
        OS = sb("OS", [P, INNER])
        OTH, OTL = sb("OTH", [P, CH, P], f16), sb("OTL", [P, CH, P], f16)
        R = sb("R", [P, D])
        ra = sb("ra", [P, D])
        X1 = sb("X1", [P, NW, D])
        s1, m1, v1, r1 = sb("s1", [P, 6]), sb("m1", [P, 2]), sb("v1", [P, 1]), sb("r1", [P, 1])
        s2, m2, v2, r2 = sb("s2", [P, 6]), sb("m2", [P, 2]), sb("v2", [P, 1]), sb("r2", [P, 1])

        T, TH, TL = GF, GH, GL
        TT = X[:].rearrange("p w d -> p (w d)")
        L, L2, Lm = sb("L", [P, NW, E]), sb("L2", [P, NW, E]), sb("Lm", [P, NW, E])
        lmax, rv, esum, gp = (sb(n, [P, NW]) for n in ("lmax", "rv", "esum", "gp"))
        M16, MX16 = sb("M16", [P, NW, E], f16), sb("MX16", [P, NW, E], f16)
        pos, ebase, kept, slot1, slotv, gix = (sb(n, [P, NW]) for n in ("pos", "ebase", "kept", "slot1", "slotv", "gix"))
        gidx = sb("gidx", [P, NW], u32)
        SEC = WB[:].bitcast(f16).rearrange("p (w s) -> p w s", s=SLOTS)
        DTH, DTL = sb("DTH", [P, SLOTS], f16), sb("DTL", [P, SLOTS], f16)
        HA = SM_flat[:, 0:2 * FC * CAP].rearrange("p (a s) -> p a s", a=2)
        HS = sb("HS", [P, E, FC, CAP])
        EO = OS[0:CAP, :].rearrange("p (e d) -> p e d", d=D)
        Y = X
        OUT = XN

        ps = [ctx.enter_context(nc.psum_tensor(f"ps{i}", [P, 512], f32)) for i in range(8)]
        SB_, PJ = [ps[0], ps[1]], [ps[2], ps[3]]
        PTG, OB, MISC = ps[5], ps[6], ps[7]
        PT, PTB = ps[4], [ps[4], ps[7]]
        YB = OB[:, GRP * HD:GRP * HD + D]

        top_dram = nc.dram_tensor("top_scratch", [NW, G], f32, kind="Internal").ap()
        eo_dram = nc.dram_tensor("expert_scratch", [SLOTS + 1, D], f32, kind="Internal").ap()

        ld_x = [sem(f"ld_x{i}") for i in range(4)]
        (ld_small, ld_w, ld_moe, top_out, top_in, zrow_out, eo_out, gathered, s_out) = map(
            sem, ("ld_small", "ld_w", "ld_moe", "top_out", "top_in", "zrow_out", "eo_out", "gathered", "s_out"))
        (c_pool, c_wmax, c_wred, c_wsc, c_wh, c_wl, c_stat, c_rstd, c_g, c_gh, c_gl, c_gt, c_gth, c_gtl) = map(
            sem, ("c_pool", "c_wmax", "c_wred", "c_wsc", "c_wh", "c_wl", "c_stat", "c_rstd", "c_g", "c_gh", "c_gl",
                  "c_gt", "c_gth", "c_gtl"))
        dve_chain, pool_chain, act_chain = sem("dve_chain"), sem("pool_chain"), sem("act_chain")
        (c_scol, c_srow, c_t16, c_sel, c_cum, c_ngt, c_tot, c_oh, c_hg, c_hgs, c_gi, c_gir, c_kg, c_kgs, c_kgp,
         c_vg, c_vgh, c_vgl, c_b1) = map(
            sem, ("c_scol", "c_srow", "c_t16", "c_sel", "c_cum", "c_ngt", "c_tot", "c_oh", "c_hg", "c_hgs", "c_gi",
                  "c_gir", "c_kg", "c_kgs", "c_kgp", "c_vg", "c_vgh", "c_vgl", "c_b1"))
        (scores_done, scores_read, exp_done, rinv_ready, unit_done, unit_hi, unit_lo, k_padded,
         pt_done, pt_hi, pt_lo, ptg_done, ptg_hi, ptg_lo, pv_done, o_ready, y_done, y_read, var_ready, eps_added,
         ln_rstd, ln_step, mask_set, pg_ready, v_head, v_split, ra_ready, x1_ready) = map(
            sem, ("scores_done", "scores_read", "exp_done", "rinv_ready", "unit_done", "unit_hi",
                  "unit_lo", "k_padded", "pt_done", "pt_hi", "pt_lo", "ptg_done", "ptg_hi", "ptg_lo", "pv_done",
                  "o_ready", "y_done", "y_read", "var_ready", "eps_added", "ln_rstd", "ln_step", "mask_set", "pg_ready",
                  "v_head", "v_split", "ra_ready", "x1_ready"))
        (t_ready, tl_ready, th_ready, tt_done, tt_sb, lg_done, m_ready, lm_ready, le_ready, mcum, sec_ready,
         disp_done, dt_hi, dt_lo, h_done, h_act, h_sum, e_done, eo_sb, idx_ready, w1_hi, w1_lo, fin_var, fin_rstd,
         fin_mul, fin_add) = map(
            sem, ("t_ready", "tl_ready", "th_ready", "tt_done", "tt_sb", "lg_done", "m_ready", "lm_ready",
                  "le_ready", "mcum", "sec_ready", "disp_done", "dt_hi", "dt_lo", "h_done", "h_act", "h_sum", "e_done",
                  "eo_sb", "idx_ready", "w1_hi", "w1_lo", "fin_var", "fin_rstd", "fin_mul", "fin_add"))

        x_v = x[0].rearrange("(w p) d -> p w d", p=P)
        out_v = out[0].rearrange("(w p) d -> p w d", p=P)
        XL = 4

        FIRST = ["k0", "q0", "k1", "q1", "v0"]
        STEP = [["k0", "q0"], ["v1", "oT1"], ["k1", "q1"], ["v0", "oT0"]]

        def units(w, j):
            if not isinstance(w, int):
                return STEP[j]
            if w == NW:
                return ["oT1"] if j == 0 else []
            none = ["oT1"] if w == 0 else ["k0", "q0", "k1", "q1", "v0"] if w == NW - 1 else []
            return [u for u in STEP[j] if u not in none]

        order = [(-1, u) for u in FIRST] + [(w, u) for w in range(NW + 1) for j in range(NG) for u in units(w, j)]
        order_lo = [x for x in order if x[1][0] != "v"]

        def place(seq, name, w):
            if isinstance(w, int):
                return seq.index((w, name))
            per = seq.index((2, name)) - seq.index((1, name))
            assert all(seq.index((i, name)) == seq.index((1, name)) + per * (i - 1) for i in range(1, NW - 1))
            return w * per + (seq.index((1, name)) - per)

        def unit_no(name, w):
            return place(order, name, w)

        def unit_bank(name, w):
            return PJ[order.index((w if isinstance(w, int) else 2, name)) % 2]

        def wait_split(eng, name, w):
            if name[0] == "v":
                eng.wait_ge(unit_hi, place(order, name, w) + 1)
            else:
                eng.wait_ge(unit_lo, place(order_lo, name, w) + 1)

        def wait_bank(eng, name, w):
            static = isinstance(w, int)
            w2, name2 = order[order.index((w if static else 2, name)) - 2]
            wait_split(eng, name2, w2 if static else w if w2 == 2 else w - 1)

        def later(w, j, k):
            w, j = (w, j + k) if j + k < NG else (w + 1, j + k - NG)
            return None if isinstance(w, int) and w == NW else (w, j)

        def at_start(w, j):
            return isinstance(w, int) and w == 0 and j < 2

        with nc.Block() as block:

            @block.sync
            def _(sp):
                for i in range(NW // XL):
                    sp.dma_start(X[:, i * XL:(i + 1) * XL, :], x_v[:, i * XL:(i + 1) * XL, :]).then_inc(ld_x[i], 16)
                for i, w in enumerate((w_q, w_k, w_v)):
                    sp.dma_start(WF[i], w).then_inc(ld_w, 16)
                sp.dma_start(WF[3].rearrange("p (c d) -> p c d", d=D),
                             w_out.rearrange("(c p) d -> p c d", p=P)).then_inc(ld_w, 16)
                sp.dma_start(w1_sb[:], w1.rearrange("e d f -> d e f")).then_inc(ld_moe, 16)
                sp.dma_start(w2_sb[:], w2.rearrange("e (c p) d -> p e c d", p=P)).then_inc(ld_moe, 16)
                sp.wait_ge(c_t16, 1)
                sp.dma_start(top_dram, t16[:]).then_inc(top_out, 16)
                sp.wait_ge(top_out, 16)
                sp.dma_start(tall[:], top_dram.rearrange("(a w) g -> a (w g)", a=1).partition_broadcast(P)
                             .rearrange("p a n -> p (a n)")).then_inc(top_in, 16)
                for i in range(2):
                    sp.wait_ge(eo_sb, (i + 1) * E // 2)
                    e0, e1 = i * E // 2, (i + 1) * E // 2
                    sp.dma_start(eo_dram[e0 * CAP:e1 * CAP, :].rearrange("(e s) d -> s e d", s=CAP),
                                 EO[:, e0:e1, :]).then_inc(eo_out, 16)
                for i in range(NW // XL):
                    sp.wait_ge(fin_add, i + 1)
                    sp.dma_start(out_v[:, i * XL:(i + 1) * XL, :], OUT[:, i * XL:(i + 1) * XL, :]).then_inc(s_out, 16)
                sp.wait_ge(s_out, 16 * (NW // XL))

            @block.gpsimd
            def _(pool):
                g = nc.gpsimd
                g.memset(mhalf[:], -0.5)
                g.memset(ident[:], 0.0)
                g.memset(upper[:], 1.0)
                g.memset(ones[:], 1.0)
                g.memset(mask[:, 0:P], 0.0)
                g.memset(zero_row[:], 0.0)
                g.memset(epscol[:], LN_EPS)
                g.memset(VGH[:], 0.0)
                g.memset(VGL[:], 0.0)
                g.memset(half_of[:], 1.0)
                g.memset(pfa[:], 0.0)
                g.memset(pfb[:], 0.0)
                g.iota(iota_g[:], pattern=[[1, G]], base=1, channel_multiplier=0, allow_small_or_imprecise_dtypes=True)
                g.iota(iota_s[:], pattern=[[1, SLOTS]], base=0, channel_multiplier=0,
                       allow_small_or_imprecise_dtypes=True)
                g.iota(ntok[:], pattern=[[P, NW]], base=0, channel_multiplier=1, allow_small_or_imprecise_dtypes=True)
                g.iota(rev_e[:], pattern=[[-1, E]], base=E, channel_multiplier=0, allow_small_or_imprecise_dtypes=True)
                g.iota(base_e[:], pattern=[[CAP, E]], base=0, channel_multiplier=0,
                       allow_small_or_imprecise_dtypes=True).then_inc(pool_chain, 1)
                pool.wait_ge(pool_chain, 1)
                g.affine_select(out=ident[:], in_=ident[:], compare_op=ALU.not_equal, fill=1.0, base=0,
                                pattern=[[-1, P]], channel_multiplier=1)
                g.affine_select(out=upper[:], in_=upper[:], compare_op=ALU.is_ge, fill=0.0, base=0,
                                pattern=[[1, P]], channel_multiplier=-1)
                g.affine_select(out=mask[:, 0:P], in_=mask[:, 0:P], compare_op=ALU.is_ge, fill=NEG, base=0,
                                pattern=[[-1, P]], channel_multiplier=1)
                g.affine_select(out=half_of[:, 0:1], in_=half_of[:, 0:1], compare_op=ALU.is_ge, fill=0.0, base=HD - 1,
                                pattern=[[0, 1]], channel_multiplier=-1)
                g.affine_select(out=half_of[:, 1:2], in_=half_of[:, 1:2], compare_op=ALU.is_ge, fill=0.0, base=-HD,
                                pattern=[[0, 1]], channel_multiplier=1).then_inc(c_pool, 1)
                g.dma_start(eo_dram[SLOTS:SLOTS + 1, :], zero_row[:]).then_inc(zrow_out, 16)

                for i in range(2):
                    pool.wait_ge(c_stat, i + 1)
                    dst = (rstd, rms)[i]
                    g.tensor_tensor(dst[:], vtmp[:], mhalf[:], ALU.pow).then_inc(c_rstd, 1)
                pool.wait_ge(c_wmax, 1)
                g.partition_all_reduce(wred[:], wmax[:], P, RED.max).then_inc(c_wred, 1)

                pool.wait_ge(c_kgs, 1)
                for src, dst in ((KGH, KPH), (KGL, KPL)):
                    for a in range(2):
                        last = g.tensor_scalar(dst[:, :, a, P:K1], src[:], half_of[:, a:a + 1], 1.0, ALU.mult, ALU.mult)
                last.then_inc(c_kgp, 1)

                def pad_keys(half, part):
                    c = slice(half * CH // 2, (half + 1) * CH // 2)
                    src, dst = ((KNH, KPH), (KNL, KPL))[part]
                    for a in range(2):
                        last = g.tensor_scalar(dst[:, c, a, 0:P], src[:, c, :], half_of[:, a:a + 1], 1.0, ALU.mult, ALU.mult)
                    if part == 1:
                        last.then_inc(k_padded, 1)

                def keys_ready(half, hi_count, lo_count, scores_count, pads_before):
                    pool.wait_ge(unit_hi, hi_count)
                    pool.wait_ge(unit_lo, lo_count)
                    if scores_count is not None:
                        pool.wait_ge(scores_done, scores_count)
                    if pads_before is not None:
                        pool.wait_ge(k_padded, pads_before)
                    g.tensor_tensor(idle_p[:], mhalf[:, 0:1], mhalf[:, 0:1], ALU.add)

                def ln_pow(n, var, vt, r):
                    pool.wait_ge(var_ready, n)
                    g.tensor_tensor(vt[:], var[:, 1:2], epscol[:], ALU.add).then_inc(eps_added, 1)
                    pool.wait_ge(eps_added, n)
                    g.tensor_tensor(r[:], vt[:], mhalf[:, 0:1], ALU.pow).then_inc(ln_rstd, 1)

                def split_v(half, unit, readers, splits_before):
                    v_s = slice(half * 512, (half + 1) * 512)
                    pool.wait_ge(unit_hi, unit + 1)
                    if readers is not None:
                        pool.wait_ge(pv_done, readers)
                        pool.wait_ge(v_split, splits_before)
                    g.tensor_tensor(idle_q[:], mhalf[:, 0:1], mhalf[:, 0:1], ALU.add)
                    g.tensor_scalar(VH[:, v_s], VF[:, v_s], 1.0, None, ALU.mult).then_inc(v_head, 1)
                    pool.wait_ge(v_head, splits_before + 1)
                    g.tensor_tensor(VL[:, v_s], VF[:, v_s], VH[:, v_s], ALU.subtract).then_inc(v_split, 1)

                def body(w, first=False, last=False):
                    if not last:
                        keys_ready(0, unit_no("k0", w) + 1, place(order_lo, "k0", w) + 1, w * 8 + 4, w * 2 + 2)
                        pad_keys(0, 0)
                        pad_keys(0, 1)
                    split_v(1, unit_no("v1", w), None if first else w * 4, w * 2 + 1)
                    if not last:
                        keys_ready(1, unit_no("k1", w) + 1, place(order_lo, "k1", w) + 1, w * 8 + 8, w * 2 + 3)
                    if not first:
                        ln_pow(w * 2 - 1, m1, v1, r1)
                    if not last:
                        pad_keys(1, 0)
                    if not first:
                        add_x(w)
                    if not last:
                        pad_keys(1, 1)
                    if not first:
                        ln_pow(w * 2, m2, v2, r2)
                    if not last:
                        split_v(0, unit_no("v0", w), w * 4 + 2, w * 2 + 2)

                def add_x(w):
                    pool.wait_ge(ra_ready, w)
                    g.tensor_tensor(X1[:, w - 1, :], ra[:], X[:, w - 1, :], ALU.add).then_inc(x1_ready, 1)

                for half in range(2):
                    keys_ready(half, 2 * half + 1, 2 * half + 1, None, half or None)
                    pad_keys(half, 0)
                    pad_keys(half, 1)
                split_v(0, 4, None, 0)
                body(0, first=True)
                with pool.Fori(1, NW - 1) as w:
                    body(w)
                body(NW - 1, last=True)
                ln_pow(2 * NW - 1, m1, v1, r1)
                add_x(NW)
                ln_pow(2 * NW, m2, v2, r2)

                for i in range(4):
                    q = slice(i * NW // 4, (i + 1) * NW // 4)
                    pool.wait_ge(t_ready, NW)
                    pool.wait_ge(th_ready, i + 1)
                    g.tensor_tensor(TL[:, q, :], T[:, q, :], TH[:, q, :], ALU.subtract).then_inc(tl_ready, 1)

                pool.wait_ge(idx_ready, 1)
                pool.wait_ge(eo_out, 32)
                pool.wait_ge(zrow_out, 16)
                for w in range(NW):
                    g.indirect_dma_start(out=Y[:, w, :], out_offset=None, in_=eo_dram,
                                         in_offset=bass.IndirectOffsetOnAxis(ap=gidx[:, w:w + 1], axis=0)
                                         ).then_inc(gathered, 16)
                for i in range(NW // XL):
                    c = slice(i * XL, (i + 1) * XL)
                    pool.wait_ge(fin_var, i + 1)
                    g.tensor_tensor(rstd[:, c], vtmp[:, c], mhalf[:, c], ALU.pow).then_inc(fin_rstd, 1)

            @block.scalar
            def _(act):
                a_ = nc.scalar
                act.dma_start(nwcol[:], norm_w.rearrange("(p a) -> p a", a=1)).then_inc(ld_small, 16)
                act.dma_start(nwrow[:], norm_w.rearrange("(a d) -> a d", a=1).partition_broadcast(P)
                              .rearrange("p a d -> p (a d)")).then_inc(ld_small, 16)
                act.dma_start(swrow[:], scorer_w.rearrange("d a -> a d").partition_broadcast(P)
                              .rearrange("p a d -> p (a d)")).then_inc(ld_small, 16)
                act.dma_start(sbcol[:], scorer_b.rearrange("(a d) -> a d", a=1).partition_broadcast(P)
                              .rearrange("p a d -> p (a d)")).then_inc(ld_small, 16)
                act.dma_start(gw_sb[:], gate_w).then_inc(ld_small, 16)
                act.dma_start(gb_sb[:], gate_b.rearrange("(a d) -> a d", a=1).partition_broadcast(P)
                              .rearrange("p a d -> p (a d)")).then_inc(ld_small, 16)
                act.dma_start(b1r[:], b1.rearrange("e (c p) -> (e c) p", p=P)).then_inc(ld_small, 16)
                act.dma_start(b2b[:], b2.rearrange("(a e) d -> a (e d)", a=1).partition_broadcast(P)
                              .rearrange("p a (e d) -> p (a e) d", e=E)).then_inc(ld_small, 16)

                act.wait_ge(c_g, 1)
                a_.activation(GH[:], GF[:], ACT.Copy).then_inc(c_gh, 1)
                for i in range(4):
                    act.wait_ge(c_gt, i + 1)
                    a_.activation(GTH[:, i * 512:(i + 1) * 512], PJ[i % 2][:], ACT.Copy).then_inc(c_gth, 1)
                act.wait_ge(c_wsc, 1)
                for i in range(4):
                    a_.activation(WH[i], WF[i], ACT.Copy, scale=wsc[:, i:i + 1]).then_inc(c_wh, 1)

                def head_of(unit, dst, bank):
                    act.wait_ge(unit_done, unit + 1)
                    a_.activation(dst, bank[:], ACT.Copy).then_inc(unit_hi, 1)

                def dest(name):
                    half = int(name[-1])
                    if name[0] == "v":
                        return VF[:, half * 512:(half + 1) * 512]
                    t = {"q": QH, "k": KNH, "o": OTH}[name[0]]
                    return t[:, half * 4:(half + 1) * 4, :].rearrange("p c n -> p (c n)")

                for i, name in enumerate(FIRST):
                    head_of(i, dest(name), PJ[i % 2])

                act.wait_ge(c_vg, 1)
                for half in range(2):
                    for i in range(GRP):
                        src = PT if half == 0 else OB
                        last = a_.activation(
                            VGH[i * G:(i + 1) * G, half * 2:half * 2 + 2, i * HD:(i + 1) * HD],
                            src[i * G:(i + 1) * G, :].rearrange("p (j i d) -> p j i d", j=2, i=GRP)[:, :, i, :], ACT.Copy)
                last.then_inc(c_vgh, 1)

                def exps(w, j):
                    act.wait_ge(scores_read, w * 4 + (j + 1))
                    if not at_start(w, j):
                        act.wait_ge(rinv_ready, w * 4 + (j - 1))
                        act.wait_ge(pg_ready, w * 4 + (j - 1))
                        act.wait_ge(pt_done, w * 4 + (j - 1))
                    p = j % 2
                    for i in range(GRP):
                        last = a_.activation(PR[:, p, i, :], SM[:, p, i, :], ACT.Exp, bias=mn[:, p, i:i + 1], scale=-1.0,
                                             accum_out=ssum[:, p, i:i + 1])
                    last.then_inc(exp_done, 1)

                def body(w, first=False):
                    for j in range(NG):
                        n = later(w, j, 1)
                        if n:
                            exps(*n)
                        p = j % 2
                        if not at_start(w, j):
                            act.wait_ge(pv_done, w * 4 + (j - 1))
                        act.wait_ge(pt_done, w * 4 + (j + 1))
                        a_.activation(PTH[:, p].rearrange("p h n -> p (h n)"), PTB[p][:], ACT.Copy).then_inc(pt_hi, 1)
                        act.wait_ge(ptg_done, w * 4 + (j + 1))
                        a_.activation(PGH[:, p], PTG[:, 0:P], ACT.Copy).then_inc(ptg_hi, 1)
                        for name in units(w, j):
                            if name == "v1" and not first:
                                act.wait_ge(v_split, w * 2)
                            if name == "v0":
                                act.wait_ge(v_split, w * 2 + 1)
                            if name in ("q0", "k0"):
                                act.wait_ge(scores_done, w * 8 + 4)
                                act.wait_ge(k_padded, w * 2 + 1)
                            if name in ("q1", "k1"):
                                act.wait_ge(scores_done, w * 8 + 8)
                                act.wait_ge(k_padded, w * 2 + 2)
                            head_of(unit_no(name, w), dest(name), unit_bank(name, w))

                exps(0, 0)
                body(0, first=True)
                with act.Fori(1, NW - 1) as w:
                    body(w)
                body(NW - 1)
                head_of(unit_no("oT1", NW), dest("oT1"), unit_bank("oT1", NW))

                act.wait_ge(t_ready, NW)
                for i in range(4):
                    q = slice(i * NW // 4, (i + 1) * NW // 4)
                    a_.activation(TH[:, q, :], T[:, q, :], ACT.Copy).then_inc(th_ready, 1)
                for i in range(4):
                    act.wait_ge(tt_done, i + 1)
                    a_.activation(TT[:, i * 512:(i + 1) * 512], ps[i][:], ACT.Copy).then_inc(tt_sb, 1)
                for i in range(4):
                    a_.activation(W1H[:, 2 * i:2 * i + 2, :], w1_sb[:, 2 * i:2 * i + 2, :], ACT.Copy,
                                  scale=wsc[:, 4:5]).then_inc(w1_hi, 1)
                act.wait_ge(lm_ready, 1)
                a_.activation(L2[:], Lm[:], ACT.Exp).then_inc(le_ready, 1)
                act.wait_ge(disp_done, 1)
                a_.activation(DTH[:, 0:512], ps[0][:], ACT.Copy).then_inc(dt_hi, 1)
                a_.activation(DTH[:, 512:SLOTS], ps[1][:, 0:SLOTS - 512], ACT.Copy).then_inc(dt_hi, 1)
                for e in range(E):
                    act.wait_ge(h_sum, e + 1)
                    a_.activation(HS[:, e].rearrange("p c s -> p (c s)"), HA[:, e % 2, :], ACT.Gelu_apprx_tanh
                                  ).then_inc(h_act, 1)

            @block.vector
            def _(dve):
                v = nc.vector
                chain = [0]

                def link(ins):
                    chain[0] += 1
                    ins.then_inc(dve_chain, 1)
                    dve.wait_ge(dve_chain, chain[0])

                for w in range(NW):
                    if w % XL == 0:
                        dve.wait_ge(ld_x[w // XL], 16)
                    last = v.bn_stats(st6[:, w, :], X[:, w, :])
                link(last)
                for w in range(NW):
                    last = v.bn_aggr(mv[:, w, :], st6[:, w, :])
                link(last)
                v.tensor_scalar(vtmp[:], mv[:, :, 1], LN_EPS, None, ALU.add).then_inc(c_stat, 1)
                dve.wait_ge(c_rstd, 1)
                link(v.tensor_tensor(rms[:], rstd[:], rstd[:], ALU.mult))
                link(v.tensor_tensor(rms[:], rms[:], mv[:, :, 1], ALU.mult))
                v.tensor_scalar(vtmp[:], rms[:], RMS_EPS, None, ALU.add).then_inc(c_stat, 1)
                for w in range(NW):
                    last = v.tensor_scalar(XN[:, w, :], X[:, w, :], mv[:, w, 0:1], rstd[:, w:w + 1],
                                           ALU.subtract, ALU.mult)
                link(last)
                dve.wait_ge(c_rstd, 2)
                for w in range(NW):
                    last = v.tensor_scalar(GF[:, w, :], XN[:, w, :], rms[:, w:w + 1], None, ALU.mult)
                last.then_inc(c_g, 1)
                dve.wait_ge(c_g, 1)

                dve.wait_ge(ld_small, 16 * 8)
                link(v.tensor_tensor(nwrow[:], nwrow[:], swrow[:], ALU.mult))
                for w in range(NW):
                    last = v.tensor_tensor_reduce(out=X1[:, w, :], in0=GF[:, w, :], in1=nwrow[:], scale=1.0, scalar=0.0,
                                                  op0=ALU.mult, op1=ALU.add, accum_out=scol[:, w:w + 1])
                link(last)
                v.tensor_scalar(scol[:], scol[:], sbcol[:], None, ALU.add).then_inc(c_scol, 1)

                dve.wait_ge(ld_w, 64)
                dve.wait_ge(ld_moe, 32)
                for i in range(4):
                    v.tensor_reduce(wmax[:, i:i + 1], WF[i], AX.X, ALU.max, apply_absolute_value=True)
                link(v.tensor_reduce(wmax[:, 4:5], w1_sb[:], AX.XY, ALU.max, apply_absolute_value=True))
                link(v.tensor_reduce(nwabs[:], nwcol[:], AX.X, ALU.max, apply_absolute_value=True))
                v.tensor_scalar(wmax[:, 0:3], wmax[:, 0:3], nwabs[:], None, ALU.mult).then_inc(c_wmax, 1)

                dve.wait_ge(c_gh, 1)
                v.tensor_tensor(GL[:], GF[:], GH[:], ALU.subtract).then_inc(c_gl, 1)
                for i in range(4):
                    dve.wait_ge(c_gth, i + 1)
                    v.tensor_tensor(GTL[:, i * 512:(i + 1) * 512], PJ[i % 2][:], GTH[:, i * 512:(i + 1) * 512],
                                    ALU.subtract).then_inc(c_gtl, 1)

                dve.wait_ge(c_wred, 1)
                link(v.tensor_scalar(wred[:], wred[:], 1e-30, None, ALU.max))
                link(v.tensor_scalar(wpow[:].bitcast(u32), wred[:].bitcast(u32), EXPONENT, None, ALU.bitwise_and))
                link(v.reciprocal(winv[:], wpow[:]))
                link(v.tensor_scalar(wsc[:], winv[:], WS, None, ALU.mult))
                link(v.tensor_scalar(wsc[:, 0:3], wsc[:, 0:3], nwcol[:], None, ALU.mult))
                link(v.tensor_tensor(cexp[:], wpow[:, 0:1], wpow[:, 1:2], ALU.mult))
                v.tensor_scalar(cneg[:], cexp[:], -(HD ** -0.5) / WS ** 2, None, ALU.mult)
                link(v.tensor_tensor(cy[:], wpow[:, 2:3], wpow[:, 3:4], ALU.mult))
                v.tensor_scalar(cy[:], cy[:], 1 / WS ** 2, None, ALU.mult)
                v.tensor_scalar(ch[:], wpow[:, 4:5], 1 / WS, None, ALU.mult).then_inc(c_wsc, 1)
                for i in range(4):
                    dve.wait_ge(c_wh, i + 1)
                    v.scalar_tensor_tensor(WL[i], WF[i], wsc[:, i:i + 1], WH[i], ALU.mult, ALU.subtract
                                           ).then_inc(c_wl, 1)

                dve.wait_ge(c_srow, 1)
                link(v.tensor_copy(srow[:], MISC[0:NW, 0:P]))
                for r in range(G // 8):
                    link(v.max(t16[:, 8 * r:8 * r + 8], srow[:]))
                    if r < G // 8 - 1:
                        link(v.match_replace(srow[:], t16[:, 8 * r:8 * r + 8], srow[:], -3e38))
                dve.sem_inc(c_t16, 1)
                def rest_of(unit, dst, hi, bank):
                    dve.wait_ge(unit_hi, unit + 1)
                    v.tensor_tensor(dst, bank[:], hi, ALU.subtract).then_inc(unit_lo, 1)

                def parts(name):
                    half = int(name[-1])
                    return [t[:, half * 4:(half + 1) * 4, :].rearrange("p c n -> p (c n)") for t in
                            {"q": (QL, QH), "k": (KNL, KNH), "o": (OTL, OTH)}[name[0]]]

                for i, name in enumerate(FIRST):
                    if name[0] != "v":
                        rest_of(i, *parts(name), PJ[i % 2])
                dve.wait_ge(top_in, 16)
                for r in range(G // 8):
                    link(v.max(tmax[:], tall[:]))
                    if r < G // 8 - 1:
                        link(v.match_replace(tall[:], tmax[:], tall[:], -3e38))
                v.tensor_scalar(gteq[:, :, 0], scol[:], tmax[:, 7:8], None, ALU.is_gt)
                link(v.tensor_scalar(gteq[:, :, 1], scol[:], tmax[:, 7:8], None, ALU.is_equal))
                dve.wait_ge(c_pool, 1)

                def window_prefix(src, n):
                    a, b = pfa, pfb
                    link(v.tensor_copy(a[:, PAD:PAD + NW * n], src))
                    k = n
                    while k < NW * n:
                        link(v.tensor_tensor(b[:, PAD:PAD + NW * n], a[:, PAD:PAD + NW * n],
                                             a[:, PAD - k:PAD + NW * n - k], ALU.add))
                        a, b = b, a
                        k *= 2
                    return a

                pf = window_prefix(gteq[:].rearrange("p w e -> p (w e)"), 2)
                v.tensor_copy(gteq16[:], gteq[:])
                v.tensor_copy(tot16[:], pf[:, PAD + 2 * NW - 2:PAD + 2 * NW - 1])
                v.tensor_copy(gtex16[:].rearrange("p w e -> p (w e)"), pf[:, PAD - 2:PAD + 2 * NW - 2]).then_inc(c_sel, 1)
                dve.wait_ge(c_cum, 1)
                cum = MISC[:, 128:128 + 2 * NW].rearrange("p (w e) -> p w e", e=2)
                link(v.tensor_copy(ngt[:], MISC[:, 192:193]))
                link(v.tensor_scalar(need[:], ngt[:], -1.0, float(G), ALU.mult, ALU.add))
                link(v.tensor_scalar(keq[:], cum[:, :, 1], need[:], None, ALU.is_le))
                link(v.tensor_tensor(keq[:], keq[:], gteq[:, :, 1], ALU.mult))
                link(v.tensor_scalar(kslot[:], cum[:, :, 1], ngt[:], None, ALU.add))
                link(v.tensor_tensor(kslot[:], kslot[:], keq[:], ALU.mult))
                link(v.tensor_tensor(gslot[:], cum[:, :, 0], gteq[:, :, 0], ALU.mult))
                link(v.tensor_tensor(gslot[:], gslot[:], kslot[:], ALU.add))
                link(v.tensor_tensor(OH[:], gslot[:].unsqueeze(2).broadcast_to([P, NW, G]),
                                     iota_g[:].unsqueeze(1).broadcast_to([P, NW, G]), ALU.is_equal))
                dve.sem_inc(c_oh, 1)
                link(v.tensor_tensor(OHN[:], OH[:], ntok[:].unsqueeze(2).broadcast_to([P, NW, G]), ALU.mult))
                link(v.tensor_reduce(gi_c[:], OHN[:].rearrange("p w g -> p g w"), AX.X, ALU.add))
                v.tensor_copy(gi_s[:], gi_c[:]).then_inc(c_gi, 1)
                dve.wait_ge(c_gir, 1)
                link(v.tensor_copy(gi_c[:], MISC[:, 256:256 + G]))
                link(v.tensor_tensor(GM[:], gi_c[:].unsqueeze(1).broadcast_to([P, NW, G]),
                                     ntok[:].unsqueeze(2).broadcast_to([P, NW, G]), ALU.is_gt))
                link(v.tensor_scalar(GM[:], GM[:], NEG, None, ALU.mult))
                dve.wait_ge(c_hg, 1)
                v.tensor_copy(HGH[:], PT[:, 0:G].unsqueeze(1).broadcast_to([P, 4, G]))
                v.tensor_copy(HGL[:], PT[:, G:2 * G].unsqueeze(1).broadcast_to([P, 4, G])).then_inc(c_hgs, 1)
                dve.wait_ge(c_kg, 1)
                kg = PTG[:, 0:CH * G].rearrange("p (c g) -> p c g", g=G)
                link(v.tensor_copy(KGH[:], kg))
                v.tensor_tensor(KGL[:], kg, KGH[:], ALU.subtract).then_inc(c_kgs, 1)

                dve.wait_ge(c_vgh, 1)
                for half in range(2):
                    for i in range(GRP):
                        src = PT if half == 0 else OB
                        dst = (slice(i * G, (i + 1) * G), slice(half * 2, half * 2 + 2), slice(i * HD, (i + 1) * HD))
                        last = v.tensor_tensor(
                            VGL[dst], src[i * G:(i + 1) * G, :].rearrange("p (j i d) -> p j i d", j=2, i=GRP)[:, :, i, :],
                            VGH[dst], ALU.subtract)
                last.then_inc(c_vgl, 1)
                dve.wait_ge(c_b1, 1)
                v.tensor_copy(b1c[:], MISC[:, 448:448 + E * FC]).then_inc(y_read, 1)

                def maxima(w, j):
                    if j == 0:
                        if not (isinstance(w, int) and w == 0):
                            dve.wait_ge(scores_read, w * 4)
                        v.tensor_copy(mask[:, P:K1], GM[:, w, :]).then_inc(mask_set, 1)
                        dve.wait_ge(mask_set, w + 1)
                    dve.wait_ge(scores_done, w * 8 + (2 * j + 2))
                    if not at_start(w, j):
                        dve.wait_ge(exp_done, w * 4 + (j - 1))
                    v.memset(idle_v[:], 0.0)
                    p = j % 2
                    for i in range(GRP):
                        last = v.tensor_tensor_reduce(
                            out=SM[:, p, i, :], in0=SB_[i // 2][:, (i % 2) * K1:(i % 2 + 1) * K1], in1=mask[:],
                            scale=cneg[:], scalar=3e38, op0=ALU.add, op1=ALU.min, accum_out=mn[:, p, i:i + 1])
                    last.then_inc(scores_read, 1)

                def take_pg(w, j):
                    p = j % 2
                    dve.wait_ge(exp_done, w * 4 + (j + 1))
                    if not (isinstance(w, int) and w == 0 and j == 0):
                        dve.wait_ge(ptg_done, w * 4 + j)
                    v.tensor_copy(PG[:], PR[:, p, :, P:K1]).then_inc(pg_ready, 1)

                def invert(w, j):
                    p = j % 2
                    if not at_start(w, j):
                        dve.wait_ge(o_ready, w * 4 + (j - 1))
                    v.reciprocal(rinv[:, p, :], ssum[:, p, :]).then_inc(rinv_ready, 1)

                def take_o(w, j):
                    p = j % 2
                    dve.wait_ge(pv_done, w * 4 + (j + 1))
                    dve.wait_ge(rinv_ready, w * 4 + (j + 1))
                    if j == 0 and not (isinstance(w, int) and w == 0):
                        dve.wait_ge(unit_done, unit_no("oT0", w - 1) + 1)
                    if j == 2 and not (isinstance(w, int) and w == 0):
                        dve.wait_ge(unit_done, unit_no("oT1", w) + 1)
                    v.tensor_tensor(OS[:, j * GRP * HD:(j + 1) * GRP * HD].rearrange("p (h d) -> p h d", d=HD),
                                    OB[:, 0:GRP * HD].rearrange("p (h d) -> p h d", d=HD),
                                    rinv[:, p, :].unsqueeze(2).broadcast_to([P, GRP, HD]), ALU.mult).then_inc(o_ready, 1)

                def take_r(w):
                    dve.wait_ge(y_done, w)
                    v.scalar_tensor_tensor(R[:], YB, cy[:], XN[:, w - 1, :], ALU.mult, ALU.add
                                           ).then_inc(y_read, 1)
                    dve.wait_ge(y_read, w + 1)
                    v.bn_stats(s1[:], R[:]).then_inc(ln_step, 1)
                    dve.wait_ge(ln_step, w * 2 - 1)
                    v.memset(idle_w[:], 0.0)
                    v.bn_aggr(m1[:], s1[:]).then_inc(var_ready, 1)

                def take_ra(w):
                    dve.wait_ge(ln_rstd, w * 2 - 1)
                    dve.wait_ge(var_ready, w * 2 - 1)
                    v.tensor_scalar(ra[:], R[:], m1[:, 0:1], r1[:], ALU.subtract, ALU.mult).then_inc(ra_ready, 1)

                def take_x1(w):
                    dve.wait_ge(x1_ready, w)
                    v.bn_stats(s2[:], X1[:, w - 1, :]).then_inc(ln_step, 1)
                    dve.wait_ge(ln_step, w * 2)
                    v.memset(idle_w[:], 0.0)
                    v.bn_aggr(m2[:], s2[:]).then_inc(var_ready, 1)

                def take_t(w):
                    dve.wait_ge(ln_rstd, w * 2)
                    dve.wait_ge(var_ready, w * 2)
                    v.tensor_scalar(T[:, w - 1, :], X1[:, w - 1, :], m2[:, 0:1], r2[:], ALU.subtract, ALU.mult
                                    ).then_inc(t_ready, 1)

                def body(w, first=False):
                    for j in range(NG):
                        ahead = later(w, j, 2)
                        if ahead:
                            maxima(*ahead)
                        if not first and j == 3:
                            take_ra(w)
                        p = j % 2
                        dve.wait_ge(pt_hi, w * 4 + (j + 1))
                        v.tensor_tensor(PTL[:, p].rearrange("p h n -> p (h n)"), PTB[p][:],
                                        PTH[:, p].rearrange("p h n -> p (h n)"), ALU.subtract).then_inc(pt_lo, 1)
                        dve.wait_ge(ptg_hi, w * 4 + (j + 1))
                        v.tensor_tensor(PGL[:, p], PTG[:, 0:P], PGH[:, p], ALU.subtract).then_inc(ptg_lo, 1)
                        if not first and j == 3:
                            take_x1(w)
                        n = later(w, j, 1)
                        if n:
                            take_pg(*n)
                        if j > 0:
                            take_o(w, j - 1)
                        elif not first:
                            take_o(w - 1, NG - 1)
                        if n:
                            invert(*n)
                        if not first and j == 2:
                            take_r(w)
                        for name in units(w, j):
                            if name[0] != "v":
                                rest_of(unit_no(name, w), *parts(name), unit_bank(name, w))
                        if not first and j == 3:
                            take_t(w)

                maxima(0, 0)
                maxima(0, 1)
                take_pg(0, 0)
                invert(0, 0)
                body(0, first=True)
                with dve.Fori(1, NW - 1) as w:
                    body(w)
                body(NW - 1)
                take_o(NW - 1, NG - 1)
                rest_of(unit_no("oT1", NW), *parts("oT1"), unit_bank("oT1", NW))
                take_r(NW)
                take_ra(NW)
                take_x1(NW)
                take_t(NW)

                dve.wait_ge(lg_done, 1)
                link(v.tensor_tensor(L[:], MISC[:, 0:NW * E].rearrange("p (w e) -> p w e", e=E),
                                     gb_sb[:].unsqueeze(1).broadcast_to([P, NW, E]), ALU.add))
                link(v.tensor_reduce(lmax[:], L[:], AX.X, ALU.max))
                lmax_b = lmax[:].unsqueeze(2).broadcast_to([P, NW, E])
                v.tensor_tensor(Lm[:], L[:], lmax_b, ALU.subtract).then_inc(lm_ready, 1)
                link(v.tensor_tensor(L[:], L[:], lmax_b, ALU.is_equal))
                link(v.tensor_tensor(L[:], L[:], rev_e[:].unsqueeze(1).broadcast_to([P, NW, E]), ALU.mult))
                link(v.tensor_reduce(rv[:], L[:], AX.X, ALU.max))
                link(v.tensor_tensor(L[:], L[:], rv[:].unsqueeze(2).broadcast_to([P, NW, E]), ALU.is_equal))
                link(v.memset(pfa[:, 0:PAD], 0.0))
                pf = window_prefix(L[:].rearrange("p w e -> p (w e)"), E)
                v.tensor_copy(M16[:], L[:])
                v.tensor_copy(MX16[:].rearrange("p w e -> p (w e)"), pf[:, PAD - E:PAD + NW * E - E]).then_inc(m_ready, 1)
                dve.wait_ge(le_ready, 1)
                link(v.tensor_reduce(esum[:], L2[:], AX.X, ALU.add))
                v.reciprocal(gp[:], esum[:])
                link(v.tensor_tensor(L2[:], L[:], base_e[:].unsqueeze(1).broadcast_to([P, NW, E]), ALU.mult))
                link(v.tensor_reduce(ebase[:], L2[:], AX.X, ALU.add))
                dve.wait_ge(mcum, 1)
                link(v.tensor_tensor(L[:], MISC[:, 128:128 + NW * E].rearrange("p (w e) -> p w e", e=E), L[:], ALU.mult))
                link(v.tensor_reduce(pos[:], L[:], AX.X, ALU.add))
                v.tensor_scalar(kept[:], pos[:], float(CAP), None, ALU.is_le)
                link(v.tensor_tensor(slot1[:], pos[:], ebase[:], ALU.add))
                link(v.tensor_tensor(slot1[:], slot1[:], kept[:], ALU.mult))
                link(v.tensor_scalar(slotv[:], slot1[:], -1.0, None, ALU.add))
                for w in range(NW):
                    v.tensor_scalar(SEC[:, w, :], iota_s[:], slotv[:, w:w + 1], None, ALU.is_equal).then_inc(sec_ready, 1)
                link(v.tensor_scalar(gix[:], kept[:], -float(SLOTS + 1), float(SLOTS + 1), ALU.mult, ALU.add))
                link(v.tensor_tensor(gix[:], gix[:], slotv[:], ALU.add))
                v.tensor_copy(gidx[:], gix[:]).then_inc(idx_ready, 1)
                for i in range(4):
                    dve.wait_ge(w1_hi, i + 1)
                    e = slice(2 * i, 2 * i + 2)
                    v.scalar_tensor_tensor(W1L[:, e].rearrange("p e f -> p (e f)"), w1_sb[:, e].rearrange("p e f -> p (e f)"),
                                           wsc[:, 4:5], W1H[:, e].rearrange("p e f -> p (e f)"), ALU.mult, ALU.subtract
                                           ).then_inc(w1_lo, 1)
                dve.wait_ge(dt_hi, 1)
                v.tensor_tensor(DTL[:, 0:512], ps[0][:], DTH[:, 0:512], ALU.subtract).then_inc(dt_lo, 1)
                dve.wait_ge(dt_hi, 2)
                v.tensor_tensor(DTL[:, 512:SLOTS], ps[1][:, 0:SLOTS - 512], DTH[:, 512:SLOTS], ALU.subtract).then_inc(dt_lo, 1)

                def bias_out(e):
                    dve.wait_ge(e_done, e + 1)
                    v.tensor_tensor(EO[:, e, :], ps[6 + e % 2][0:CAP, 0:D], b2b[0:CAP, e, :], ALU.add).then_inc(eo_sb, 1)

                for e in range(E):
                    dve.wait_ge(h_done, e + 1)
                    if e >= 2:
                        dve.wait_ge(h_act, e - 1)
                    v.scalar_tensor_tensor(HA[:, e % 2, :].rearrange("p (c s) -> p c s", s=CAP),
                                           ps[2 + e % 4][:, 0:FC * CAP].rearrange("p (c s) -> p c s", s=CAP), ch[:],
                                           b1c[:, e * FC:(e + 1) * FC].unsqueeze(2).broadcast_to([P, FC, CAP]),
                                           ALU.mult, ALU.add).then_inc(h_sum, 1)
                    if e >= 1:
                        bias_out(e - 1)
                bias_out(E - 1)

                for i in range(NW // XL):
                    c = slice(i * XL, (i + 1) * XL)
                    dve.wait_ge(gathered, 16 * NW)
                    for w in range(i * XL, (i + 1) * XL):
                        last = v.bn_stats(st6[:, w, :], Y[:, w, :])
                    link(last)
                    for w in range(i * XL, (i + 1) * XL):
                        last = v.bn_aggr(mv[:, w, :], st6[:, w, :])
                    link(last)
                    link(v.tensor_tensor(vtmp[:, c], mv[:, c, 1], gp[:, c], ALU.mult))
                    link(v.tensor_tensor(vtmp[:, c], vtmp[:, c], gp[:, c], ALU.mult))
                    link(v.tensor_scalar(vtmp[:, c], vtmp[:, c], LN_EPS, None, ALU.add))
                    dve.sem_inc(fin_var, 1)
                for i in range(NW // XL):
                    c = slice(i * XL, (i + 1) * XL)
                    dve.wait_ge(fin_rstd, i + 1)
                    link(v.tensor_tensor(rms[:, c], rstd[:, c], gp[:, c], ALU.mult))
                    for w in range(i * XL, (i + 1) * XL):
                        last = v.tensor_scalar(Y[:, w, :], Y[:, w, :], mv[:, w, 0:1], rms[:, w:w + 1],
                                               ALU.subtract, ALU.mult)
                    link(last)
                    v.tensor_tensor(OUT[:, c, :], Y[:, c, :], X1[:, c, :], ALU.add).then_inc(fin_add, 1)

            @block.tensor
            def _(pe):
                mm, tr = nc.tensor.matmul, nc.tensor.transpose

                def three(dst, lh, ll, rh, rl, start, stop):
                    mm(dst, lh, rh, start=start, stop=False)
                    mm(dst, lh, rl, start=False, stop=False)
                    return mm(dst, ll, rh, start=False, stop=stop)

                pe.wait_ge(c_pool, 1)
                pe.wait_ge(c_g, 1)
                for i in range(4):
                    if i >= 2:
                        pe.wait_ge(c_gtl, i - 1)
                    for k in range(4):
                        last = tr(PJ[i % 2][:, k * P:(k + 1) * P], GF[:, 4 * i + k, :], ident[:])
                    last.then_inc(c_gt, 1)
                pe.wait_ge(c_scol, 1)
                tr(MISC[0:NW, 0:P], scol[:], ident[:]).then_inc(c_srow, 1)

                def weight_unit(name, w, bank):
                    half = int(name[-1])
                    gh, gl = GTH[:, bass.ts(w, P)], GTL[:, bass.ts(w, P)]
                    if name[0] == "v":
                        f = slice(half * 512, (half + 1) * 512)
                        last = three(bank[:], gh, gl, WH[2][:, f], WL[2][:, f], True, True)
                    else:
                        i = "qk".index(name[0])
                        for c in range(4):
                            f = slice((half * 4 + c) * P, (half * 4 + c + 1) * P)
                            last = three(bank[:, c * P:(c + 1) * P], WH[i][:, f], WL[i][:, f], gh, gl, True, True)
                    last.then_inc(unit_done, 1)

                pe.wait_ge(c_wl, 3)
                pe.wait_ge(c_gtl, 4)
                for i, name in enumerate(FIRST):
                    if i >= 2:
                        wait_bank(pe, name, -1)
                    weight_unit(name, 0, PJ[i % 2])

                pe.wait_ge(c_sel, 1)
                mm(MISC[:, 128:128 + 2 * NW], upper[:], gteq16[:].rearrange("p w e -> p (w e)"), start=True, stop=False)
                mm(MISC[:, 128:128 + 2 * NW], ones[:], gtex16[:].rearrange("p w e -> p (w e)"), start=False, stop=True)
                mm(MISC[:, 192:193], ones[:], tot16[:], start=True, stop=True).then_inc(c_cum, 1)
                pe.wait_ge(c_gi, 1)
                mm(MISC[:, 256:256 + G], ones[:], gi_s[:], start=True, stop=True).then_inc(c_gir, 1)
                pe.wait_ge(c_gl, 1)
                for part, src in ((0, GH), (G, GL)):
                    for w in range(NW):
                        last = mm(PT[:, part:part + G], src[:, w, :], OH[:, w, :], start=(w == 0), stop=(w == NW - 1))
                last.then_inc(c_hg, 1)
                pe.wait_ge(c_hgs, 1)
                for c in range(CH):
                    f = slice(c * P, (c + 1) * P)
                    last = three(PTG[:, c * G:(c + 1) * G], WH[1][:, f], WL[1][:, f], HGH[:, 0, :], HGL[:, 0, :], True, True)
                last.then_inc(c_kg, 1)
                hgh, hgl = (t[:].rearrange("p a g -> p (a g)") for t in (HGH, HGL))
                for half, bank in enumerate((PT, OB)):
                    f = slice(half * 512, (half + 1) * 512)
                    last = three(bank[:], hgh, hgl, WH[2][:, f], WL[2][:, f], True, True)
                last.then_inc(c_vg, 1)
                pe.wait_ge(ld_small, 16 * 8)
                tr(MISC[:, 448:448 + E * FC], b1r[:], ident[0:E * FC, 0:E * FC]).then_inc(c_b1, 1)
                pe.wait_ge(c_kgp, 1)
                pe.wait_ge(c_vgl, 1)
                pe.wait_ge(c_wl, 4)

                def scores(w, j, made):
                    if j in (0, 2):
                        half = j // 2
                        pe.wait_ge(k_padded, w * 2 + (half + 1))
                        wait_split(pe, f"q{half}", made)
                    if not (isinstance(w, int) and w == 0 and j == 0):
                        pe.wait_ge(scores_read, w * 4 + j)
                    for a in range(2):
                        c = 2 * j + a
                        three(SB_[a][:, 0:2 * K1], QH[:, c, :], QL[:, c, :], KPH[:, c].rearrange("p a k -> p (a k)"),
                              KPL[:, c].rearrange("p a k -> p (a k)"), True, True).then_inc(scores_done, 1)

                def turn_probs(w, j):
                    p = j % 2
                    pe.wait_ge(exp_done, w * 4 + (j + 1))
                    if not at_start(w, j):
                        pe.wait_ge(pt_lo, w * 4 + (j - 1))
                    for i in range(GRP):
                        last = tr(PTB[p][:, i * P:(i + 1) * P], PR[:, p, i, 0:P], ident[:])
                    last.then_inc(pt_done, 1)
                    pe.wait_ge(pg_ready, w * 4 + (j + 1))
                    if not (isinstance(w, int) and w == 0 and j == 0):
                        pe.wait_ge(ptg_lo, w * 4 + j)
                    tr(PTG[:, 0:P], PG[:].rearrange("p h g -> p (h g)"), ident[:]).then_inc(ptg_done, 1)

                def values(w, j):
                    if not (isinstance(w, int) and w == 0 and j == 0):
                        pe.wait_ge(o_ready, w * 4 + j)
                    if j in (0, 2):
                        pe.wait_ge(v_split, w * 2 + (j // 2 + 1))
                    if j == 2:
                        pe.wait_ge(y_read, w + 1)
                    pe.wait_ge(ptg_lo, w * 4 + (j + 1))
                    pe.wait_ge(pt_lo, w * 4 + (j + 1))
                    p = j % 2
                    three(OB[:, 0:GRP * HD], PGH[:, p], PGL[:, p], VGH[:, j, :], VGL[:, j, :], True, False)
                    for i in range(GRP):
                        f = slice((GRP * j + i) * HD, (GRP * j + i + 1) * HD)
                        last = three(OB[:, i * HD:(i + 1) * HD], PTH[:, p, i, :], PTL[:, p, i, :], VH[:, f], VL[:, f],
                                     False, i == GRP - 1)
                    last.then_inc(pv_done, 1)

                def turn_o(name, w):
                    half = int(name[-1])
                    pe.wait_ge(o_ready, w * 4 + 2 if half == 0 else w * 4)
                    for c in range(4):
                        f = slice((half * 4 + c) * P, (half * 4 + c + 1) * P)
                        last = tr(unit_bank(name, w)[:, c * P:(c + 1) * P], OS[:, f], ident[:])
                    last.then_inc(unit_done, 1)

                def project(w):
                    wait_split(pe, "oT1", w)
                    pe.wait_ge(o_ready, w * 4 + 1 if not isinstance(w, int) or w < NW else w * 4)
                    for c in range(CH):
                        f = slice(c * D, (c + 1) * D)
                        last = three(YB, OTH[:, c, :], OTL[:, c, :], WH[3][:, f], WL[3][:, f], c == 0, c == CH - 1)
                    last.then_inc(y_done, 1)

                def body(w, first=False):
                    for j in range(NG):
                        n = later(w, j, 2)
                        if n:
                            scores(*n, w if j >= 2 else (w - 1))
                        if j == 2 and not first:
                            project(w)
                        if j > 0:
                            values(w, j - 1)
                        elif not first:
                            values(w - 1, NG - 1)
                        for name in units(w, j):
                            wait_bank(pe, name, w)
                            if name[0] == "o":
                                turn_o(name, w)
                            else:
                                weight_unit(name, w if name == "v1" else w + 1, unit_bank(name, w))
                        n = later(w, j, 1)
                        if n:
                            turn_probs(*n)

                scores(0, 0, -1)
                scores(0, 1, -1)
                turn_probs(0, 0)
                body(0, first=True)
                with pe.Fori(1, NW - 1) as w:
                    body(w)
                body(NW - 1)
                values(NW - 1, NG - 1)
                wait_bank(pe, "oT1", NW)
                turn_o("oT1", NW)
                project(NW)

                pe.wait_ge(t_ready, NW)
                for i in range(4):
                    for k in range(4):
                        last = tr(ps[i][:, k * P:(k + 1) * P], T[:, 4 * i + k, :], ident[:])
                    last.then_inc(tt_done, 1)
                pe.wait_ge(y_read, NW + 1)
                for w in range(NW):
                    if w % 4 == 0:
                        pe.wait_ge(tt_sb, w // 4 + 1)
                    last = mm(MISC[:, w * E:(w + 1) * E], TT[:, w * P:(w + 1) * P], gw_sb[:], start=True, stop=True)
                last.then_inc(lg_done, 1)
                pe.wait_ge(m_ready, 1)
                me = MISC[:, 128:128 + NW * E]
                mm(me, upper[:], M16[:].rearrange("p w e -> p (w e)"), start=True, stop=False)
                mm(me, ones[:], MX16[:].rearrange("p w e -> p (w e)"), start=False, stop=True).then_inc(mcum, 1)
                pe.wait_ge(tt_sb, 4)
                for w in range(NW):
                    pe.wait_ge(sec_ready, w + 1)
                    pe.wait_ge(tl_ready, w // 4 + 1)
                    for src in (TH, TL):
                        a, b = (w == 0 and src is TH), (w == NW - 1 and src is TL)
                        mm(ps[0][:], src[:, w, :], SEC[:, w, 0:512], start=a, stop=b)
                        last = mm(ps[1][:, 0:SLOTS - 512], src[:, w, :], SEC[:, w, 512:SLOTS], start=a, stop=b)
                last.then_inc(disp_done, 1)

                pe.wait_ge(dt_lo, 2)

                def down(e):
                    pe.wait_ge(h_act, e + 1)
                    if e >= 2:
                        pe.wait_ge(eo_sb, e - 1)
                    for c in range(FC):
                        last = mm(ps[6 + e % 2][0:CAP, 0:D], HS[:, e, c, :], w2_sb[:, e, c, :], start=(c == 0), stop=(c == FC - 1))
                    last.then_inc(e_done, 1)

                for e in range(E):
                    pe.wait_ge(w1_lo, e // 2 + 1)
                    if e >= 4:
                        pe.wait_ge(h_sum, e - 3)
                    s = slice(e * CAP, (e + 1) * CAP)
                    for c in range(FC):
                        f = slice(c * P, (c + 1) * P)
                        last = three(ps[2 + e % 4][:, c * CAP:(c + 1) * CAP], W1H[:, e, f], W1L[:, e, f],
                                     DTH[:, s], DTL[:, s], True, True)
                    last.then_inc(h_done, 1)
                    if e >= 2:
                        down(e - 2)
                down(E - 2)
                down(E - 1)


_INS = ['L0_attn_x', 'L0_attn_norm_w', 'L0_attn_w_q', 'L0_attn_w_k', 'L0_attn_w_v', 'L0_attn_w_out',
        'L0_attn_scorer_w', 'L0_attn_scorer_b', 'L0_ffn_gate_w', 'L0_ffn_gate_b', 'L0_ffn_w1', 'L0_ffn_b1',
        'L0_ffn_w2', 'L0_ffn_b2']


def kernel(**inputs):
    import numpy as _np
    import concourse.bacc as _bacc
    from concourse import mybir as _mybir
    from concourse.bass_utils import run_bass_kernel_spmd as _run

    nc = _bacc.Bacc("TRN2", target_bir_lowering=False, num_devices=1)
    arrays, args = {}, []
    for name in _INS:
        a = _np.ascontiguousarray(inputs[name])
        arrays[f"in_{name}"] = a
        args.append(nc.dram_tensor(f"in_{name}", a.shape, _mybir.dt.from_np(a.dtype), kind="ExternalInput").ap())
    shape = inputs['L0_attn_x'].shape
    args.append(nc.dram_tensor("out_0", shape, _mybir.dt.float32, kind="ExternalOutput").ap())
    build(nc, *args)
    r = _run(nc, [arrays], core_ids=[0])
    return r.results[0]["out_0"]
```

```python
from contextlib import ExitStack

import concourse.bass as bass
from concourse import mybir


def build(nc, x, norm_w, w_q, w_k, w_v, w_out, scorer_w, scorer_b, gate_w, gate_b, w1, b1, w2, b2, out):
    f32, f16, u32 = mybir.dt.float32, mybir.dt.float16, mybir.dt.uint32
    ALU, ACT, AX = mybir.AluOpType, mybir.ActivationFunctionType, mybir.AxisListType
    RED = bass.bass_isa.ReduceOp

    P = 128
    S, D = x.shape[1], x.shape[2]
    INNER = w_q.shape[1]
    HD = 64
    H = INNER // HD
    NW = S // P
    G = 32
    K1 = P + G
    CH = INNER // P
    GRP = 4
    NG = H // GRP
    E, F = w1.shape[0], w1.shape[2]
    CAP = 80
    SLOTS = E * CAP
    FC = F // P
    NEG = -2e38
    RMS_EPS, LN_EPS = 1e-6, 1e-5
    WS = 16.0
    EXPONENT = 0x7F800000

    ctx = ExitStack()
    with ctx:
        def sb(name, shape, dt=f32):
            return ctx.enter_context(nc.sbuf_tensor(name, shape, dt))

        def sem(name):
            return ctx.enter_context(nc.semaphore(name))

        X = sb("X", [P, NW, D])
        XN = sb("XN", [P, NW, D])
        GF = sb("GF", [P, NW, D])
        GH, GL = sb("GH", [P, NW, D], f16), sb("GL", [P, NW, D], f16)
        GTH, GTL = sb("GTH", [P, NW, K1], f16), sb("GTL", [P, NW, K1], f16)
        WB = sb("WB", [P, 5 * INNER])
        WF = [WB[:, i * INNER:(i + 1) * INNER] for i in range(4)]
        WPH, WPL = sb("WPH", [P, 4 * INNER], f16), sb("WPL", [P, 4 * INNER], f16)
        MH, ML = (t[:, 0:H * P].rearrange("p (h n) -> p h n", n=P) for t in (WPH, WPL))
        WVH, WVL = (t[:, 2 * INNER:3 * INNER] for t in (WPH, WPL))
        WOH, WOL = (t[:, 3 * INNER:4 * INNER] for t in (WPH, WPL))
        nwcol, nwrow, swrow = sb("nwcol", [P, 1]), sb("nwrow", [P, D]), sb("swrow", [P, D])
        sbcol, nwabs = sb("sbcol", [P, 1]), sb("nwabs", [P, 1])
        gw_sb, gb_sb = sb("gw_sb", [P, E]), sb("gb_sb", [P, E])
        w1_sb, w2_sb = sb("w1_sb", [P, E, F]), sb("w2_sb", [P, E, FC, D])
        W1H, W1L = (t[:].rearrange("p (e f) -> p e f", f=F) for t in (WPH, WPL))
        b1r, b1c, b2b = sb("b1r", [E * FC, P]), sb("b1c", [P, E * FC]), sb("b2b", [P, E, D])

        ident = sb("ident", [P, P])
        upper = sb("upper", [P, P], f16)
        ones = sb("ones", [P, P], f16)
        mask = sb("mask", [P, K1])
        iota_g = sb("iota_g", [P, G])
        iota_s = sb("iota_s", [P, SLOTS], f16)
        ntok = sb("ntok", [P, NW])
        rev_e, base_e = sb("rev_e", [P, E]), sb("base_e", [P, E])
        mhalf = sb("mhalf", [P, NW])
        zero_row = sb("zero_row", [1, D + 2])
        epscol = sb("epscol", [P, 1])
        idle_q, idle_v, idle_w = (sb(n, [P, 1]) for n in ("idle_q", "idle_v", "idle_w"))

        st6 = sb("st6", [P, NW, 6])
        mv = sb("mv", [P, NW, 2])
        vtmp, rstd, rms, std = (sb(n, [P, NW]) for n in ("vtmp", "rstd", "rms", "std"))
        wmax, wred, wpow, winv, wsc = (sb(n, [P, 4]) for n in ("wmax", "wred", "wpow", "winv", "wsc"))
        msc, cneg = sb("msc", [P, 1]), sb("cneg", [P, 1])
        gs, vg_eps, nb_g, nb_x = (sb(n, [P, NW]) for n in ("gs", "vg_eps", "nb_g", "nb_x"))
        cy, ch = sb("cy", [P, 1]), sb("ch", [P, 1])
        w1max2 = sb("w1max2", [P, 2])
        w1max, w1red, w1pow, w1sc = (sb(n, [P, 1]) for n in ("w1max", "w1red", "w1pow", "w1sc"))

        scol = sb("scol", [P, NW])
        srow, t16 = sb("srow", [NW, P]), sb("t16", [NW, G])
        tmax = sb("tmax", [P, 8])
        gteq = sb("gteq", [P, NW, 2])
        gteq16 = sb("gteq16", [P, NW, 2], f16)
        tot16, tot, ngt, need = sb("tot16", [P, 1], f16), sb("tot", [P, 1]), sb("ngt", [P, 1]), sb("need", [P, 1])
        keq, kslot, gslot = (sb(n, [P, NW]) for n in ("keq", "kslot", "gslot"))
        OH = sb("OH", [P, NW, G], f16)
        gi_c, ntok16 = sb("gi_c", [P, G]), sb("ntok16", [P, NW], f16)
        GM = sb("GM", [P, NW, G])
        HGH, HGL = sb("HGH", [P, 4, G], f16), sb("HGL", [P, 4, G], f16)

        AH, AL = sb("AH", [P, H, P], f16), sb("AL", [P, H, P], f16)
        WQT, WKT = (t[:].rearrange("p h n -> p (h n)").bitcast(f32) for t in (AH, AL))
        VF = sb("VF", [P, INNER])
        VH, VL = sb("VH", [P, INNER], f16), sb("VL", [P, INNER], f16)
        VGH, VGL = sb("VGH", [P, NG, GRP * HD], f16), sb("VGL", [P, NG, GRP * HD], f16)
        SM, PR = sb("SM", [P, 2, GRP, K1]), sb("PR", [P, 2, GRP, K1])
        SM_flat = SM[:].rearrange("p a h k -> p (a h k)")
        tall = SM_flat[:, 0:NW * G]
        mn, ssum, rinv = (sb(n, [P, 2, GRP]) for n in ("mn", "ssum", "rinv"))
        PG = sb("PG", [P, GRP, G])
        PTH, PTL = sb("PTH", [P, 2, GRP, P], f16), sb("PTL", [P, 2, GRP, P], f16)
        PGH, PGL = sb("PGH", [P, 2, P], f16), sb("PGL", [P, 2, P], f16)
        OS = sb("OS", [P, INNER])
        OTH, OTL = sb("OTH", [P, CH, P], f16), sb("OTL", [P, CH, P], f16)
        R = sb("R", [P, D])
        ra = sb("ra", [P, D])
        X1 = sb("X1", [P, NW, D])
        s1, m1, v1, r1 = sb("s1", [P, 6]), sb("m1", [P, 2]), sb("v1", [P, 1]), sb("r1", [P, 1])
        s2, m2, v2, r2 = sb("s2", [P, 6]), sb("m2", [P, 2]), sb("v2", [P, 1]), sb("r2", [P, 1])

        T, TH, TL = GF, GH, GL
        TT = X[:].rearrange("p w d -> p (w d)")
        L, L2, Lm = sb("L", [P, NW, E]), sb("L2", [P, NW, E]), sb("Lm", [P, NW, E])
        lmax, rv, esum, gp, gp2 = (sb(n, [P, NW]) for n in ("lmax", "rv", "esum", "gp", "gp2"))
        M16 = sb("M16", [P, NW, E], f16)
        pos, ebase, kept, slot1, slotv, gix = (sb(n, [P, NW]) for n in ("pos", "ebase", "kept", "slot1", "slotv", "gix"))
        gidx = sb("gidx", [P, NW], u32)
        SEC = WB[:].bitcast(f16).rearrange("p (w s) -> p w s", s=SLOTS)
        DTH, DTL = sb("DTH", [P, SLOTS], f16), sb("DTL", [P, SLOTS], f16)
        HA = SM_flat[:, 0:2 * FC * CAP].rearrange("p (a s) -> p a s", a=2)
        HS = sb("HS", [P, E, FC, CAP])
        EO = PR[:].rearrange("p a h k -> p (a h k)")[0:CAP, 0:E * (D + 2)].rearrange("p (e d) -> p e d", d=D + 2)
        st_e = sb("st_e", [CAP, E, 6])
        Y = sb("Y", [P, NW, D + 2])
        OUT = XN

        ps = [ctx.enter_context(nc.psum_tensor(f"ps{i}", [P, 512], f32)) for i in range(8)]
        SB_, PJ = [ps[0], ps[1]], [ps[2], ps[3]]
        PTG, OB, MISC = ps[5], ps[6], ps[7]
        VG_BANKS = (OB, ps[3])
        PT, PTB = ps[4], [ps[4], ps[7]]
        YB = OB[:, GRP * HD:GRP * HD + D]

        MB = [ps[0], ps[1], ps[4], ps[5]]

        def product_at(h):
            return h % 2 * (H // 2) + h // 2

        def product(h):
            i = product_at(h)
            return MB[i // 4][:, (i % 4) * P:(i % 4 + 1) * P]

        BANKS = (0, 2, 1, 3)

        def heads_in(t, i):
            h = [h for h in range(H) if product_at(h) // 4 == i]
            return t[:, h[0]:h[-1] + 1:2, :]

        top_dram = nc.dram_tensor("top_scratch", [NW, G], f32, kind="Internal").ap()
        eo_dram = nc.dram_tensor("expert_scratch", [SLOTS + 1, D + 2], f32, kind="Internal").ap()

        ld_x = [sem(f"ld_x{i}") for i in range(4)]
        gathered = [sem(f"gathered{i}") for i in range(4)]
        ld_w = [sem(f"ld_w{n}") for n in "qkvo"]
        (ld_nw, ld_small, ld_moe, top_out, top_in, zrow_out, eo_out, s_out) = map(
            sem, ("ld_nw", "ld_small", "ld_moe", "top_out", "top_in", "zrow_out", "eo_out", "s_out"))
        (c_pool, c_wmax, c_wred, c_wsc, c_wh, c_wl, c_stat, c_rstd, c_g, c_gh, c_gl, c_gt, c_gth, c_gtl) = map(
            sem, ("c_pool", "c_wmax", "c_wred", "c_wsc", "c_wh", "c_wl", "c_stat", "c_rstd", "c_g", "c_gh", "c_gl",
                  "c_gt", "c_gth", "c_gtl"))
        dve_chain, pool_chain = sem("dve_chain"), sem("pool_chain")
        (c_scol, c_srow, c_t16, c_sel, c_cum, c_oh, c_hg, c_hgs, c_gir, c_gk, c_wt, c_wts,
         c_mm, c_wn, c_g2, c_nbg, c_nbx, c_xn, c_ws, c_wvoh, c_wvol, c_w1max, c_w1red, c_w1sc, c_vg, c_vgh, c_vgl) = map(
            sem, ("c_scol", "c_srow", "c_t16", "c_sel", "c_cum", "c_oh", "c_hg", "c_hgs",
                  "c_gir", "c_gk", "c_wt", "c_wts", "c_mm", "c_wn", "c_g2", "c_nbg",
                  "c_nbx", "c_xn", "c_ws", "c_wvoh", "c_wvol", "c_w1max", "c_w1red", "c_w1sc", "c_vg", "c_vgh", "c_vgl"))
        (scores_done, scores_read, exp_done, rinv_ready, unit_done, unit_hi, unit_lo,
         pt_done, pt_hi, pt_lo, ptg_done, ptg_hi, ptg_lo, pv_done, o_ready, y_done, y_read, var_ready, eps_added,
         ln_rstd, ln_step, mask_set, pg_ready, v_head, v_split, ra_ready, x1_ready) = map(
            sem, ("scores_done", "scores_read", "exp_done", "rinv_ready", "unit_done", "unit_hi",
                  "unit_lo", "pt_done", "pt_hi", "pt_lo", "ptg_done", "ptg_hi", "ptg_lo", "pv_done",
                  "o_ready", "y_done", "y_read", "var_ready", "eps_added", "ln_rstd", "ln_step", "mask_set", "pg_ready",
                  "v_head", "v_split", "ra_ready", "x1_ready"))
        (t_ready, tl_ready, th_ready, tt_done, tt_sb, lg_done, m_ready, lm_ready, le_ready, mcum, sec_ready,
         disp_done, dt_hi, dt_lo, h_done, h_act, h_sum, e_done, eo_sb, eo_rows, idx_ready, w1_hi, w1_lo, fin_var,
         fin_std, fin_add) = map(
            sem, ("t_ready", "tl_ready", "th_ready", "tt_done", "tt_sb", "lg_done", "m_ready", "lm_ready",
                  "le_ready", "mcum", "sec_ready", "disp_done", "dt_hi", "dt_lo", "h_done", "h_act", "h_sum", "e_done",
                  "eo_sb", "eo_rows", "idx_ready", "w1_hi", "w1_lo", "fin_var", "fin_std", "fin_add"))

        x_v = x[0].rearrange("(w p) d -> p w d", p=P)
        out_v = out[0].rearrange("(w p) d -> p w d", p=P)
        XL = 4
        LO, HI = slice(0, NW // 2), slice(NW // 2, NW)

        FIRST = ["a0", "a1", "a2", "a3", "v0"]
        STEP = [["a0", "v1"], ["oT1", "a1"], ["a2", "v0"], ["a3", "oT0"]]

        def units(w, j):
            if not isinstance(w, int):
                return STEP[j]
            if w == NW:
                return ["oT1"] if j == 0 else []
            none = ["oT1"] if w == 0 else FIRST if w == NW - 1 else []
            return [u for u in STEP[j] if u not in none]

        order = [(-1, u) for u in FIRST] + [(w, u) for w in range(NW + 1) for j in range(NG) for u in units(w, j)]
        order_lo = [x for x in order if x[1][0] != "v"]

        def place(seq, name, w):
            if isinstance(w, int):
                return seq.index((w, name))
            per = seq.index((2, name)) - seq.index((1, name))
            assert all(seq.index((i, name)) == seq.index((1, name)) + per * (i - 1) for i in range(1, NW - 1))
            return w * per + (seq.index((1, name)) - per)

        def unit_no(name, w):
            return place(order, name, w)

        def unit_bank(name, w):
            return PJ[order.index((w if isinstance(w, int) else 2, name)) % 2]

        def wait_split(eng, name, w):
            if name[0] == "v":
                eng.wait_ge(unit_hi, place(order, name, w) + 1)
            else:
                eng.wait_ge(unit_lo, place(order_lo, name, w) + 1)

        def wait_bank(eng, name, w):
            static = isinstance(w, int)
            w2, name2 = order[order.index((w if static else 2, name)) - 2]
            wait_split(eng, name2, w2 if static else w if w2 == 2 else w - 1)

        def later(w, j, k):
            w, j = (w, j + k) if j + k < NG else (w + 1, j + k - NG)
            return None if isinstance(w, int) and w == NW else (w, j)

        def at_start(w, j):
            return isinstance(w, int) and w == 0 and j < 2

        with nc.Block() as block:

            @block.sync
            def _(sp):
                for i in range(NW // XL):
                    sp.dma_start(X[:, i * XL:(i + 1) * XL, :], x_v[:, i * XL:(i + 1) * XL, :]).then_inc(ld_x[i], 16)
                for i, w in enumerate((w_q, w_k, w_v)):
                    sp.dma_start(WF[i], w).then_inc(ld_w[i], 16)
                sp.dma_start(WF[3].rearrange("p (c d) -> p c d", d=D),
                             w_out.rearrange("(c p) d -> p c d", p=P)).then_inc(ld_w[3], 16)
                sp.dma_start(w1_sb[:], w1.rearrange("e d f -> d e f")).then_inc(ld_moe, 16)
                sp.dma_start(w2_sb[:], w2.rearrange("e (c p) d -> p e c d", p=P)).then_inc(ld_moe, 16)
                sp.wait_ge(c_t16, 1)
                sp.dma_start(top_dram, t16[:]).then_inc(top_out, 16)
                sp.wait_ge(top_out, 16)
                sp.dma_start(tall[:], top_dram.rearrange("(a w) g -> a (w g)", a=1).partition_broadcast(P)
                             .rearrange("p a n -> p (a n)")).then_inc(top_in, 16)
                for i in range(2):
                    sp.wait_ge(eo_rows, (i + 1) * E // 2)
                    e0, e1 = i * E // 2, (i + 1) * E // 2
                    sp.dma_start(eo_dram[e0 * CAP:e1 * CAP, :].rearrange("(e s) d -> s e d", s=CAP),
                                 EO[:, e0:e1, :]).then_inc(eo_out, 16)
                for i in range(NW // XL):
                    sp.wait_ge(fin_add, i + 1)
                    sp.dma_start(out_v[:, i * XL:(i + 1) * XL, :], OUT[:, i * XL:(i + 1) * XL, :]).then_inc(s_out, 16)
                sp.wait_ge(s_out, 16 * (NW // XL))

            @block.gpsimd
            def _(pool):
                g = nc.gpsimd
                g.memset(mhalf[:], -0.5)
                g.memset(ident[:], 0.0)
                g.memset(upper[:], 1.0)
                g.memset(ones[:], 1.0)
                g.memset(mask[:, 0:P], 0.0)
                g.memset(zero_row[:], 0.0)
                g.memset(epscol[:], LN_EPS)
                g.memset(VGH[:], 0.0)
                g.memset(VGL[:], 0.0)
                g.iota(iota_g[:], pattern=[[1, G]], base=1, channel_multiplier=0, allow_small_or_imprecise_dtypes=True)
                g.iota(iota_s[:], pattern=[[1, SLOTS]], base=0, channel_multiplier=0,
                       allow_small_or_imprecise_dtypes=True)
                g.iota(ntok[:], pattern=[[P, NW]], base=0, channel_multiplier=1, allow_small_or_imprecise_dtypes=True)
                g.iota(rev_e[:], pattern=[[-1, E]], base=E, channel_multiplier=0, allow_small_or_imprecise_dtypes=True)
                g.iota(base_e[:], pattern=[[CAP, E]], base=0, channel_multiplier=0,
                       allow_small_or_imprecise_dtypes=True).then_inc(pool_chain, 1)
                pool.wait_ge(pool_chain, 1)
                g.affine_select(out=ident[:], in_=ident[:], compare_op=ALU.not_equal, fill=1.0, base=0,
                                pattern=[[-1, P]], channel_multiplier=1)
                g.affine_select(out=upper[:], in_=upper[:], compare_op=ALU.is_ge, fill=0.0, base=0,
                                pattern=[[1, P]], channel_multiplier=-1)
                g.affine_select(out=mask[:, 0:P], in_=mask[:, 0:P], compare_op=ALU.is_ge, fill=NEG, base=0,
                                pattern=[[-1, P]], channel_multiplier=1).then_inc(c_pool, 1)
                g.dma_start(eo_dram[SLOTS:SLOTS + 1, :], zero_row[:]).then_inc(zrow_out, 16)

                for i, (src, dst, c) in enumerate(((vg_eps, gs, HI), (vg_eps, gs, LO), (vtmp, rstd, slice(0, NW)))):
                    pool.wait_ge(c_stat, 1)
                    g.tensor_tensor(dst[:, c], src[:, c], mhalf[:, c], ALU.pow).then_inc(c_rstd, 1)
                    if i == 1:
                        pool.wait_ge(c_wmax, 1)
                        g.partition_all_reduce(wred[:], wmax[:], P, RED.max).then_inc(c_wred, 1)
                pool.wait_ge(c_gh, 1)
                g.tensor_tensor(GL[:], GF[:], GH[:], ALU.subtract).then_inc(c_gl, 1)
                for i, hi, lo in ((2, WVH, WVL), (3, WOH, WOL)):
                    pool.wait_ge(c_wvoh, i - 1)
                    g.tensor_tensor(lo, WF[i], hi, ALU.subtract).then_inc(c_wvol, 1)

                def ln_pow(n, var, vt, r):
                    pool.wait_ge(var_ready, n)
                    g.tensor_tensor(vt[:], var[:, 1:2], epscol[:], ALU.add).then_inc(eps_added, 1)
                    pool.wait_ge(eps_added, n)
                    g.tensor_tensor(r[:], vt[:], mhalf[:, 0:1], ALU.pow).then_inc(ln_rstd, 1)

                def split_v(half, unit, readers, splits_before):
                    v_s = slice(half * 512, (half + 1) * 512)
                    pool.wait_ge(unit_hi, unit + 1)
                    if readers is not None:
                        pool.wait_ge(pv_done, readers)
                        pool.wait_ge(v_split, splits_before)
                    g.tensor_tensor(idle_q[:], mhalf[:, 0:1], mhalf[:, 0:1], ALU.add)
                    g.tensor_scalar(VH[:, v_s], VF[:, v_s], 1.0, None, ALU.mult).then_inc(v_head, 1)
                    pool.wait_ge(v_head, splits_before + 1)
                    g.tensor_tensor(VL[:, v_s], VF[:, v_s], VH[:, v_s], ALU.subtract).then_inc(v_split, 1)

                def body(w, first=False, last=False):
                    split_v(1, unit_no("v1", w), None if first else w * 4, w * 2 + 1)
                    if not first:
                        ln_pow(w * 2 - 1, m1, v1, r1)
                        add_x(w)
                        ln_pow(w * 2, m2, v2, r2)
                    if not last:
                        split_v(0, unit_no("v0", w), w * 4 + 2, w * 2 + 2)

                def add_x(w):
                    pool.wait_ge(ra_ready, w)
                    g.tensor_tensor(X1[:, w - 1, :], ra[:], X[:, w - 1, :], ALU.add).then_inc(x1_ready, 1)

                split_v(0, 4, None, 0)
                body(0, first=True)
                with pool.Fori(1, NW - 2, 2) as w:
                    body(w)
                    body(w + 1)
                body(NW - 1, last=True)

                def rest_of_t(i):
                    q = slice(i * NW // 4, (i + 1) * NW // 4)
                    pool.wait_ge(th_ready, i + 1)
                    g.tensor_tensor(TL[:, q, :], T[:, q, :], TH[:, q, :], ALU.subtract).then_inc(tl_ready, 1)

                ln_pow(2 * NW - 1, m1, v1, r1)
                add_x(NW)
                ln_pow(2 * NW, m2, v2, r2)
                pool.wait_ge(c_w1max, 1)
                g.partition_all_reduce(w1red[:], w1max[:], P, RED.max).then_inc(c_w1red, 1)
                for i in range(4):
                    rest_of_t(i)

                pool.wait_ge(idx_ready, 1)
                pool.wait_ge(eo_out, 32)
                pool.wait_ge(zrow_out, 16)
                for w in range(NW):
                    g.indirect_dma_start(out=Y[:, w, :], out_offset=None, in_=eo_dram,
                                         in_offset=bass.IndirectOffsetOnAxis(ap=gidx[:, w:w + 1], axis=0)
                                         ).then_inc(gathered[w // XL], 16)

            @block.scalar
            def _(act):
                a_ = nc.scalar
                act.dma_start(nwcol[:], norm_w.rearrange("(p a) -> p a", a=1)).then_inc(ld_nw, 16)
                act.dma_start(nwrow[:], norm_w.rearrange("(a d) -> a d", a=1).partition_broadcast(P)
                              .rearrange("p a d -> p (a d)")).then_inc(ld_small, 16)
                act.dma_start(swrow[:], scorer_w.rearrange("d a -> a d").partition_broadcast(P)
                              .rearrange("p a d -> p (a d)")).then_inc(ld_small, 16)
                act.dma_start(sbcol[:], scorer_b.rearrange("(a d) -> a d", a=1).partition_broadcast(P)
                              .rearrange("p a d -> p (a d)")).then_inc(ld_small, 16)
                act.dma_start(gw_sb[:], gate_w).then_inc(ld_small, 16)
                act.dma_start(gb_sb[:], gate_b.rearrange("(a d) -> a d", a=1).partition_broadcast(P)
                              .rearrange("p a d -> p (a d)")).then_inc(ld_small, 16)
                act.dma_start(b1r[:], b1.rearrange("e (c p) -> (e c) p", p=P)).then_inc(ld_small, 16)
                act.dma_start(b2b[:], b2.rearrange("(a e) d -> a (e d)", a=1).partition_broadcast(P)
                              .rearrange("p a (e d) -> p (a e) d", e=E)).then_inc(ld_small, 16)

                act.wait_ge(ld_nw, 16)
                for i in range(2):
                    act.wait_ge(ld_w[i], 16)
                    a_.activation(WF[i], WF[i], ACT.Copy, scale=nwcol[:]).then_inc(c_wn, 1)
                act.wait_ge(c_nbg, 1)
                for w in range(NW // 2, NW):
                    last = a_.activation(GF[:, w, :], X[:, w, :], ACT.Identity, bias=nb_g[:, w:w + 1], scale=gs[:, w:w + 1])
                last.then_inc(c_g2, 1)
                for i in range(4):
                    act.wait_ge(c_wt, i + 1)
                    a_.activation((WQT, WKT)[i // 2][:, (i % 2) * 512:(i % 2 + 1) * 512], MB[i][:], ACT.Copy).then_inc(c_wts, 1)
                for i in range(4):
                    if i == 2:
                        act.wait_ge(c_g, 1)
                        act.wait_ge(c_g2, 1)
                        a_.activation(GH[:], GF[:], ACT.Copy).then_inc(c_gh, 1)
                    act.wait_ge(c_gt, i + 1)
                    a_.activation(GTH[:, 4 * i:4 * i + 4, 0:P], PJ[i % 2][:].rearrange("p (w n) -> p w n", n=P),
                                  ACT.Copy).then_inc(c_gth, 1)
                act.wait_ge(c_wsc, 1)
                for n, i in enumerate(BANKS):
                    act.wait_ge(c_mm, n + 1)
                    a_.activation(heads_in(MH, i), MB[i][:].rearrange("p (h n) -> p h n", n=P), ACT.Copy, scale=msc[:]
                                  ).then_inc(c_wh, 1)
                for i, hi in ((2, WVH), (3, WOH)):
                    a_.activation(WF[i], WF[i], ACT.Copy, scale=wsc[:, i:i + 1]).then_inc(c_ws, 1)
                    act.wait_ge(c_ws, i - 1)
                    a_.activation(hi, WF[i], ACT.Copy).then_inc(c_wvoh, 1)

                def head_of(unit, dst, bank):
                    act.wait_ge(unit_done, unit + 1)
                    a_.activation(dst, bank[:], ACT.Copy).then_inc(unit_hi, 1)

                def dest(name):
                    half = int(name[-1])
                    if name[0] == "v":
                        return VF[:, half * 512:(half + 1) * 512]
                    t = {"a": AH, "o": OTH}[name[0]]
                    return t[:, half * 4:(half + 1) * 4, :].rearrange("p c n -> p (c n)")

                for i, name in enumerate(FIRST):
                    head_of(i, dest(name), PJ[i % 2])

                act.wait_ge(c_nbx, 1)
                for w in range(NW):
                    last = a_.activation(XN[:, w, :], X[:, w, :], ACT.Identity, bias=nb_x[:, w:w + 1], scale=rstd[:, w:w + 1])
                last.then_inc(c_xn, 1)
                def exps(w, j):
                    act.wait_ge(scores_read, w * 4 + (j + 1))
                    if not at_start(w, j):
                        act.wait_ge(rinv_ready, w * 4 + (j - 1))
                        act.wait_ge(pg_ready, w * 4 + (j - 1))
                        act.wait_ge(pt_done, w * 4 + (j - 1))
                    p = j % 2
                    for i in range(GRP):
                        last = a_.activation(PR[:, p, i, :], SM[:, p, i, :], ACT.Exp, bias=mn[:, p, i:i + 1], scale=-1.0,
                                             accum_out=ssum[:, p, i:i + 1])
                    last.then_inc(exp_done, 1)

                def take_pg(w, j):
                    if not (isinstance(w, int) and w == 0 and j == 0):
                        act.wait_ge(ptg_done, w * 4 + j)
                    act.wait_ge(exp_done, w * 4 + (j + 1))
                    a_.activation(PG[:], PR[:, j % 2, :, P:K1], ACT.Copy).then_inc(pg_ready, 1)

                def body(w, first=False):
                    for j in range(NG):
                        p = j % 2
                        if not at_start(w, j):
                            act.wait_ge(pv_done, w * 4 + (j - 1))
                        act.wait_ge(pt_done, w * 4 + (j + 1))
                        a_.activation(PTH[:, p].rearrange("p h n -> p (h n)"), PTB[p][:], ACT.Copy).then_inc(pt_hi, 1)
                        n = later(w, j, 1)
                        if n:
                            exps(*n)
                        act.wait_ge(ptg_done, w * 4 + (j + 1))
                        a_.activation(PGH[:, p], PTG[:, 0:P], ACT.Copy).then_inc(ptg_hi, 1)
                        for name in units(w, j):
                            if name == "v1" and not first:
                                act.wait_ge(v_split, w * 2)
                            if name == "v0":
                                act.wait_ge(v_split, w * 2 + 1)
                            if name[0] == "a":
                                act.wait_ge(scores_done, w * 8 + (2 * int(name[-1]) + 2))
                            head_of(unit_no(name, w), dest(name), unit_bank(name, w))
                        if n:
                            take_pg(*n)

                exps(0, 0)
                act.wait_ge(c_vg, 1)
                for half in range(2):
                    for i in range(GRP):
                        src = VG_BANKS[half]
                        last = a_.activation(
                            VGH[i * G:(i + 1) * G, half * 2:half * 2 + 2, i * HD:(i + 1) * HD],
                            src[i * G:(i + 1) * G, :].rearrange("p (j i d) -> p j i d", j=2, i=GRP)[:, :, i, :], ACT.Copy)
                last.then_inc(c_vgh, 1)
                take_pg(0, 0)
                body(0, first=True)
                with act.Fori(1, NW - 2, 2) as w:
                    body(w)
                    body(w + 1)
                body(NW - 1)

                def head_of_t(i):
                    q = slice(i * NW // 4, (i + 1) * NW // 4)
                    act.wait_ge(t_ready, (i + 1) * NW // 4)
                    a_.activation(TH[:, q, :], T[:, q, :], ACT.Copy).then_inc(th_ready, 1)

                def take_tt(i):
                    act.wait_ge(tt_done, i + 1)
                    a_.activation(TT[:, i * 512:(i + 1) * 512], ps[i % 2][:], ACT.Copy).then_inc(tt_sb, 1)

                take_tt(0)
                take_tt(1)
                head_of(unit_no("oT1", NW), dest("oT1"), unit_bank("oT1", NW))
                head_of_t(0)
                head_of_t(1)
                head_of_t(2)
                take_tt(2)
                take_tt(3)
                head_of_t(3)
                act.wait_ge(lm_ready, 1)
                a_.activation(L2[:], Lm[:], ACT.Exp).then_inc(le_ready, 1)
                act.wait_ge(c_w1sc, 1)
                for i in range(4):
                    a_.activation(W1H[:, 2 * i:2 * i + 2, :], w1_sb[:, 2 * i:2 * i + 2, :], ACT.Copy,
                                  scale=w1sc[:]).then_inc(w1_hi, 1)
                act.wait_ge(disp_done, 1)
                a_.activation(DTH[:, 0:512], ps[0][:], ACT.Copy).then_inc(dt_hi, 1)
                a_.activation(DTH[:, 512:SLOTS], ps[1][:, 0:SLOTS - 512], ACT.Copy).then_inc(dt_hi, 1)
                for e in range(E):
                    act.wait_ge(h_sum, e + 1)
                    a_.activation(HS[:, e].rearrange("p c s -> p (c s)"), HA[:, e % 2, :], ACT.Gelu_apprx_tanh
                                  ).then_inc(h_act, 1)
                for i in range(NW // XL):
                    c = slice(i * XL, (i + 1) * XL)
                    act.wait_ge(fin_var, i + 1)
                    a_.activation(std[:, c], vtmp[:, c], ACT.Sqrt).then_inc(fin_std, 1)

            @block.vector
            def _(dve):
                v = nc.vector
                chain = [0]

                def link(ins):
                    chain[0] += 1
                    ins.then_inc(dve_chain, 1)
                    dve.wait_ge(dve_chain, chain[0])

                for i in range(NW // XL):
                    dve.wait_ge(ld_x[i], 16)
                    for w in range(i * XL, (i + 1) * XL):
                        last = v.bn_stats(st6[:, w, :], X[:, w, :])
                link(last)
                for w in range(NW):
                    last = v.bn_aggr(mv[:, w, :], st6[:, w, :])
                link(last)
                link(v.tensor_scalar(vtmp[:], mv[:, :, 1], LN_EPS, None, ALU.add))
                v.scalar_tensor_tensor(vg_eps[:], vtmp[:], RMS_EPS, mv[:, :, 1], ALU.mult, ALU.add).then_inc(c_stat, 1)
                dve.wait_ge(ld_nw, 16)
                link(v.tensor_reduce(nwabs[:], nwcol[:], AX.X, ALU.max, apply_absolute_value=True))
                dve.wait_ge(c_wn, 1)
                v.tensor_reduce(wmax[:, 0:1], WF[0], AX.X, ALU.max, apply_absolute_value=True)
                dve.wait_ge(c_rstd, 1)
                v.scalar_tensor_tensor(nb_g[:, HI], mv[:, HI, 0], -1.0, gs[:, HI], ALU.mult, ALU.mult).then_inc(c_nbg, 1)
                dve.wait_ge(c_rstd, 2)
                for w in range(NW // 2):
                    last = v.tensor_scalar(GF[:, w, :], X[:, w, :], mv[:, w, 0:1], gs[:, w:w + 1], ALU.subtract, ALU.mult)
                last.then_inc(c_g, 1)
                dve.wait_ge(c_wn, 2)
                v.tensor_reduce(wmax[:, 1:2], WF[1], AX.X, ALU.max, apply_absolute_value=True)
                dve.wait_ge(ld_w[2], 16)
                last = v.tensor_reduce(wmax[:, 2:3], WF[2], AX.X, ALU.max, apply_absolute_value=True)
                dve.wait_ge(ld_w[3], 16)
                v.tensor_reduce(wmax[:, 3:4], WF[3], AX.X, ALU.max, apply_absolute_value=True)
                link(last)
                v.tensor_scalar(wmax[:, 2:3], wmax[:, 2:3], nwabs[:], None, ALU.mult).then_inc(c_wmax, 1)

                def rests_of_gt(i):
                    dve.wait_ge(c_gth, i + 1)
                    v.tensor_tensor(GTL[:, 4 * i:4 * i + 4, 0:P], PJ[i % 2][:].rearrange("p (w n) -> p w n", n=P),
                                    GTH[:, 4 * i:4 * i + 4, 0:P], ALU.subtract).then_inc(c_gtl, 1)

                rests_of_gt(0)
                rests_of_gt(1)
                dve.wait_ge(c_g, 1)
                dve.wait_ge(c_g2, 1)

                dve.wait_ge(ld_small, 16 * 7)
                link(v.tensor_tensor(swrow[:], nwrow[:], swrow[:], ALU.mult))
                for w in range(NW):
                    last = v.tensor_tensor_reduce(out=X1[:, w, :], in0=GF[:, w, :], in1=swrow[:], scale=1.0, scalar=0.0,
                                                  op0=ALU.mult, op1=ALU.add, accum_out=scol[:, w:w + 1])
                link(last)
                v.tensor_scalar(scol[:], scol[:], sbcol[:], None, ALU.add).then_inc(c_scol, 1)

                rests_of_gt(2)
                rests_of_gt(3)
                dve.wait_ge(c_wred, 1)
                link(v.tensor_scalar(wred[:], wred[:], 1e-15, None, ALU.max))
                link(v.tensor_scalar(wpow[:].bitcast(u32), wred[:].bitcast(u32), EXPONENT, None, ALU.bitwise_and))
                link(v.reciprocal(winv[:], wpow[:]))
                v.tensor_tensor(msc[:], winv[:, 0:1], winv[:, 1:2], ALU.mult)
                link(v.tensor_scalar(wsc[:], winv[:], WS, None, ALU.mult))
                v.tensor_scalar(wsc[:, 2:3], wsc[:, 2:3], nwcol[:], None, ALU.mult)
                v.tensor_tensor(cneg[:], wpow[:, 0:1], wpow[:, 1:2], ALU.mult)
                link(v.tensor_tensor(cy[:], wpow[:, 2:3], wpow[:, 3:4], ALU.mult))
                v.tensor_scalar(cneg[:], cneg[:], -(HD ** -0.5), None, ALU.mult)
                v.tensor_scalar(cy[:], cy[:], 1 / WS ** 2, None, ALU.mult).then_inc(c_wsc, 1)

                dve.wait_ge(c_srow, 1)
                link(v.tensor_copy(srow[:], MISC[0:NW, 0:P]))
                for r in range(G // 8):
                    link(v.max(t16[:, 8 * r:8 * r + 8], srow[:]))
                    if r < G // 8 - 1:
                        link(v.match_replace(srow[:], t16[:, 8 * r:8 * r + 8], srow[:], -3e38))
                dve.sem_inc(c_t16, 1)
                def rest_of(unit, dst, hi, bank):
                    dve.wait_ge(unit_hi, unit + 1)
                    v.tensor_tensor(dst, bank[:], hi, ALU.subtract).then_inc(unit_lo, 1)

                def parts(name):
                    half = int(name[-1])
                    return [t[:, half * 4:(half + 1) * 4, :].rearrange("p c n -> p (c n)") for t in
                            {"a": (AL, AH), "o": (OTL, OTH)}[name[0]]]

                for n, i in enumerate(BANKS):
                    dve.wait_ge(c_wh, n + 1)
                    v.scalar_tensor_tensor(heads_in(ML, i), MB[i][:].rearrange("p (h n) -> p h n", n=P), msc[:],
                                           heads_in(MH, i), ALU.mult, ALU.subtract).then_inc(c_wl, 1)
                dve.wait_ge(c_rstd, 3)
                v.scalar_tensor_tensor(nb_x[:], mv[:, :, 0], -1.0, rstd[:], ALU.mult, ALU.mult).then_inc(c_nbx, 1)
                dve.wait_ge(top_in, 16)
                for r in range(G // 8):
                    link(v.max(tmax[:], tall[:]))
                    if r < G // 8 - 1:
                        link(v.match_replace(tall[:], tmax[:], tall[:], -3e38))
                        rest_of(r, *parts(FIRST[r]), PJ[r % 2])
                v.tensor_scalar(gteq[:, :, 0], scol[:], tmax[:, 7:8], None, ALU.is_gt)
                link(v.tensor_scalar(gteq[:, :, 1], scol[:], tmax[:, 7:8], None, ALU.is_equal))
                dve.wait_ge(c_pool, 1)

                v.tensor_reduce(tot[:], gteq[:, :, 0], AX.X, ALU.add)
                link(v.tensor_copy(gteq16[:], gteq[:]))
                v.tensor_copy(tot16[:], tot[:]).then_inc(c_sel, 1)
                rest_of(3, *parts(FIRST[3]), PJ[1])
                dve.wait_ge(c_cum, 1)
                cum = MISC[:, 128:128 + 2 * NW].rearrange("p (w e) -> p w e", e=2)
                link(v.tensor_copy(ngt[:], MISC[:, 192:193]))
                link(v.tensor_scalar(need[:], ngt[:], -1.0, float(G), ALU.mult, ALU.add))
                link(v.tensor_scalar(keq[:], cum[:, :, 1], need[:], None, ALU.is_le))
                link(v.tensor_tensor(keq[:], keq[:], gteq[:, :, 1], ALU.mult))
                link(v.tensor_scalar(kslot[:], cum[:, :, 1], ngt[:], None, ALU.add))
                link(v.tensor_tensor(kslot[:], kslot[:], keq[:], ALU.mult))
                link(v.tensor_tensor(gslot[:], cum[:, :, 0], gteq[:, :, 0], ALU.mult))
                link(v.tensor_tensor(gslot[:], gslot[:], kslot[:], ALU.add))
                v.tensor_copy(ntok16[:], ntok[:])
                link(v.tensor_tensor(OH[:], gslot[:].unsqueeze(2).broadcast_to([P, NW, G]),
                                     iota_g[:].unsqueeze(1).broadcast_to([P, NW, G]), ALU.is_equal))
                dve.sem_inc(c_oh, 1)
                dve.wait_ge(c_gir, 1)
                link(v.tensor_copy(gi_c[:], MISC[:, 256:256 + G]))
                link(v.tensor_tensor(GM[:], gi_c[:].unsqueeze(1).broadcast_to([P, NW, G]),
                                     ntok[:].unsqueeze(2).broadcast_to([P, NW, G]), ALU.is_gt))
                link(v.tensor_scalar(GM[:], GM[:], NEG, None, ALU.mult))
                dve.wait_ge(c_hg, 1)
                v.tensor_copy(HGH[:], PT[:, 0:G].unsqueeze(1).broadcast_to([P, 4, G]))
                v.tensor_copy(HGL[:], PT[:, G:2 * G].unsqueeze(1).broadcast_to([P, 4, G])).then_inc(c_hgs, 1)
                dve.wait_ge(c_hgs, 1)
                for src, dst in ((HGH, GTH), (HGL, GTL)):
                    last = v.tensor_copy(dst[:, :, P:K1], src[:, 0:1, :].broadcast_to([P, NW, G]))
                last.then_inc(c_gk, 1)

                dve.wait_ge(c_xn, 1)
                v.tensor_copy(b1c[:], MISC[:, 448:448 + E * FC]).then_inc(y_read, 1)

                def maxima(w, j):
                    if j == 0:
                        if not (isinstance(w, int) and w == 0):
                            dve.wait_ge(scores_read, w * 4)
                        v.tensor_copy(mask[:, P:K1], GM[:, w, :]).then_inc(mask_set, 1)
                        dve.wait_ge(mask_set, w + 1)
                    dve.wait_ge(scores_done, w * 8 + (2 * j + 2))
                    if not at_start(w, j):
                        dve.wait_ge(exp_done, w * 4 + (j - 1))
                    v.memset(idle_v[:], 0.0)
                    p = j % 2
                    for i in range(GRP):
                        last = v.tensor_tensor_reduce(
                            out=SM[:, p, i, :], in0=SB_[i // 2][:, (i % 2) * K1:(i % 2 + 1) * K1], in1=mask[:],
                            scale=cneg[:], scalar=3e38, op0=ALU.add, op1=ALU.min, accum_out=mn[:, p, i:i + 1])
                    last.then_inc(scores_read, 1)

                def invert(w, j):
                    p = j % 2
                    dve.wait_ge(exp_done, w * 4 + (j + 1))
                    if not at_start(w, j):
                        dve.wait_ge(o_ready, w * 4 + (j - 1))
                    v.reciprocal(rinv[:, p, :], ssum[:, p, :]).then_inc(rinv_ready, 1)

                def take_o(w, j):
                    p = j % 2
                    dve.wait_ge(pv_done, w * 4 + (j + 1))
                    dve.wait_ge(rinv_ready, w * 4 + (j + 1))
                    if j == 0 and not (isinstance(w, int) and w == 0):
                        dve.wait_ge(unit_done, unit_no("oT0", w - 1) + 1)
                    if j == 2 and not (isinstance(w, int) and w == 0):
                        dve.wait_ge(unit_done, unit_no("oT1", w) + 1)
                    v.tensor_tensor(OS[:, j * GRP * HD:(j + 1) * GRP * HD].rearrange("p (h d) -> p h d", d=HD),
                                    OB[:, 0:GRP * HD].rearrange("p (h d) -> p h d", d=HD),
                                    rinv[:, p, :].unsqueeze(2).broadcast_to([P, GRP, HD]), ALU.mult).then_inc(o_ready, 1)

                def take_r(w):
                    dve.wait_ge(y_done, w)
                    v.scalar_tensor_tensor(R[:], YB, cy[:], XN[:, w - 1, :], ALU.mult, ALU.add
                                           ).then_inc(y_read, 1)
                    dve.wait_ge(y_read, w + 1)
                    v.bn_stats(s1[:], R[:]).then_inc(ln_step, 1)
                    dve.wait_ge(ln_step, w * 2 - 1)
                    v.memset(idle_w[:], 0.0)
                    v.bn_aggr(m1[:], s1[:]).then_inc(var_ready, 1)

                def take_ra(w):
                    dve.wait_ge(ln_rstd, w * 2 - 1)
                    dve.wait_ge(var_ready, w * 2 - 1)
                    v.tensor_scalar(ra[:], R[:], m1[:, 0:1], r1[:], ALU.subtract, ALU.mult).then_inc(ra_ready, 1)

                def take_x1(w):
                    dve.wait_ge(x1_ready, w)
                    v.bn_stats(s2[:], X1[:, w - 1, :]).then_inc(ln_step, 1)
                    dve.wait_ge(ln_step, w * 2)
                    v.memset(idle_w[:], 0.0)
                    v.bn_aggr(m2[:], s2[:]).then_inc(var_ready, 1)

                def take_t(w):
                    dve.wait_ge(ln_rstd, w * 2)
                    dve.wait_ge(var_ready, w * 2)
                    v.tensor_scalar(T[:, w - 1, :], X1[:, w - 1, :], m2[:, 0:1], r2[:], ALU.subtract, ALU.mult
                                    ).then_inc(t_ready, 1)

                def body(w, first=False):
                    for j in range(NG):
                        ahead = later(w, j, 2)
                        if ahead:
                            maxima(*ahead)
                        p = j % 2
                        dve.wait_ge(pt_hi, w * 4 + (j + 1))
                        v.tensor_tensor(PTL[:, p].rearrange("p h n -> p (h n)"), PTB[p][:],
                                        PTH[:, p].rearrange("p h n -> p (h n)"), ALU.subtract).then_inc(pt_lo, 1)
                        if not first and j == 3:
                            take_ra(w)
                        n = later(w, j, 1)
                        if j > 0:
                            take_o(w, j - 1)
                        elif not first:
                            take_o(w - 1, NG - 1)
                        dve.wait_ge(ptg_hi, w * 4 + (j + 1))
                        v.tensor_tensor(PGL[:, p], PTG[:, 0:P], PGH[:, p], ALU.subtract).then_inc(ptg_lo, 1)
                        if n:
                            invert(*n)
                        if not first and j == 2:
                            take_r(w)
                        if not first and j == 3:
                            take_x1(w)
                        for name in units(w, j):
                            if name[0] != "v":
                                rest_of(unit_no(name, w), *parts(name), unit_bank(name, w))
                        if not first and j == 3:
                            take_t(w)

                maxima(0, 0)
                maxima(0, 1)
                dve.wait_ge(c_vgh, 1)
                for half in range(2):
                    for i in range(GRP):
                        src = VG_BANKS[half]
                        dst = (slice(i * G, (i + 1) * G), slice(half * 2, half * 2 + 2), slice(i * HD, (i + 1) * HD))
                        last = v.tensor_tensor(
                            VGL[dst], src[i * G:(i + 1) * G, :].rearrange("p (j i d) -> p j i d", j=2, i=GRP)[:, :, i, :],
                            VGH[dst], ALU.subtract)
                last.then_inc(c_vgl, 1)
                invert(0, 0)
                body(0, first=True)
                with dve.Fori(1, NW - 2, 2) as w:
                    body(w)
                    body(w + 1)
                body(NW - 1)
                take_o(NW - 1, NG - 1)
                rest_of(unit_no("oT1", NW), *parts("oT1"), unit_bank("oT1", NW))
                dve.wait_ge(ld_moe, 32)
                v.tensor_reduce(w1max2[:, 0:1], w1_sb[:, 0:E // 2], AX.XY, ALU.max, apply_absolute_value=True)
                take_r(NW)
                take_ra(NW)
                take_x1(NW)
                take_t(NW)
                link(v.tensor_reduce(w1max2[:, 1:2], w1_sb[:, E // 2:E], AX.XY, ALU.max, apply_absolute_value=True))
                v.tensor_reduce(w1max[:], w1max2[:], AX.X, ALU.max).then_inc(c_w1max, 1)
                dve.wait_ge(c_w1red, 1)
                link(v.tensor_scalar(w1red[:], w1red[:], 1e-30, None, ALU.max))
                link(v.tensor_scalar(w1pow[:].bitcast(u32), w1red[:].bitcast(u32), EXPONENT, None, ALU.bitwise_and))
                link(v.reciprocal(w1sc[:], w1pow[:]))
                v.tensor_scalar(ch[:], w1pow[:], 1 / WS, None, ALU.mult)
                v.tensor_scalar(w1sc[:], w1sc[:], WS, None, ALU.mult).then_inc(c_w1sc, 1)

                dve.wait_ge(lg_done, 1)
                link(v.tensor_tensor(L[:], MISC[:, 0:NW * E].rearrange("p (w e) -> p w e", e=E),
                                     gb_sb[:].unsqueeze(1).broadcast_to([P, NW, E]), ALU.add))
                link(v.tensor_reduce(lmax[:], L[:], AX.X, ALU.max))
                lmax_b = lmax[:].unsqueeze(2).broadcast_to([P, NW, E])
                v.tensor_tensor(Lm[:], L[:], lmax_b, ALU.subtract).then_inc(lm_ready, 1)
                link(v.tensor_tensor(L[:], L[:], lmax_b, ALU.is_equal))
                link(v.tensor_tensor(L[:], L[:], rev_e[:].unsqueeze(1).broadcast_to([P, NW, E]), ALU.mult))
                link(v.tensor_reduce(rv[:], L[:], AX.X, ALU.max))
                link(v.tensor_tensor(L[:], L[:], rv[:].unsqueeze(2).broadcast_to([P, NW, E]), ALU.is_equal))
                v.tensor_copy(M16[:], L[:]).then_inc(m_ready, 1)
                dve.wait_ge(le_ready, 1)
                link(v.tensor_reduce(esum[:], L2[:], AX.X, ALU.add))
                v.reciprocal(gp[:], esum[:])
                link(v.tensor_tensor(L2[:], L[:], base_e[:].unsqueeze(1).broadcast_to([P, NW, E]), ALU.mult))
                link(v.tensor_reduce(ebase[:], L2[:], AX.X, ALU.add))
                dve.wait_ge(mcum, 1)
                link(v.tensor_tensor(L[:], MISC[:, 128:128 + NW * E].rearrange("p (w e) -> p w e", e=E), L[:], ALU.mult))
                link(v.tensor_reduce(pos[:], L[:], AX.X, ALU.add))
                v.tensor_scalar(kept[:], pos[:], float(CAP), None, ALU.is_le)
                link(v.tensor_tensor(slot1[:], pos[:], ebase[:], ALU.add))
                link(v.tensor_tensor(slot1[:], slot1[:], kept[:], ALU.mult))
                link(v.tensor_scalar(slotv[:], slot1[:], -1.0, None, ALU.add))
                for w in range(NW):
                    v.tensor_scalar(SEC[:, w, :], iota_s[:], slotv[:, w:w + 1], None, ALU.is_equal).then_inc(sec_ready, 1)
                link(v.tensor_scalar(gix[:], kept[:], -float(SLOTS + 1), float(SLOTS + 1), ALU.mult, ALU.add))
                link(v.tensor_tensor(gix[:], gix[:], slotv[:], ALU.add))
                v.tensor_copy(gidx[:], gix[:]).then_inc(idx_ready, 1)
                for i in range(4):
                    dve.wait_ge(w1_hi, i + 1)
                    e = slice(2 * i, 2 * i + 2)
                    v.scalar_tensor_tensor(W1L[:, e].rearrange("p e f -> p (e f)"), w1_sb[:, e].rearrange("p e f -> p (e f)"),
                                           w1sc[:], W1H[:, e].rearrange("p e f -> p (e f)"), ALU.mult, ALU.subtract
                                           ).then_inc(w1_lo, 1)
                dve.wait_ge(dt_hi, 1)
                v.tensor_tensor(DTL[:, 0:512], ps[0][:], DTH[:, 0:512], ALU.subtract).then_inc(dt_lo, 1)
                dve.wait_ge(dt_hi, 2)
                v.tensor_tensor(DTL[:, 512:SLOTS], ps[1][:, 0:SLOTS - 512], DTH[:, 512:SLOTS], ALU.subtract).then_inc(dt_lo, 1)

                def bias_out(e):
                    dve.wait_ge(e_done, e + 1)
                    link(v.tensor_tensor(EO[:, e, 0:D], ps[6 + e % 2][0:CAP, 0:D], b2b[0:CAP, e, :], ALU.add))
                    dve.sem_inc(eo_sb, 1)
                    link(v.bn_stats(st_e[:, e, :], EO[:, e, 0:D]))
                    v.bn_aggr(EO[:, e, D:D + 2], st_e[:, e, :]).then_inc(eo_rows, 1)

                for e in range(E):
                    dve.wait_ge(h_done, e + 1)
                    if e >= 2:
                        dve.wait_ge(h_act, e - 1)
                    v.scalar_tensor_tensor(HA[:, e % 2, :].rearrange("p (c s) -> p c s", s=CAP),
                                           ps[2 + e % 4][:, 0:FC * CAP].rearrange("p (c s) -> p c s", s=CAP), ch[:],
                                           b1c[:, e * FC:(e + 1) * FC].unsqueeze(2).broadcast_to([P, FC, CAP]),
                                           ALU.mult, ALU.add).then_inc(h_sum, 1)
                    if e >= 1:
                        bias_out(e - 1)
                bias_out(E - 1)

                link(v.tensor_tensor(gp2[:], gp[:], gp[:], ALU.mult))
                for i in range(NW // XL):
                    c = slice(i * XL, (i + 1) * XL)
                    dve.wait_ge(gathered[i], 16 * XL)
                    link(v.tensor_tensor(vtmp[:, c], Y[:, c, D + 1], gp2[:, c], ALU.mult))
                    v.tensor_scalar(vtmp[:, c], vtmp[:, c], LN_EPS, None, ALU.add).then_inc(fin_var, 1)
                    dve.wait_ge(fin_std, i + 1)
                    link(v.reciprocal(rstd[:, c], std[:, c]))
                    link(v.tensor_tensor(rms[:, c], rstd[:, c], rstd[:, c], ALU.mult))
                    v.tensor_tensor(rstd[:, c], rstd[:, c], gp[:, c], ALU.mult)
                    link(v.tensor_tensor(rms[:, c], rms[:, c], vtmp[:, c], ALU.mult))
                    link(v.tensor_scalar(rms[:, c], rms[:, c], -0.5, 1.5, ALU.mult, ALU.add))
                    link(v.tensor_tensor(rms[:, c], rms[:, c], rstd[:, c], ALU.mult))
                    for w in range(i * XL, (i + 1) * XL):
                        last = v.tensor_scalar(OUT[:, w, :], Y[:, w, 0:D], Y[:, w, D:D + 1], rms[:, w:w + 1],
                                               ALU.subtract, ALU.mult)
                    link(last)
                    v.tensor_tensor(OUT[:, c, :], OUT[:, c, :], X1[:, c, :], ALU.add).then_inc(fin_add, 1)

            @block.tensor
            def _(pe):
                mm, tr = nc.tensor.matmul, nc.tensor.transpose

                def three(dst, lh, ll, rh, rl, start, stop):
                    mm(dst, lh, rh, start=start, stop=False)
                    mm(dst, lh, rl, start=False, stop=False)
                    return mm(dst, ll, rh, start=False, stop=stop)

                def running_count(dst, src, n):
                    mm(dst, upper[:], src, start=True, stop=False)
                    for k in range(1, NW):
                        last = mm(dst[:, k * n:NW * n], ones[:], src[:, 0:(NW - k) * n], start=False, stop=(k == NW - 1))
                    return last

                pe.wait_ge(c_pool, 1)
                for i in range(4):
                    if i % 2 == 0:
                        pe.wait_ge(c_wn, i // 2 + 1)
                    for k in range(4):
                        c = (i % 2) * 4 + k
                        last = tr(MB[i][:, k * P:(k + 1) * P], WF[i // 2][:, c * P:(c + 1) * P], ident[:])
                    last.then_inc(c_wt, 1)

                def turn_g(i):
                    if i >= 2:
                        pe.wait_ge(c_gtl, i - 1)
                    for k in range(4):
                        last = tr(PJ[i % 2][:, k * P:(k + 1) * P], GF[:, 4 * i + k, :], ident[:])
                    last.then_inc(c_gt, 1)

                def products(heads):
                    for h in heads:
                        rows, cols = slice((h % 2) * HD, (h % 2 + 1) * HD), slice(h // 2 * P, (h // 2 + 1) * P)
                        last = mm(product(h), WQT[rows, cols], WKT[rows, cols], start=True, stop=True)
                        if h % 8 >= 6:
                            last.then_inc(c_mm, 1)

                pe.wait_ge(c_g, 1)
                turn_g(0)
                turn_g(1)
                pe.wait_ge(c_wts, 4)
                products(range(H // 2))
                pe.wait_ge(c_g2, 1)
                turn_g(2)
                turn_g(3)
                pe.wait_ge(c_scol, 1)
                tr(MISC[0:NW, 0:P], scol[:], ident[:]).then_inc(c_srow, 1)
                products(range(H // 2, H))

                def weight_unit(name, w, bank):
                    k = int(name[-1])
                    gh, gl = GTH[:, w, 0:P], GTL[:, w, 0:P]
                    if name[0] == "v":
                        f = slice(k * 512, (k + 1) * 512)
                        last = three(bank[:], gh, gl, WVH[:, f], WVL[:, f], True, True)
                    else:
                        for c in range(4):
                            h = 4 * k + c
                            last = three(bank[:, c * P:(c + 1) * P], MH[:, h, :], ML[:, h, :], gh, gl, True, True)
                    last.then_inc(unit_done, 1)

                pe.wait_ge(c_wl, 4)
                pe.wait_ge(c_gtl, 4)
                for i, name in enumerate(FIRST):
                    if name[0] == "v":
                        pe.wait_ge(c_wvol, 1)
                    if i >= 2:
                        wait_bank(pe, name, -1)
                    weight_unit(name, 0, PJ[i % 2])

                pe.wait_ge(c_sel, 1)
                running_count(MISC[:, 128:128 + 2 * NW], gteq16[:].rearrange("p w e -> p (w e)"), 2)
                mm(MISC[:, 192:193], ones[:], tot16[:], start=True, stop=True).then_inc(c_cum, 1)
                pe.wait_ge(c_oh, 1)
                for w in range(NW):
                    last = mm(MISC[:, 256:256 + G], ntok16[:, w:w + 1].broadcast_to([P, P]), OH[:, w, :],
                              start=(w == 0), stop=(w == NW - 1))
                pe.wait_ge(ld_small, 16 * 7)
                tr(MISC[:, 448:448 + E * FC], b1r[:], ident[0:E * FC, 0:E * FC]).then_inc(c_gir, 1)
                pe.wait_ge(c_gl, 1)
                for part, src in ((0, GH), (G, GL)):
                    for w in range(NW):
                        last = mm(PT[:, part:part + G], src[:, w, :], OH[:, w, :], start=(w == 0), stop=(w == NW - 1))
                last.then_inc(c_hg, 1)
                pe.wait_ge(c_hgs, 1)
                pe.wait_ge(c_gk, 1)

                def global_values():
                    hgh, hgl = (t[:].rearrange("p a g -> p (a g)") for t in (HGH, HGL))
                    wait_split(pe, "a3", -1)
                    for half, bank in enumerate(VG_BANKS):
                        f = slice(half * 512, (half + 1) * 512)
                        last = three(bank[:], hgh, hgl, WVH[:, f], WVL[:, f], True, True)
                    last.then_inc(c_vg, 1)

                def scores(w, j, made):
                    wait_split(pe, f"a{j}", made)
                    if not (isinstance(w, int) and w == 0 and j == 0):
                        pe.wait_ge(scores_read, w * 4 + j)
                    for a in range(2):
                        for b in range(2):
                            h = GRP * j + 2 * a + b
                            last = three(SB_[a][:, b * K1:(b + 1) * K1], AH[:, h, :], AL[:, h, :], GTH[:, w, :], GTL[:, w, :],
                                         True, True)
                        last.then_inc(scores_done, 1)

                def turn_probs(w, j):
                    p = j % 2
                    pe.wait_ge(exp_done, w * 4 + (j + 1))
                    if not at_start(w, j):
                        pe.wait_ge(pt_lo, w * 4 + (j - 1))
                    for i in range(GRP):
                        last = tr(PTB[p][:, i * P:(i + 1) * P], PR[:, p, i, 0:P], ident[:])
                    last.then_inc(pt_done, 1)

                def turn_pg(w, j):
                    pe.wait_ge(pg_ready, w * 4 + (j + 1))
                    if not (isinstance(w, int) and w == 0 and j == 0):
                        pe.wait_ge(ptg_lo, w * 4 + j)
                    tr(PTG[:, 0:P], PG[:].rearrange("p h g -> p (h g)"), ident[:]).then_inc(ptg_done, 1)

                def values(w, j):
                    if not (isinstance(w, int) and w == 0 and j == 0):
                        pe.wait_ge(o_ready, w * 4 + j)
                    if j in (0, 2):
                        pe.wait_ge(v_split, w * 2 + (j // 2 + 1))
                    if j == 2:
                        pe.wait_ge(y_read, w + 1)
                    pe.wait_ge(ptg_lo, w * 4 + (j + 1))
                    pe.wait_ge(pt_lo, w * 4 + (j + 1))
                    p = j % 2
                    three(OB[:, 0:GRP * HD], PGH[:, p], PGL[:, p], VGH[:, j, :], VGL[:, j, :], True, False)
                    for i in range(GRP):
                        f = slice((GRP * j + i) * HD, (GRP * j + i + 1) * HD)
                        last = three(OB[:, i * HD:(i + 1) * HD], PTH[:, p, i, :], PTL[:, p, i, :], VH[:, f], VL[:, f],
                                     False, i == GRP - 1)
                    last.then_inc(pv_done, 1)

                def turn_o(name, w):
                    half = int(name[-1])
                    pe.wait_ge(o_ready, w * 4 + 2 if half == 0 else w * 4)
                    for c in range(4):
                        f = slice((half * 4 + c) * P, (half * 4 + c + 1) * P)
                        last = tr(unit_bank(name, w)[:, c * P:(c + 1) * P], OS[:, f], ident[:])
                    last.then_inc(unit_done, 1)

                def project(w):
                    wait_split(pe, "oT1", w)
                    pe.wait_ge(o_ready, w * 4 + 1 if not isinstance(w, int) or w < NW else w * 4)
                    for c in range(CH):
                        f = slice(c * D, (c + 1) * D)
                        last = three(YB, OTH[:, c, :], OTL[:, c, :], WOH[:, f], WOL[:, f], c == 0, c == CH - 1)
                    last.then_inc(y_done, 1)

                def body(w, first=False):
                    for j in range(NG):
                        n = later(w, j, 2)
                        if n:
                            scores(*n, w if j >= 2 else (w - 1))
                        turn_pg(w, j)
                        if j == 2 and not first:
                            project(w)
                        if j > 0:
                            values(w, j - 1)
                        elif not first:
                            values(w - 1, NG - 1)
                        for name in units(w, j):
                            wait_bank(pe, name, w)
                            if name[0] == "o":
                                turn_o(name, w)
                            else:
                                weight_unit(name, w if name == "v1" else w + 1, unit_bank(name, w))
                        n = later(w, j, 1)
                        if n:
                            turn_probs(*n)

                scores(0, 0, -1)
                global_values()
                scores(0, 1, -1)
                turn_probs(0, 0)
                pe.wait_ge(c_vgl, 1)
                pe.wait_ge(c_wvol, 2)
                body(0, first=True)
                with pe.Fori(1, NW - 2, 2) as w:
                    body(w)
                    body(w + 1)
                body(NW - 1)

                def turn_t(i):
                    pe.wait_ge(t_ready, (i + 1) * NW // 4)
                    for k in range(4):
                        last = tr(ps[i % 2][:, k * P:(k + 1) * P], T[:, 4 * i + k, :], ident[:])
                    last.then_inc(tt_done, 1)

                def logits(i):
                    pe.wait_ge(tt_sb, i + 1)
                    for w in range(i * NW // 4, (i + 1) * NW // 4):
                        last = mm(MISC[:, w * E:(w + 1) * E], TT[:, w * P:(w + 1) * P], gw_sb[:], start=True, stop=True)
                    if i == 3:
                        last.then_inc(lg_done, 1)

                pe.wait_ge(scores_read, 4 * NW)
                turn_t(0)
                turn_t(1)
                values(NW - 1, NG - 1)
                wait_bank(pe, "oT1", NW)
                turn_o("oT1", NW)
                pe.wait_ge(pt_lo, 4 * NW)
                logits(0)
                logits(1)
                project(NW)
                turn_t(2)
                logits(2)
                turn_t(3)
                logits(3)

                pe.wait_ge(m_ready, 1)
                running_count(MISC[:, 128:128 + NW * E], M16[:].rearrange("p w e -> p (w e)"), E).then_inc(mcum, 1)
                pe.wait_ge(tt_sb, 4)
                for w in range(NW):
                    pe.wait_ge(sec_ready, w + 1)
                    pe.wait_ge(tl_ready, w // 4 + 1)
                    for src in (TH, TL):
                        a, b = (w == 0 and src is TH), (w == NW - 1 and src is TL)
                        mm(ps[0][:], src[:, w, :], SEC[:, w, 0:512], start=a, stop=b)
                        last = mm(ps[1][:, 0:SLOTS - 512], src[:, w, :], SEC[:, w, 512:SLOTS], start=a, stop=b)
                last.then_inc(disp_done, 1)

                def down(e):
                    pe.wait_ge(h_act, e + 1)
                    if e >= 2:
                        pe.wait_ge(eo_sb, e - 1)
                    for c in range(FC):
                        last = mm(ps[6 + e % 2][0:CAP, 0:D], HS[:, e, c, :], w2_sb[:, e, c, :], start=(c == 0), stop=(c == FC - 1))
                    last.then_inc(e_done, 1)

                for e in range(E):
                    pe.wait_ge(w1_lo, e // 2 + 1)
                    if e >= 4:
                        pe.wait_ge(h_sum, e - 3)
                    pe.wait_ge(dt_lo, 1 if (e + 1) * CAP <= 512 else 2)
                    s = slice(e * CAP, (e + 1) * CAP)
                    for c in range(FC):
                        f = slice(c * P, (c + 1) * P)
                        last = three(ps[2 + e % 4][:, c * CAP:(c + 1) * CAP], W1H[:, e, f], W1L[:, e, f],
                                     DTH[:, s], DTL[:, s], True, True)
                    last.then_inc(h_done, 1)
                    if e >= 2:
                        down(e - 2)
                down(E - 2)
                down(E - 1)


_INS = ['L0_attn_x', 'L0_attn_norm_w', 'L0_attn_w_q', 'L0_attn_w_k', 'L0_attn_w_v', 'L0_attn_w_out',
        'L0_attn_scorer_w', 'L0_attn_scorer_b', 'L0_ffn_gate_w', 'L0_ffn_gate_b', 'L0_ffn_w1', 'L0_ffn_b1',
        'L0_ffn_w2', 'L0_ffn_b2']


def kernel(**inputs):
    import numpy as _np
    import concourse.bacc as _bacc
    from concourse import mybir as _mybir
    from concourse.bass_utils import run_bass_kernel_spmd as _run

    nc = _bacc.Bacc("TRN2", target_bir_lowering=False, num_devices=1)
    arrays, args = {}, []
    for name in _INS:
        a = _np.ascontiguousarray(inputs[name])
        arrays[f"in_{name}"] = a
        args.append(nc.dram_tensor(f"in_{name}", a.shape, _mybir.dt.from_np(a.dtype), kind="ExternalInput").ap())
    shape = inputs['L0_attn_x'].shape
    args.append(nc.dram_tensor("out_0", shape, _mybir.dt.float32, kind="ExternalOutput").ap())
    build(nc, *args)
    r = _run(nc, [arrays], core_ids=[0])
    return r.results[0]["out_0"]
```
